# Optimizing a Trainium2 kernel written in Bass

```python
import numpy as np
import jax
import jax.numpy as jnp

def _softmax(x, axis=-1):
    return jax.nn.softmax(x, axis=axis)

def _gelu(x):
    return jax.nn.gelu(x, approximate=True)

def _silu(x):
    return jax.nn.silu(x)

def _sigmoid(x):
    return jax.nn.sigmoid(x)

def _layernorm(x, axis=-1, eps=1e-05):
    m = jnp.mean(x, axis=axis, keepdims=True)
    v = jnp.var(x, axis=axis, keepdims=True)
    return (x - m) / jnp.sqrt(v + eps)

def _scatter_add(tgt, idx, src, axis=0):
    return tgt.at[idx].add(src)

def _segment_sum(src, seg, n):
    return jax.ops.segment_sum(src, seg, n)
kernel_name = 'mk_gnn_resnorm_d4_gnn_r32_eda0b3'

def setup_inputs(seed: int=0):
    np.random.seed(seed)
    _w = jnp.asarray

    def _rec_inputs():
        import jax
        import jax.numpy as jnp
        _gk = jax.random.key(seed)
        x = -0.0005121 + 1.001 * jax.random.normal(jax.random.fold_in(_gk, 1), (3125, 64), jnp.float32)
        src = jax.random.randint(jax.random.fold_in(_gk, 2), (100000,), 0, 3125, jnp.int32)
        dst = jax.random.randint(jax.random.fold_in(_gk, 3), (100000,), 0, 3125, jnp.int32)
        _o = jnp.argsort(dst, stable=True)
        src = src[_o]
        dst = dst[_o]
        edge_attr_16 = 0.000254156 + 0.999948 * jax.random.normal(jax.random.fold_in(_gk, 12), (100000, 16), jnp.float32)
        edge_attr_64 = 1.36993e-05 + 0.999972 * jax.random.normal(jax.random.fold_in(_gk, 13), (100000, 64), jnp.float32)
        edge_attr_9 = 0.000739051 + 0.999958 * jax.random.normal(jax.random.fold_in(_gk, 14), (100000, 9), jnp.float32)
        edge_type_64 = jax.random.randint(jax.random.fold_in(_gk, 16), (100000,), 0, 64, jnp.int32)
        edge_weight1 = jax.random.uniform(jax.random.fold_in(_gk, 17), (100000, 1), jnp.float32, 0.0, 0.999998)
        return (x, src, dst, edge_attr_16, edge_attr_64, edge_attr_9, edge_type_64, edge_weight1)
    x, src, dst, edge_attr_16, edge_attr_64, edge_attr_9, edge_type_64, edge_weight1 = _rec_inputs()

    def _L0_gnn_setup():
        import jax, jax.numpy as jnp
        import numpy as np
        N, E = (50000, 25000)
        NODE_DIM, EDGE_DIM, HEADS = (64, 16, 4)
        C = NODE_DIM // HEADS
        NEG_SLOPE = 0.2
        BN_EPS = 1e-05
        key = jax.random.key(seed)
        ks = jax.random.split(key, 12)
        glorot = lambda k, shape: jax.random.normal(k, shape, jnp.float32) * np.sqrt(2.0 / (shape[0] + shape[-1]))
        return {'x': jax.random.normal(ks[0], (N, NODE_DIM), jnp.float32), 'edge_index': jax.random.randint(ks[1], (2, E), 0, N, jnp.int32), 'edge_attr': jax.random.normal(ks[2], (E, EDGE_DIM), jnp.float32), 'W_l': glorot(ks[3], (NODE_DIM, HEADS * C)), 'b_l': jnp.zeros((HEADS * C,), jnp.float32), 'W_r': glorot(ks[4], (NODE_DIM, HEADS * C)), 'b_r': jnp.zeros((HEADS * C,), jnp.float32), 'W_e': glorot(ks[5], (EDGE_DIM, HEADS * C)), 'att': glorot(ks[6], (HEADS, C)), 'bias': jnp.zeros((HEADS * C,), jnp.float32), 'gamma': jnp.ones((NODE_DIM,), jnp.float32), 'beta': jnp.zeros((NODE_DIM,), jnp.float32)}
    _L0_gnn_all = _L0_gnn_setup()
    _L0_gnn_in = {k: v for k, v in _L0_gnn_all.items() if k in ('W_l', 'b_l', 'W_r', 'b_r', 'W_e', 'att', 'bias', 'gamma', 'beta')}
    del _L0_gnn_all

    def _L1_gnn_setup():
        import jax, jax.numpy as jnp
        import numpy as np
        N, E = (10000, 10000)
        D, S, HE = (64, 9, 64)
        H, DQK, DV = (8, 16, 16)
        OK, OV = (H * DQK, H * DV)
        EPS_BN = 1e-05

        def tensor_product(x_e, sh, w, C):
            acc = sh[:, 0:1] * (x_e @ C[:, 0, :])
            for s in range(1, S):
                acc = acc + sh[:, s:s + 1] * (x_e @ C[:, s, :])
            return acc * w

        def mlp2(x, w1, b1, w2, b2):
            return jax.nn.relu(x @ w1 + b1) @ w2 + b2
        key = jax.random.key(seed)
        ks = jax.random.split(key, 20)
        g = lambda k, shape, fan: jax.random.normal(k, shape, jnp.float32) / np.float32(np.sqrt(fan))
        return {'tfn_features': jax.random.normal(ks[0], (N, D), jnp.float32), 'edge_features': jax.random.normal(ks[1], (E, HE), jnp.float32), 'edge_sh': jax.random.normal(ks[2], (E, S), jnp.float32), 'Wq': g(ks[3], (D, OK), D), 'Cqk': g(ks[4], (D, S, OK), D * S), 'Cv': g(ks[5], (D, S, OV), D * S), 'k_w1': g(ks[6], (HE, HE), HE), 'k_b1': jnp.zeros((HE,), jnp.float32), 'k_w2': g(ks[7], (HE, OK), HE), 'k_b2': jnp.zeros((OK,), jnp.float32), 'v_w1': g(ks[8], (HE, HE), HE), 'v_b1': jnp.zeros((HE,), jnp.float32), 'v_w2': g(ks[9], (HE, OV), HE), 'v_b2': jnp.zeros((OV,), jnp.float32), 'W_out': g(ks[10], (OV, D), OV), 'W_self': g(ks[11], (D, D), D), 'gamma': jnp.ones((D,), jnp.float32), 'beta': jnp.zeros((D,), jnp.float32), 'edge_index': jax.random.randint(ks[12], (2, E), 0, N, dtype=jnp.int32)}
    _L1_gnn_all = _L1_gnn_setup()
    _L1_gnn_in = {k: v for k, v in _L1_gnn_all.items() if k in ('Wq', 'Cqk', 'Cv', 'k_w1', 'k_b1', 'k_w2', 'k_b2', 'v_w1', 'v_b1', 'v_w2', 'v_b2', 'W_out', 'W_self', 'gamma', 'beta')}
    del _L1_gnn_all

    def _L2_gnn_setup():
        import jax, jax.numpy as jnp
        import numpy as np
        N = 50000
        E = 25000
        IN = 64
        H = 4
        D = 16
        OH = H * D
        SCALE = float(np.sqrt(IN))
        LN_EPS = 1e-05
        key = jax.random.key(seed)
        ks = jax.random.split(key, 16)
        w = 0.05
        return {'feats': jax.random.normal(ks[0], (N, IN), jnp.float32), 'Wq': jax.random.normal(ks[1], (IN, OH), jnp.float32) * w, 'bq': jnp.zeros((OH,), jnp.float32), 'Wk': jax.random.normal(ks[2], (IN, OH), jnp.float32) * w, 'bk': jnp.zeros((OH,), jnp.float32), 'Wv': jax.random.normal(ks[3], (IN, OH), jnp.float32) * w, 'bv': jnp.zeros((OH,), jnp.float32), 'Wo': jax.random.normal(ks[4], (OH, OH), jnp.float32) * w, 'bo': jnp.zeros((OH,), jnp.float32), 'Wf': jax.random.normal(ks[5], (IN, OH), jnp.float32) * w, 'bf': jnp.zeros((OH,), jnp.float32), 'gamma': jnp.ones((OH,), jnp.float32), 'beta': jnp.zeros((OH,), jnp.float32), 'src': jax.random.randint(ks[6], (E,), 0, N, jnp.int32), 'dst': jax.random.randint(ks[7], (E,), 0, N, jnp.int32)}
    _L2_gnn_all = _L2_gnn_setup()
    _L2_gnn_in = {k: v for k, v in _L2_gnn_all.items() if k in ('Wq', 'bq', 'Wk', 'bk', 'Wv', 'bv', 'Wo', 'bo', 'Wf', 'bf', 'gamma', 'beta')}
    del _L2_gnn_all

    def _L3_gnn_setup():
        import jax, jax.numpy as jnp
        import numpy as np
        N_NODES = 50000
        N_EDGES = 50000
        IN_F = 64
        OUT_F = 64
        NUM_RELS = 64
        NUM_BASES = 64
        BN_EPS = 1e-05
        key = jax.random.key(seed)
        ks = jax.random.split(key, 12)
        node_feats = jax.random.normal(ks[0], (N_NODES, IN_F), dtype=jnp.float32)
        src = jax.random.randint(ks[1], (N_EDGES,), 0, N_NODES, dtype=jnp.int32)
        dst = jax.random.randint(ks[2], (N_EDGES,), 0, N_NODES, dtype=jnp.int32)
        etype = jax.random.randint(ks[3], (N_EDGES,), 0, NUM_RELS, dtype=jnp.int32)
        norm = jax.random.uniform(ks[4], (N_EDGES, 1), dtype=jnp.float32)
        basis = jax.random.normal(ks[5], (NUM_BASES, IN_F, OUT_F), dtype=jnp.float32) * (1.0 / np.sqrt(IN_F))
        comp = jax.random.normal(ks[6], (NUM_RELS, NUM_BASES), dtype=jnp.float32) * (1.0 / np.sqrt(NUM_BASES))
        bias = jnp.zeros((OUT_F,), dtype=jnp.float32)
        res_w = jax.random.normal(ks[7], (OUT_F, IN_F), dtype=jnp.float32) * (1.0 / np.sqrt(IN_F))
        res_b = jnp.zeros((OUT_F,), dtype=jnp.float32)
        gamma = jnp.ones((OUT_F,), dtype=jnp.float32)
        beta = jnp.zeros((OUT_F,), dtype=jnp.float32)
        return {'node_feats': node_feats, 'src': src, 'dst': dst, 'etype': etype, 'norm': norm, 'basis': basis, 'comp': comp, 'bias': bias, 'res_w': res_w, 'res_b': res_b, 'gamma': gamma, 'beta': beta}
    _L3_gnn_all = _L3_gnn_setup()
    _L3_gnn_in = {k: v for k, v in _L3_gnn_all.items() if k in ('basis', 'comp', 'bias', 'res_w', 'res_b', 'gamma', 'beta')}
    del _L3_gnn_all
    return {'x': x, 'src': src, 'dst': dst, 'edge_attr_16': edge_attr_16, 'edge_attr_64': edge_attr_64, 'edge_attr_9': edge_attr_9, 'edge_type_64': edge_type_64, 'edge_weight1': edge_weight1, 'L0_gnn_W_l': _L0_gnn_in['W_l'], 'L0_gnn_b_l': _L0_gnn_in['b_l'], 'L0_gnn_W_r': _L0_gnn_in['W_r'], 'L0_gnn_b_r': _L0_gnn_in['b_r'], 'L0_gnn_W_e': _L0_gnn_in['W_e'], 'L0_gnn_att': _L0_gnn_in['att'], 'L0_gnn_bias': _L0_gnn_in['bias'], 'L0_gnn_gamma': _L0_gnn_in['gamma'], 'L0_gnn_beta': _L0_gnn_in['beta'], 'L1_gnn_Wq': _L1_gnn_in['Wq'], 'L1_gnn_Cqk': _L1_gnn_in['Cqk'], 'L1_gnn_Cv': _L1_gnn_in['Cv'], 'L1_gnn_k_w1': _L1_gnn_in['k_w1'], 'L1_gnn_k_b1': _L1_gnn_in['k_b1'], 'L1_gnn_k_w2': _L1_gnn_in['k_w2'], 'L1_gnn_k_b2': _L1_gnn_in['k_b2'], 'L1_gnn_v_w1': _L1_gnn_in['v_w1'], 'L1_gnn_v_b1': _L1_gnn_in['v_b1'], 'L1_gnn_v_w2': _L1_gnn_in['v_w2'], 'L1_gnn_v_b2': _L1_gnn_in['v_b2'], 'L1_gnn_W_out': _L1_gnn_in['W_out'], 'L1_gnn_W_self': _L1_gnn_in['W_self'], 'L1_gnn_gamma': _L1_gnn_in['gamma'], 'L1_gnn_beta': _L1_gnn_in['beta'], 'L2_gnn_Wq': _L2_gnn_in['Wq'], 'L2_gnn_bq': _L2_gnn_in['bq'], 'L2_gnn_Wk': _L2_gnn_in['Wk'], 'L2_gnn_bk': _L2_gnn_in['bk'], 'L2_gnn_Wv': _L2_gnn_in['Wv'], 'L2_gnn_bv': _L2_gnn_in['bv'], 'L2_gnn_Wo': _L2_gnn_in['Wo'], 'L2_gnn_bo': _L2_gnn_in['bo'], 'L2_gnn_Wf': _L2_gnn_in['Wf'], 'L2_gnn_bf': _L2_gnn_in['bf'], 'L2_gnn_gamma': _L2_gnn_in['gamma'], 'L2_gnn_beta': _L2_gnn_in['beta'], 'L3_gnn_basis': _L3_gnn_in['basis'], 'L3_gnn_comp': _L3_gnn_in['comp'], 'L3_gnn_bias': _L3_gnn_in['bias'], 'L3_gnn_res_w': _L3_gnn_in['res_w'], 'L3_gnn_res_b': _L3_gnn_in['res_b'], 'L3_gnn_gamma': _L3_gnn_in['gamma'], 'L3_gnn_beta': _L3_gnn_in['beta']}

def reference(x, src, dst, edge_attr_16, edge_attr_64, edge_attr_9, edge_type_64, edge_weight1, L0_gnn_W_l, L0_gnn_b_l, L0_gnn_W_r, L0_gnn_b_r, L0_gnn_W_e, L0_gnn_att, L0_gnn_bias, L0_gnn_gamma, L0_gnn_beta, L1_gnn_Wq, L1_gnn_Cqk, L1_gnn_Cv, L1_gnn_k_w1, L1_gnn_k_b1, L1_gnn_k_w2, L1_gnn_k_b2, L1_gnn_v_w1, L1_gnn_v_b1, L1_gnn_v_w2, L1_gnn_v_b2, L1_gnn_W_out, L1_gnn_W_self, L1_gnn_gamma, L1_gnn_beta, L2_gnn_Wq, L2_gnn_bq, L2_gnn_Wk, L2_gnn_bk, L2_gnn_Wv, L2_gnn_bv, L2_gnn_Wo, L2_gnn_bo, L2_gnn_Wf, L2_gnn_bf, L2_gnn_gamma, L2_gnn_beta, L3_gnn_basis, L3_gnn_comp, L3_gnn_bias, L3_gnn_res_w, L3_gnn_res_b, L3_gnn_gamma, L3_gnn_beta):
    import jax
    import jax.numpy as jnp

    def _L0_gnn_ref(x, edge_index, edge_attr, W_l, b_l, W_r, b_r, W_e, att, bias, gamma, beta):
        import jax, jax.numpy as jnp
        import numpy as np
        N, E = (50000, 25000)
        NODE_DIM, EDGE_DIM, HEADS = (64, 16, 4)
        C = NODE_DIM // HEADS
        NEG_SLOPE = 0.2
        BN_EPS = 1e-05
        src, dst = (edge_index[0], edge_index[1])
        n = x.shape[0]
        xl = (x @ W_l + b_l).reshape(n, HEADS, C)
        xr = (x @ W_r + b_r).reshape(n, HEADS, C)
        e = (edge_attr @ W_e).reshape(-1, HEADS, C)
        g = jax.nn.leaky_relu(xl[src] + xr[dst] + e, NEG_SLOPE)
        logits = jnp.einsum('ehc,hc->eh', g, att)
        amax = jax.ops.segment_max(logits, dst, num_segments=n)
        ex = jnp.exp(logits - amax[dst])
        denom = jax.ops.segment_sum(ex, dst, num_segments=n)
        alpha = ex / (denom[dst] + 1e-16)
        msg = xl[src] * alpha[..., None]
        out = jax.ops.segment_sum(msg, dst, num_segments=n).reshape(n, HEADS * C) + bias
        mean = out.mean(axis=0)
        var = out.var(axis=0)
        out = (out - mean) * jax.lax.rsqrt(var + BN_EPS) * gamma + beta
        return jax.nn.gelu(out + x, approximate=False)

    def _L1_gnn_ref(tfn_features, edge_features, edge_sh, Wq, Cqk, Cv, k_w1, k_b1, k_w2, k_b2, v_w1, v_b1, v_w2, v_b2, W_out, W_self, gamma, beta, edge_index):
        import jax, jax.numpy as jnp
        import numpy as np
        N, E = (10000, 10000)
        D, S, HE = (64, 9, 64)
        H, DQK, DV = (8, 16, 16)
        OK, OV = (H * DQK, H * DV)
        EPS_BN = 1e-05

        def tensor_product(x_e, sh, w, C):
            acc = sh[:, 0:1] * (x_e @ C[:, 0, :])
            for s in range(1, S):
                acc = acc + sh[:, s:s + 1] * (x_e @ C[:, s, :])
            return acc * w

        def mlp2(x, w1, b1, w2, b2):
            return jax.nn.relu(x @ w1 + b1) @ w2 + b2
        edge_dst, edge_src = (edge_index[0], edge_index[1])
        n = tfn_features.shape[0]
        q = (tfn_features @ Wq).reshape(n, H, DQK)
        x_dst = tfn_features[edge_dst]
        wk = mlp2(edge_features, k_w1, k_b1, k_w2, k_b2)
        wv = mlp2(edge_features, v_w1, v_b1, v_w2, v_b2)
        k = tensor_product(x_dst, edge_sh, wk, Cqk).reshape(-1, H, DQK)
        v = tensor_product(x_dst, edge_sh, wv, Cv).reshape(-1, H, DV)
        attn = jnp.einsum('ehd,ehd->eh', q[edge_src], k)
        amax = jax.ops.segment_max(attn, edge_src, num_segments=n)
        ex = jnp.exp(attn - amax[edge_src])
        denom = jax.ops.segment_sum(ex, edge_src, num_segments=n)
        alpha = ex / (denom[edge_src] + 1e-16)
        upd = jax.ops.segment_sum(v * alpha[..., None], edge_src, num_segments=n)
        upd = upd.reshape(n, OV) @ W_out
        out = tfn_features @ W_self + upd
        mu = out.mean(axis=0)
        var = out.var(axis=0)
        return (out - mu) * jax.lax.rsqrt(var + EPS_BN) * gamma + beta

    def _L2_gnn_ref(feats, Wq, bq, Wk, bk, Wv, bv, Wo, bo, Wf, bf, gamma, beta, src, dst):
        import jax, jax.numpy as jnp
        import numpy as np
        N = 50000
        E = 25000
        IN = 64
        H = 4
        D = 16
        OH = H * D
        SCALE = float(np.sqrt(IN))
        LN_EPS = 1e-05
        n = feats.shape[0]
        q = (feats @ Wq + bq).reshape(n, H, D)
        k = (feats @ Wk + bk).reshape(n, H, D)
        v = (feats @ Wv + bv).reshape(n, H, D)
        score = jnp.sum(k[src] * q[dst], axis=-1)
        score = jnp.exp(jnp.clip(score / SCALE, -5.0, 5.0))
        wv = jax.ops.segment_sum(v[src] * score[..., None], dst, num_segments=n)
        z = jax.ops.segment_sum(score, dst, num_segments=n)
        wv = wv / (z[..., None] + 1.0)
        o = wv.reshape(n, OH) @ Wo + bo
        h = feats @ Wf + bf + o
        mu = jnp.mean(h, axis=-1, keepdims=True)
        var = jnp.var(h, axis=-1, keepdims=True)
        ln = (h - mu) * jax.lax.rsqrt(var + LN_EPS) * gamma + beta
        return h + ln

    def _L3_gnn_ref(node_feats, src, dst, etype, norm, basis, comp, bias, res_w, res_b, gamma, beta):
        import jax, jax.numpy as jnp
        import numpy as np
        N_NODES = 50000
        N_EDGES = 50000
        IN_F = 64
        OUT_F = 64
        NUM_RELS = 64
        NUM_BASES = 64
        BN_EPS = 1e-05
        N = node_feats.shape[0]
        R = comp.shape[0]
        W = jnp.einsum('rb,bio->rio', comp, basis)
        msg = node_feats[src] * norm
        seg = etype.astype(jnp.int32) * N + dst
        s = jax.ops.segment_sum(msg, seg, num_segments=R * N)
        s = s.reshape(R, N, -1)
        h = jnp.einsum('rni,rio->no', s, W) + bias
        h = jax.nn.relu(h)
        res = jax.nn.relu(node_feats @ res_w.T + res_b)
        y = h + res
        mean = jnp.mean(y, axis=0)
        var = jnp.var(y, axis=0)
        return (y - mean) * jax.lax.rsqrt(var + BN_EPS) * gamma + beta
    edge_index = jnp.stack([src, dst])
    x = _layernorm(x + _L0_gnn_ref(x, edge_index, edge_attr_16, L0_gnn_W_l, L0_gnn_b_l, L0_gnn_W_r, L0_gnn_b_r, L0_gnn_W_e, L0_gnn_att, L0_gnn_bias, L0_gnn_gamma, L0_gnn_beta), axis=-1)
    x = _layernorm(x + _L1_gnn_ref(x, edge_attr_64, edge_attr_9, L1_gnn_Wq, L1_gnn_Cqk, L1_gnn_Cv, L1_gnn_k_w1, L1_gnn_k_b1, L1_gnn_k_w2, L1_gnn_k_b2, L1_gnn_v_w1, L1_gnn_v_b1, L1_gnn_v_w2, L1_gnn_v_b2, L1_gnn_W_out, L1_gnn_W_self, L1_gnn_gamma, L1_gnn_beta, edge_index), axis=-1)
    x = _layernorm(x + _L2_gnn_ref(x, L2_gnn_Wq, L2_gnn_bq, L2_gnn_Wk, L2_gnn_bk, L2_gnn_Wv, L2_gnn_bv, L2_gnn_Wo, L2_gnn_bo, L2_gnn_Wf, L2_gnn_bf, L2_gnn_gamma, L2_gnn_beta, src, dst), axis=-1)
    x = _layernorm(x + _L3_gnn_ref(x, src, dst, edge_type_64, edge_weight1, L3_gnn_basis, L3_gnn_comp, L3_gnn_bias, L3_gnn_res_w, L3_gnn_res_b, L3_gnn_gamma, L3_gnn_beta), axis=-1)
    return x

_drawn_inputs = setup_inputs


def setup_inputs(seed=0):
    import zlib

    import numpy as np

    out = dict(_drawn_inputs(seed))
    spreads = {'L0_gnn_b_l': (0.0, 0.366),
     'L0_gnn_b_r': (0.0, 0.393),
     'L0_gnn_bias': (0.0, 0.8),
     'L0_gnn_gamma': (1.0, 0.2),
     'L0_gnn_beta': (0.0, 0.1),
     'L1_gnn_k_b1': (0.0, 0.1),
     'L1_gnn_k_b2': (0.0, 0.1),
     'L1_gnn_v_b1': (0.0, 0.1),
     'L1_gnn_v_b2': (0.0, 0.1),
     'L1_gnn_gamma': (1.0, 0.2),
     'L1_gnn_beta': (0.0, 0.1),
     'L2_gnn_bq': (0.0, 0.8),
     'L2_gnn_bk': (0.0, 0.8),
     'L2_gnn_bv': (0.0, 0.1),
     'L2_gnn_bo': (0.0, 0.1),
     'L2_gnn_bf': (0.0, 0.1),
     'L2_gnn_gamma': (1.0, 0.2),
     'L2_gnn_beta': (0.0, 0.1),
     'L3_gnn_bias': (0.0, 0.627),
     'L3_gnn_res_b': (0.0, 0.436),
     'L3_gnn_gamma': (1.0, 0.2),
     'L3_gnn_beta': (0.0, 0.1)}
    factors = {'L2_gnn_Wq': 8.0, 'L2_gnn_Wk': 8.0}
    for name, (base, spread) in spreads.items():
        noise = np.random.default_rng([zlib.crc32(name.encode()), seed]).standard_normal(out[name].shape)
        drawn = base * np.exp(spread * noise) if base else spread * noise
        out[name] = jnp.asarray(drawn.astype(out[name].dtype))
    for name, factor in factors.items():
        out[name] = (out[name] * factor).astype(out[name].dtype)
    return out
```

```python
import concourse.bass as bass
from concourse import mybir
from contextlib import ExitStack

F32 = mybir.dt.float32
I32 = mybir.dt.int32
BF16 = mybir.dt.bfloat16
ALU = mybir.AluOpType
ACT = mybir.ActivationFunctionType
AX = mybir.AxisListType

NODES, EDGES, D = 3125, 100000, 64
P = 128
K = 25
NP = NODES // K
NPAD = P * K
C = 8
J = 784
NCH = J // C
EPAD = P * J
RELS = 64
SH = 9
CH = 16
HEADS = [4, 8, 4, 4]
SUMS = [68, 136, 68, 64]
ROW = [s + h for s, h in zip(SUMS, HEADS)]
NEG = -1.0e30
MAGIC = 12582912.0
GROUPS = [(k, min(4, K - k)) for k in range(0, K, 4)]
assert NP * K == NODES and NCH % 2 == 0 and EPAD >= EDGES

W_COLS = {}
_at = 0
for _n, _w in (("W_l", 64), ("W_r", 64), ("Wq1", 128), ("W_self", 64), ("k_w1", 64), ("v_w1", 64), ("Wk", 64),
               ("Wv", 64), ("Wq2", 64), ("Wf", 64), ("Wo", 64), ("res_w", 64), ("comp", 64)):
    W_COLS[_n] = (_at, _at + _w)
    _at += _w
W_ALL = _at
V_NAMES = ["b_l", "b_r", "zero_q0", "zero_q1", "zero_s", "bk", "bv", "bq", "bf", "att", "bias0", "gamma0", "beta0",
           "gamma1", "beta1", "bo", "gamma2", "beta2", "bias3", "res_b", "gamma3", "beta3"]
V_AT = {n: i * 64 for i, n in enumerate(V_NAMES)}
V_ALL = 64 * len(V_NAMES)


def graph_kernel(nc, x, dst_shifted, src, ea16, ea64, ea9, etype, ew, w64, we, cfix, w2, b1, b2, wout, vecs, basis,
                 out):
    scratch = {}

    def dram(name, shape, dt=F32):
        scratch[name] = nc.dram_tensor(name, shape, dt, kind="Internal").ap()
        return scratch[name]

    xl_tab, xr_tab = dram("xl_tab", [NPAD, 64]), dram("xr_tab", [NPAD, 64])
    x1_tab, q1_tab = dram("x1_tab", [NPAD, 64]), dram("q1_tab", [NPAD, 128])
    kv_tab, q2_tab = dram("kv_tab", [NPAD, 128]), dram("q2_tab", [NPAD, 64])
    rel_tab = dram("rel_tab", [NPAD * RELS, 64])
    scan_tabs = [dram(f"scan{l}", [EPAD, ROW[l]]) for l in range(4)]
    carry_tabs = [dram(f"carry{l}", [P + 1, ROW[l]]) for l in range(4)]
    relidx = dram("relidx", [P, J], I32)
    dst_of_edges = dst_shifted[1:1 + EPAD].rearrange("(p j) -> p j", j=J)

    uses = {}

    def unique(name):
        uses[name] = uses.get(name, 0) + 1
        return name if uses[name] == 1 else f"{name}_{uses[name]}"

    top = ExitStack()
    with top:
        def sb(name, shape, dt=F32, ctx=top):
            return ctx.enter_context(nc.sbuf_tensor(unique(name), shape, dt))

        X = sb("X", [P, K, D])
        KEEP = sb("KEEP", [P, K, 64])
        W = sb("W", [64, W_ALL])
        VEC = sb("VEC", [P, V_ALL])
        WO_T = sb("WO_T", [P, 64])
        RESW_T = sb("RESW_T", [64, 64])
        REL_W = sb("REL_W", [64, RELS, 64])
        IDENT = sb("IDENT", [P, P])
        ONES = sb("ONES", [P, P])
        SAME = sb("SAME", [P, J])
        BREAK = sb("BREAK", [P, J])
        HAS = sb("HAS", [P, K])
        END_AT = sb("END_AT", [P, K], I32)
        CARRY_AT = sb("CARRY_AT", [P, K], I32)
        PASS = sb("PASS", [P, 1])
        SC = [sb(f"SC{b}", [P, 136, 1 + C]) for b in range(2)]
        MS = [sb(f"MS{b}", [P, 8, 1 + C]) for b in range(2)]

        parked = top.enter_context(nc.semaphore("parked"))

        open_semaphores = []

        def end_phase():
            nc.clear_and_free_semaphores(list(open_semaphores))
            open_semaphores.clear()
            nc.all_engine_barrier()

        def phase_semaphore(name):
            sem = nc.alloc_semaphore(unique(name))
            open_semaphores.append(sem)
            return sem

        def vec(name, n=1):
            return VEC[:, V_AT[name]:V_AT[name] + 64 * n]

        def wcol(a, b=None):
            return W[:, W_COLS[a][0]:W_COLS[b or a][1]]

        def over_nodes(v, n=NP):
            return v[0:n, :].unsqueeze(1).to_broadcast([n, K, v.shape[1]])

        class Steps:

            def __init__(self, eng, sem, base=0):
                self.eng, self.sem, self.base, self.n = eng, sem, base, 0

            def do(self, ins):
                ins.then_inc(self.sem, 1)
                self.n += 1
                return ins

            def wait(self, back=0):
                self.eng.wait_ge(self.sem, self.base + (self.n - back))

            def then(self, ins):
                self.do(ins)
                self.wait()

        def chunks(eng, step):
            step(0, 0, 0, True, False)
            step(1, 0, 1, False, False)
            with eng.Fori(1, NCH // 2 - 1) as n:
                step(n * 2, n, 0, False, False)
                step(n * 2 + 1, n, 1, False, False)
            step(NCH - 2, NCH // 2 - 1, 0, False, False)
            step(NCH - 1, NCH // 2 - 1, 1, False, True)

        def wait(eng, sem, value):
            if not isinstance(value, int) or value > 0:
                eng.wait_ge(sem, value)
                if eng is nc.sync and not isinstance(value, int):
                    eng.sem_inc(parked, 1)

        HB = 16
        with ExitStack() as ctx:
            def s(name):
                return phase_semaphore(name)

            DSTX = sb("DSTX", [P, 2, J], I32, ctx)
            TYPES = sb("TYPES", [P, 2, J], I32, ctx)
            RIDX = sb("RIDX", [P, J], I32, ctx)
            HI = sb("HI", [P, J], F32, ctx)
            LO = sb("LO", [P, J], F32, ctx)
            IOTA = sb("IOTA", [P, P], I32, ctx)
            IOTAF = sb("IOTAF", [P, P], F32, ctx)
            OH = [sb(f"OH{b}", [P, HB, P], BF16, ctx) for b in range(2)]
            OL = [sb(f"OL{b}", [P, HB, K], BF16, ctx) for b in range(2)]
            ZB = sb("ZB", [P, P], BF16, ctx)
            TRI = sb("TRI", [P, P], F32, ctx)
            BASIS = sb("BASIS", [64, 64, 64], F32, ctx)
            COMP_T = sb("COMP_T", [64, 64], F32, ctx)
            ST = sb("ST", [P, 10, K], F32, ctx)
            COUNTS = ctx.enter_context(nc.psum_tensor(unique("COUNTS"), [P, 512], F32))
            PS = ctx.enter_context(nc.psum_tensor(unique("PS"), [P, 512], F32))
            PR = [ctx.enter_context(nc.psum_tensor(unique(f"PR{b}"), [P, 512], F32)) for b in range(2)]
            loaded, dst_in, types_in, basis_in = s("loaded"), s("dst_in"), s("types_in"), s("basis_in")
            consts, dve, hot, hot_used, counted = s("consts"), s("dve"), s("hot"), s("hot_used"), s("counted")
            totals, offs, ridx_ready, ridx_out = s("totals"), s("offs"), s("ridx_ready"), s("ridx_out")
            tposed, t_copied, rel_w, rel_c = s("tposed"), s("t_copied"), s("rel_w"), s("rel_c")
            with nc.Block() as block:
                @block.sync
                def _(sp):
                    sp.dma_start(DSTX[:, 0, :], dst_shifted[1:1 + EPAD].rearrange("(p j) -> p j", j=J))\
                      .then_inc(dst_in, 16)
                    sp.dma_start(DSTX[:, 1, :], dst_shifted[0:EPAD].rearrange("(p j) -> p j", j=J))\
                      .then_inc(dst_in, 16)
                    sp.dma_start(W[:, :], w64).then_inc(loaded, 16)
                    sp.dma_start(TYPES[:, 0, :], src).then_inc(types_in, 16)
                    sp.dma_start(TYPES[:, 1, :], etype).then_inc(types_in, 16)
                    sp.dma_start(X[:, :, :], x.rearrange("(p k) f -> p k f", k=K)).then_inc(loaded, 16)
                    sp.dma_start(VEC[:, :], vecs.to_broadcast([P, V_ALL])).then_inc(loaded, 16)
                    sp.dma_start(WO_T[:, :], wout).then_inc(loaded, 16)
                    sp.dma_start(BASIS[:, :, :], basis).then_inc(basis_in, 16)
                    sp.wait_ge(ridx_ready, 1)
                    sp.dma_start(relidx, RIDX[:, :]).then_inc(ridx_out, 16)
                    sp.wait_ge(ridx_out, 16)
                    sp.wait_ge(loaded, 64)

                @block.gpsimd
                def _(pool):
                    nc.gpsimd.iota(IOTA[:, :], [[1, P]], base=0, channel_multiplier=0).then_inc(consts, 1)
                    nc.gpsimd.memset(IDENT[:, :], 0.0).then_inc(consts, 1)
                    nc.gpsimd.memset(ONES[:, :], 1.0).then_inc(consts, 1)
                    nc.gpsimd.memset(TRI[:, :], 1.0).then_inc(consts, 1)
                    nc.gpsimd.memset(ZB[:, :], 0.0).then_inc(consts, 1)
                    pool.wait_ge(consts, 5)
                    nc.gpsimd.affine_select(out=IDENT[:, :], in_=IDENT[:, :], compare_op=ALU.not_equal, fill=1.0,
                                            base=0, pattern=[[-1, P]], channel_multiplier=1).then_inc(consts, 1)
                    nc.gpsimd.affine_select(out=TRI[:, :], in_=TRI[:, :], compare_op=ALU.is_gt, fill=0.0,
                                            base=0, pattern=[[1, P]], channel_multiplier=-1).then_inc(consts, 1)

                @block.vector
                def _(v):
                    st = Steps(v, dve)
                    v.wait_ge(consts, 7)
                    st.do(nc.vector.tensor_copy(IOTAF[:, :], IOTA[:, :]))
                    v.wait_ge(dst_in, 32)
                    st.then(nc.vector.tensor_scalar(HI[:, :], DSTX[:, 0, :], 1.0 / K, -(K - 1) / 2 / K, ALU.mult,
                                                    ALU.add))
                    st.then(nc.vector.tensor_scalar(HI[:, :], HI[:, :], MAGIC, None, ALU.add))
                    st.then(nc.vector.tensor_scalar(HI[:, :], HI[:, :], -MAGIC, None, ALU.add))
                    st.then(nc.vector.scalar_tensor_tensor(out=LO[:, :], in0=HI[:, :], scalar=-float(K),
                                                           in1=DSTX[:, 0, :], op0=ALU.mult, op1=ALU.add))
                    def hots(t, b):
                        at = bass.ds(t * HB, HB)
                        nc.vector.tensor_tensor(OH[b][:, :, :], IOTAF[:, :].unsqueeze(1).to_broadcast([P, HB, P]),
                                                HI[:, at].unsqueeze(2).to_broadcast([P, HB, P]),
                                                ALU.is_equal).then_inc(hot, 1)
                        nc.vector.tensor_tensor(OL[b][:, :, :],
                                                IOTAF[:, 0:K].unsqueeze(1).to_broadcast([P, HB, K]),
                                                LO[:, at].unsqueeze(2).to_broadcast([P, HB, K]),
                                                ALU.is_equal).then_inc(hot, 1)

                    hots(0, 0)
                    hots(1, 1)
                    v.wait_ge(hot_used, 1)
                    hots(2, 0)
                    with v.Fori(1, J // HB // 2) as i:
                        v.wait_ge(hot_used, i * 2)
                        hots(i * 2 + 1, 1)
                        v.wait_ge(hot_used, i * 2 + 1)
                        hots(i * 2 + 2, 0)
                    st.do(nc.vector.tensor_tensor(SAME[:, :], DSTX[:, 0, :], DSTX[:, 1, :], ALU.is_equal))
                    st.do(nc.vector.tensor_tensor(ST[:, 0, 0:1], DSTX[:, 0, 0:1], DSTX[:, 0, J - 1:J],
                                                  ALU.is_equal))
                    st.wait()
                    st.do(nc.vector.tensor_scalar(BREAK[:, :], SAME[:, :], -1.0, -NEG, ALU.add, ALU.mult))
                    st.then(nc.vector.tensor_tensor(ST[:, 0, 0:1], ST[:, 0, 0:1], SAME[:, 0:1], ALU.mult))
                    st.do(nc.vector.tensor_scalar(PASS[:, :], ST[:, 0, 0:1], -1.0, -NEG, ALU.add, ALU.mult))
                    v.wait_ge(types_in, 32)
                    nc.vector.scalar_tensor_tensor(out=RIDX[:, :], in0=TYPES[:, 0, :], scalar=float(RELS),
                                                   in1=TYPES[:, 1, :], op0=ALU.mult, op1=ALU.add)\
                      .then_inc(ridx_ready, 1)
                    v.wait_ge(counted, 1)
                    st.then(nc.vector.tensor_copy(ST[:, 1, :], COUNTS[:, 0:K]))
                    st.then(nc.vector.tensor_tensor_scan(ST[:, 2, :], ONES[:, 0:K], ST[:, 1, :], 0.0, ALU.mult,
                                                         ALU.add))
                    nc.vector.tensor_copy(ST[:, 3, 0:1], ST[:, 2, K - 1:K]).then_inc(totals, 1)
                    v.wait_ge(offs, 1)
                    st.do(nc.vector.tensor_scalar(ST[:, 4, :], ST[:, 2, :], PS[:, 0:1], None, ALU.add))
                    st.do(nc.vector.tensor_scalar(HAS[:, :], ST[:, 1, :], 0.0, None, ALU.is_gt))
                    st.wait()
                    st.do(nc.vector.tensor_tensor(ST[:, 5, :], ST[:, 4, :], ST[:, 1, :], ALU.subtract))
                    st.then(nc.vector.tensor_scalar(ST[:, 6, :], ST[:, 4, :], -1.0, 0.0, ALU.add, ALU.max))
                    st.do(nc.vector.tensor_copy(END_AT[:, :], ST[:, 6, :]))
                    st.then(nc.vector.tensor_scalar(ST[:, 7, :], ST[:, 6, :], 1.0 / J, -(J - 1) / 2 / J, ALU.mult,
                                                    ALU.add))
                    st.then(nc.vector.tensor_scalar(ST[:, 7, :], ST[:, 7, :], MAGIC, None, ALU.add))
                    st.then(nc.vector.tensor_scalar(ST[:, 7, :], ST[:, 7, :], -MAGIC, None, ALU.add))
                    st.then(nc.vector.scalar_tensor_tensor(out=ST[:, 8, :], in0=ST[:, 7, :], scalar=float(J),
                                                           in1=ST[:, 5, :], op0=ALU.mult, op1=ALU.is_gt))
                    st.then(nc.vector.tensor_tensor(ST[:, 8, :], ST[:, 8, :], HAS[:, :], ALU.mult))
                    st.then(nc.vector.scalar_tensor_tensor(out=ST[:, 9, :], in0=ST[:, 7, :], scalar=-1.0 - P,
                                                           in1=ST[:, 8, :], op0=ALU.add, op1=ALU.mult))
                    st.then(nc.vector.tensor_scalar(CARRY_AT[:, :], ST[:, 9, :], float(P), None, ALU.add))
                    for n in range(2):
                        v.wait_ge(tposed, n + 1)
                        nc.vector.tensor_copy((RESW_T, COMP_T)[n][:, :], PR[n][0:64, 0:64]).then_inc(t_copied, 1)
                    for g in range(8):
                        v.wait_ge(rel_w, g + 1)
                        nc.vector.tensor_copy(REL_W[:, :, 8 * g:8 * g + 8],
                                              PR[g % 2][0:64, :].rearrange("i (o r) -> i r o", o=8))\
                          .then_inc(rel_c, 1)

                @block.tensor
                def _(pe):
                    pe.wait_ge(consts, 7)
                    nc.tensor.matmul(COUNTS[:, 0:K], ZB[:, :], ZB[:, 0:K], start=True, stop=False)

                    def count(t, b):
                        pe.wait_ge(hot, t * 2 + 2)
                        for c in range(HB):
                            last = nc.tensor.matmul(COUNTS[:, 0:K], OH[b][:, c, :], OL[b][:, c, :], start=False,
                                                    stop=False)
                        last.then_inc(hot_used, 1)

                    count(0, 0)
                    with pe.Fori(0, J // HB // 2) as i:
                        count(i * 2 + 1, 1)
                        count(i * 2 + 2, 0)
                    nc.tensor.matmul(COUNTS[:, 0:K], ZB[:, :], ZB[:, 0:K], start=False, stop=True)\
                      .then_inc(counted, 1)
                    pe.wait_ge(totals, 1)
                    nc.tensor.matmul(PS[:, 0:1], TRI[:, :], ST[:, 3, 0:1], start=True, stop=True)\
                      .then_inc(offs, 1)
                    pe.wait_ge(loaded, 64)
                    nc.tensor.transpose(PR[0][0:64, 0:64], wcol("res_w"), IDENT[0:64, 0:64]).then_inc(tposed, 1)
                    nc.tensor.transpose(PR[1][0:64, 0:64], wcol("comp"), IDENT[0:64, 0:64]).then_inc(tposed, 1)
                    pe.wait_ge(t_copied, 2)
                    pe.wait_ge(basis_in, 16)
                    for g in range(8):
                        if g >= 2:
                            pe.wait_ge(rel_c, g - 1)
                        for o in range(8):
                            last = nc.tensor.matmul(PR[g % 2][0:64, o * 64:o * 64 + 64],
                                                    BASIS[:, :, 8 * g + o], COMP_T[:, :], start=True, stop=True)
                        last.then_inc(rel_w, 1)

        def project(weights, n_out, biases, tables, keep):
            per = 512 // n_out
            units = [(k, min(per, K - k)) for k in range(0, K, per)]
            with ExitStack() as ctx:
                def s(name):
                    return phase_semaphore(name)

                XT = sb("XT", [64, NPAD], F32, ctx)
                TAB = sb("TAB", [P, K, n_out], F32, ctx)
                PT = [ctx.enter_context(nc.psum_tensor(unique(f"PT{b}"), [P, 512], F32)) for b in range(2)]
                PO = [ctx.enter_context(nc.psum_tensor(unique(f"PO{b}"), [P, 512], F32)) for b in range(4)]
                t_done, t_copied, m_done, m_copied, stored = (s("t_done"), s("t_copied"), s("m_done"),
                                                              s("m_copied"), s("stored"))
                with nc.Block() as block:
                    @block.tensor
                    def _(pe):
                        for g, (k0, m) in enumerate(GROUPS):
                            if g >= 2:
                                pe.wait_ge(t_copied, g - 1)
                            for c in range(m):
                                last = nc.tensor.transpose(PT[g % 2][0:64, c * P:(c + 1) * P], X[:, k0 + c, :],
                                                           IDENT[:, :])
                            last.then_inc(t_done, 1)
                        for u, (k0, m) in enumerate(units):
                            pe.wait_ge(t_copied, min((k0 + m - 1) // 4 + 1, len(GROUPS)))
                            if u >= 4:
                                pe.wait_ge(m_copied, u - 3)
                            for c in range(m):
                                last = nc.tensor.matmul(PO[u % 4][:, c * n_out:(c + 1) * n_out],
                                                        XT[:, (k0 + c) * P:(k0 + c + 1) * P], weights,
                                                        start=True, stop=True)
                            last.then_inc(m_done, 1)

                    @block.scalar
                    def _(act):
                        for g, (k0, m) in enumerate(GROUPS):
                            act.wait_ge(t_done, g + 1)
                            nc.scalar.activation(XT[:, k0 * P:(k0 + m) * P], PT[g % 2][0:64, 0:m * P], ACT.Copy)\
                              .then_inc(t_copied, 1)

                    @block.vector
                    def _(v):
                        for u, (k0, m) in enumerate(units):
                            v.wait_ge(m_done, u + 1)
                            nc.vector.tensor_tensor(
                                TAB[:, k0:k0 + m, :],
                                PO[u % 4][:, 0:m * n_out].rearrange("p (k n) -> p k n", k=m),
                                biases.unsqueeze(1).to_broadcast([P, m, n_out]), ALU.add).then_inc(m_copied, 1)
                        if keep is not None:
                            v.wait_ge(m_copied, len(units))
                            nc.vector.tensor_copy(KEEP[:, :, :], TAB[:, :, keep:keep + 64])\
                              .then_inc(m_copied, 1)

                    @block.sync
                    def _(sp):
                        sp.wait_ge(m_copied, len(units))
                        for tab, at, width in tables:
                            source = X[:, :, :] if at is None else TAB[:, :, at:at + width]
                            sp.dma_start(tab.rearrange("(p k) f -> p k f", k=K), source).then_inc(stored, 16)
                        sp.wait_ge(stored, 16 * len(tables))

        def project_relations():
            with ExitStack() as ctx:
                def s(name):
                    return phase_semaphore(name)

                XT = sb("XT", [64, NPAD], F32, ctx)
                YS = [sb(f"YS{b}", [P, RELS * 64], F32, ctx) for b in range(2)]
                PT = [ctx.enter_context(nc.psum_tensor(unique(f"PT{b}"), [P, 512], F32)) for b in range(2)]
                PO = [ctx.enter_context(nc.psum_tensor(unique(f"PO{b}"), [P, 512], F32)) for b in range(6)]
                t_done, t_copied, m_done = s("t_done"), s("t_copied"), s("m_done")
                act_copied, dve_copied = s("act_copied"), s("dve_copied")
                stored = [s("stored0"), s("stored1")]
                res_done, res_copied = s("res_done"), s("res_copied")
                rel_v = rel_tab.rearrange("(p k r) f -> k p (r f)", k=K, r=RELS)
                wv = REL_W[:, :, :].rearrange("i r o -> i (r o)")
                with nc.Block() as block:
                    @block.tensor
                    def _(pe):
                        for g, (k0, m) in enumerate(GROUPS):
                            if g >= 2:
                                pe.wait_ge(t_copied, g - 1)
                            for c in range(m):
                                last = nc.tensor.transpose(PT[g % 2][0:64, c * P:(c + 1) * P], X[:, k0 + c, :],
                                                           IDENT[:, :])
                            last.then_inc(t_done, 1)
                        pe.wait_ge(t_copied, len(GROUPS))
                        for r in range(4):
                            ks = range(8 * r, min(8 * r + 8, K))
                            if r >= 2:
                                pe.wait_ge(res_copied, r - 1)
                            for c, k in enumerate(ks):
                                last = nc.tensor.matmul(PT[r % 2][:, c * 64:c * 64 + 64], XT[:, k * P:(k + 1) * P],
                                                        RESW_T[:, :], start=True, stop=True)
                            last.then_inc(res_done, 1)
                        for u in range(K * 8):
                            k, g = u // 8, u % 8
                            if u >= 6:
                                w = u - 6
                                pe.wait_ge(act_copied if w % 2 == 0 else dve_copied, w // 2 + 1)
                            nc.tensor.matmul(PO[u % 6][:, :], XT[:, k * P:(k + 1) * P],
                                             wv[:, g * 512:(g + 1) * 512], start=True, stop=True)\
                              .then_inc(m_done, 1)

                    @block.scalar
                    def _(act):
                        for g, (k0, m) in enumerate(GROUPS):
                            act.wait_ge(t_done, g + 1)
                            nc.scalar.activation(XT[:, k0 * P:(k0 + m) * P], PT[g % 2][0:64, 0:m * P], ACT.Copy)\
                              .then_inc(t_copied, 1)
                        for u in range(0, K * 8, 2):
                            k, g = u // 8, u % 8
                            act.wait_ge(m_done, u + 1)
                            if k >= 2 and g == 0:
                                act.wait_ge(stored[k % 2], 16 * (k // 2))
                            nc.scalar.activation(YS[k % 2][:, g * 512:(g + 1) * 512], PO[u % 6][:, :], ACT.Copy)\
                              .then_inc(act_copied, 1)

                    @block.vector
                    def _(v):
                        for r in range(4):
                            m = min(8 * r + 8, K) - 8 * r
                            v.wait_ge(res_done, r + 1)
                            nc.vector.tensor_tensor(
                                KEEP[:, 8 * r:8 * r + m, :], PT[r % 2][:, 0:m * 64].rearrange("p (k n) -> p k n", k=m),
                                vec("res_b").unsqueeze(1).to_broadcast([P, m, 64]), ALU.add).then_inc(res_copied, 1)
                        v.wait_ge(res_copied, 4)
                        nc.vector.tensor_scalar(KEEP[:, :, :], KEEP[:, :, :], 0.0, None, ALU.max)\
                          .then_inc(res_copied, 1)
                        for u in range(1, K * 8, 2):
                            k, g = u // 8, u % 8
                            v.wait_ge(m_done, u + 1)
                            if k >= 2 and g == 1:
                                v.wait_ge(stored[k % 2], 16 * (k // 2))
                            nc.vector.tensor_copy(YS[k % 2][:, g * 512:(g + 1) * 512], PO[u % 6][:, :])\
                              .then_inc(dve_copied, 1)

                    @block.sync
                    def _(sp):
                        for k in range(K):
                            sp.wait_ge(act_copied, 4 * k + 4)
                            sp.wait_ge(dve_copied, 4 * k + 4)
                            sp.dma_start(rel_v[k, :, :], YS[k % 2][:, :]).then_inc(stored[k % 2], 16)
                        sp.wait_ge(stored[0], 16 * ((K + 1) // 2))
                        sp.wait_ge(stored[1], 16 * (K // 2))

        def row_view(tab, t):
            return tab.rearrange("(p j) f -> p j f", j=J)[:, bass.ds(t * C, C), :]

        def before(n, b):
            return n - (1 - b)

        class Edges:

            def __init__(self, ctx, layer, tables, indices):
                self.layer, self.tables, self.indices = layer, tables, indices
                self.H, self.R = HEADS[layer], SUMS[layer]
                self.FE = self.H * CH
                self.weights = self.R > self.FE
                self.running_max = layer < 2
                self.ctx = ctx
                H, R = self.H, self.R
                self.IDX = {n: self.pair(f"IDX_{n}", [P, C], I32) for n in indices}
                self.G = [self.pair(f"G{g}", [P, C, w]) for g, (_, w, _) in enumerate(tables)]
                self.MSG = sb("MSG", [P, R, 1 + C], F32, ctx)
                self.DEC = self.pair("DEC", [P, R, 1 + C])
                self.OUT = self.pair("OUT", [P, C, R + H])
                self.EX = self.pair("EX", [P, 2, H, C])
                self.ARG = sb("ARG", [P, 2, H, C], F32, ctx)
                self.LG = sb("LG", [P, H, 1 + C], F32, ctx)
                self.BR = sb("BR", [P, H, 1 + C], F32, ctx)
                self.T1 = sb("T1", [P, C, self.FE], F32, ctx)
                self.idx_in, self.attr_in, self.stored = (
                    [self.sem(f"{name}{b}") for b in range(2)] for name in ("idx_in", "attr_in", "stored"))
                self.rows_in = [[self.sem(f"rows{g}_in{b}") for b in range(2)] for g in range(len(tables))]
                self.ready, self.a_steps, self.b_steps = self.sem("ready"), self.sem("a_steps"), self.sem("b_steps")
                self.args_ready, self.exps_ready = self.sem("args_ready"), self.sem("exps_ready")
                self.decays_ready, self.scanned = self.sem("decays_ready"), self.sem("scanned")
                self.copied_out = self.sem("copied_out")

            def sem(self, name):
                return phase_semaphore(name)

            def pair(self, name, shape, dt=F32):
                return [sb(f"{name}{b}", shape, dt, self.ctx) for b in range(2)]

            def bank(self, name):
                return self.ctx.enter_context(nc.psum_tensor(unique(name), [P, 512], F32))

            def constants(self):
                fills = [(SC[1][:, :, :], 0.0), (MS[1][:, :, :], NEG), (self.BR[:, :, :], NEG)]
                fills += [(self.DEC[b][:, :, :], 0.0) for b in range(2)]
                fills += [(self.OUT[b][:, :, self.R:], 0.0) for b in range(2)]
                for ap, value in fills:
                    nc.gpsimd.memset(ap, value).then_inc(self.ready, 1)
                assert len(fills) == self.N_READY

            N_READY = 7

            def gathers(self, pool):
                def step(t, n, b, first, last):
                    wait(pool, self.idx_in[b], (n + 1) * (16 * len(self.indices)))
                    if not first:
                        wait(pool, self.scanned, t - 1)
                        if self.layer != 3:
                            wait(pool, self.args_ready, t - 1)
                    pool.sem_inc(parked, 1)
                    for c in range(C):
                        for g, (tab, _, which) in enumerate(self.tables):
                            pool.indirect_dma_start(
                                out=self.G[g][b][:, c, :], out_offset=None, in_=tab,
                                in_offset=bass.IndirectOffsetOnAxis(ap=self.IDX[which][b][:, c:c + 1], axis=0),
                            ).then_inc(self.rows_in[g][b], 16)
                chunks(pool, step)

            def load_indices(self, sp, t, n, b, first):
                if not first:
                    for g in range(len(self.tables)):
                        wait(sp, self.rows_in[g][b], n * (16 * C))
                for name, source in self.indices.items():
                    sp.dma_start(self.IDX[name][b][:, :], source[:, bass.ds(t * C, C)])\
                      .then_inc(self.idx_in[b], 16)

            def maxima(self, v, st, t, n, b, first):
                nc_v, H = nc.vector, self.H
                st.do(nc_v.tensor_copy(self.LG[:, :, 0:1], MS[1 - b][:, 0:H, C:C + 1]))
                st.wait()
                if not first:
                    wait(v, self.copied_out, (t - 1) * 2)
                flat = lambda ap: ap.rearrange("p h j -> p (h j)")
                st.then(nc_v.tensor_tensor_scan(flat(MS[b][:, 0:H, :]), flat(self.BR[:, :, :]),
                                                flat(self.LG[:, :, :]), 0.0, ALU.add, ALU.max))
                if not first:
                    wait(v, self.exps_ready, t)
                st.do(nc_v.tensor_tensor(self.ARG[:, 0, :, :], MS[b][:, 0:H, 0:C], MS[b][:, 0:H, 1:1 + C],
                                         ALU.subtract))
                st.then(nc_v.tensor_tensor(self.ARG[:, 1, :, :], self.LG[:, :, 1:1 + C], MS[b][:, 0:H, 1:1 + C],
                                           ALU.subtract))
                nc_v.tensor_tensor(self.ARG[:, 0, :, :], self.ARG[:, 0, :, :], self.BR[:, :, 1:1 + C], ALU.add)\
                    .then_inc(self.args_ready, 1)

            def breaks(self, st, t):
                st.do(nc.vector.tensor_scalar(self.BR[:, :, 1:1 + C],
                                              BREAK[:, bass.ds(t * C, C)].unsqueeze(1)
                                              .to_broadcast([P, self.H, C]), 1.0, None, ALU.mult))

            def sums(self, v, t, n, b, first, rows, weight=None):
                H, FE, R = self.H, self.FE, self.R
                st = Steps(v, self.b_steps, t * (3 if self.weights else 2))
                wait(v, self.decays_ready, (t + 1) * self.n_decays())
                if weight is None:
                    w = self.EX[b][:, 1, :, :].unsqueeze(2).to_broadcast([P, H, CH, C])
                    st.do(nc.vector.tensor_tensor(
                        self.MSG[:, 0:FE, 1:1 + C].rearrange("p (h c) j -> p h c j", c=CH),
                        rows.rearrange("p j (h c) -> p h c j", c=CH), w, ALU.mult))
                    st.do(nc.vector.tensor_copy(self.MSG[:, FE:R, 1:1 + C], self.EX[b][:, 1, :, :]))
                else:
                    st.do(nc.vector.tensor_tensor(self.MSG[:, :, 1:1 + C], rows.rearrange("p j f -> p f j"),
                                                  weight.unsqueeze(1).to_broadcast([P, FE, C]), ALU.mult))
                st.do(nc.vector.tensor_copy(self.MSG[:, :, 0:1], SC[1 - b][:, 0:R, C:C + 1]))
                st.wait()
                if not first:
                    wait(v, self.copied_out, (t - 1) * self.n_copies())
                flat = lambda ap: ap.rearrange("p r j -> p (r j)")
                nc.vector.tensor_tensor_scan(flat(SC[b][:, 0:R, :]), flat(self.DEC[b][:, :, :]),
                                             flat(self.MSG[:, :, :]), 0.0, ALU.mult, ALU.add)\
                    .then_inc(self.scanned, 1)
                wait(v, self.scanned, t + 1)

            def n_decays(self):
                return 2 if self.running_max else 1

            def n_copies(self):
                return 2 if self.running_max else 1

            def factors(self, act, t, n, b, first):
                H, FE, R = self.H, self.FE, self.R
                if self.layer != 3:
                    wait(act, self.args_ready, t + 1)
                if not first:
                    wait(act, self.scanned, t - 1)
                if self.running_max:
                    nc.scalar.activation(self.EX[b][:, :, :, :], self.ARG[:, :, :, :], ACT.Exp)\
                      .then_inc(self.exps_ready, 1)
                    wait(act, self.exps_ready, t + 1)
                    decay = self.EX[b][:, 0, :, :]
                    nc.scalar.activation(self.DEC[b][:, 0:FE, 1:1 + C].rearrange("p (h c) j -> p h c j", c=CH),
                                         decay.unsqueeze(2).to_broadcast([P, H, CH, C]), ACT.Copy)\
                      .then_inc(self.decays_ready, 1)
                    nc.scalar.activation(self.DEC[b][:, FE:R, 1:1 + C], decay, ACT.Copy)\
                      .then_inc(self.decays_ready, 1)
                    return
                if self.layer == 2:
                    nc.scalar.activation(self.EX[b][:, 1, :, :], self.ARG[:, 1, :, :], ACT.Exp)\
                      .then_inc(self.exps_ready, 1)
                    wait(act, self.exps_ready, t + 1)
                act.sem_inc(parked, 1)
                nc.scalar.activation(self.DEC[b][:, :, 1:1 + C],
                                     SAME[:, bass.ds(t * C, C)].unsqueeze(1).to_broadcast([P, R, C]), ACT.Copy)\
                  .then_inc(self.decays_ready, 1)

            def store_rows(self, act, t, n, b, early):
                R, H = self.R, self.H
                wait(act, self.scanned, t + 1)
                if not early:
                    wait(act, self.stored[b], n * 16)
                nc.scalar.activation(self.OUT[b][:, :, 0:R], SC[b][:, 0:R, 1:1 + C].rearrange("p r j -> p j r"),
                                     ACT.Copy).then_inc(self.copied_out, 1)
                if self.running_max:
                    nc.scalar.activation(self.OUT[b][:, :, R:R + H],
                                         MS[b][:, 0:H, 1:1 + C].rearrange("p r j -> p j r"), ACT.Copy)\
                      .then_inc(self.copied_out, 1)
                wait(act, self.copied_out, (t + 1) * self.n_copies())
                act.dma_start(row_view(scan_tabs[self.layer], t), self.OUT[b][:, :, :])\
                   .then_inc(self.stored[b], 16)

            def drain_stores(self, act):
                for b in range(2):
                    wait(act, self.stored[b], NCH // 2 * 16)

        def edges_0(src_ap, dst_ap):
            with ExitStack() as ctx:
                e = Edges(ctx, 0, [(xl_tab, 64, "src"), (xr_tab, 64, "dst")], {"src": src_ap, "dst": dst_ap})
                ATTR = e.pair("ATTR", [P, C, 16])
                ATTR_T = sb("ATTR_T", [P, P], F32, ctx)
                WE8 = sb("WE8", [P, C, 64], F32, ctx)
                TR, PROJ = [e.bank("TR0"), e.bank("TR1")], [e.bank("PROJ0"), e.bank("PROJ1")]
                attr_t, attr_c, projected, we_in, cleared = (e.sem("attr_t"), e.sem("attr_c"), e.sem("projected"),
                                                             e.sem("we_in"), e.sem("cleared"))
                with nc.Block() as block:
                    @block.sync
                    def _(sp):
                        wait(sp, cleared, 1)
                        for c in range(C):
                            sp.dma_start(WE8[16 * c:16 * c + 16, c, :], we).then_inc(we_in, 16)

                        def step(t, n, b, first, last):
                            e.load_indices(sp, t, n, b, first)
                            if not first:
                                wait(sp, attr_t, t - 1)
                            sp.dma_start(ATTR[b][:, :, :], row_view(ea16, t)).then_inc(e.attr_in[b], 16)
                        chunks(sp, step)

                    @block.gpsimd
                    def _(pool):
                        nc.gpsimd.memset(WE8[:, :, :], 0.0).then_inc(cleared, 1)
                        e.constants()
                        e.gathers(pool)

                    @block.tensor
                    def _(pe):
                        wait(pe, we_in, 16 * C)

                        def step(t, n, b, first, last):
                            wait(pe, e.attr_in[b], (n + 1) * 16)
                            nc.tensor.transpose(TR[b][:, 0:P], ATTR[b][:, :, :].rearrange("p j f -> p (j f)"),
                                                IDENT[:, :]).then_inc(attr_t, 1)
                            wait(pe, attr_c, t + 1)
                            if not first:
                                wait(pe, e.args_ready, t - 1)
                            nc.tensor.matmul(PROJ[b][:, :], ATTR_T[:, :],
                                             WE8[:, :, :].rearrange("p j f -> p (j f)"), start=True, stop=True)\
                              .then_inc(projected, 1)
                        chunks(pe, step)

                    @block.scalar
                    def _(act):
                        wait(act, e.ready, e.N_READY)

                        def step(t, n, b, first, last):
                            wait(act, attr_t, t + 1)
                            if not first:
                                wait(act, projected, t)
                            nc.scalar.activation(ATTR_T[:, :], TR[b][:, 0:P], ACT.Copy).then_inc(attr_c, 1)
                            e.factors(act, t, n, b, first)
                            e.store_rows(act, t, n, b, first)
                        chunks(act, step)
                        e.drain_stores(act)

                    @block.vector
                    def _(v):
                        wait(v, e.ready, e.N_READY)

                        def logits(t, n, b, first):
                            T, LG = e.T1, e.LG
                            st = Steps(v, e.a_steps, t * 10)
                            for g in range(2):
                                wait(v, e.rows_in[g][b], (n + 1) * (16 * C))
                            st.then(nc.vector.tensor_tensor(T[:, :, :], e.G[0][b][:, :, :], e.G[1][b][:, :, :],
                                                            ALU.add))
                            wait(v, projected, t + 1)
                            st.then(nc.vector.tensor_tensor(T[:, :, :], T[:, :, :],
                                                            PROJ[b][:, :].rearrange("p (j f) -> p j f", j=C),
                                                            ALU.add))
                            st.then(nc.vector.scalar_tensor_tensor(out=T[:, :, :], in0=T[:, :, :], scalar=0.2,
                                                                   in1=T[:, :, :], op0=ALU.mult, op1=ALU.max))
                            st.then(nc.vector.tensor_tensor(T[:, :, :], T[:, :, :],
                                                            vec("att").unsqueeze(1).to_broadcast([P, C, 64]),
                                                            ALU.mult))
                            if not first:
                                wait(v, e.args_ready, t)
                            e.breaks(st, t)
                            st.do(nc.vector.tensor_reduce(LG[:, :, 1:1 + C].rearrange("p h j -> p j h"),
                                                          T[:, :, :].rearrange("p j (h c) -> p j h c", c=CH),
                                                          AX.X, ALU.add))
                            e.maxima(v, st, t, n, b, first)
                            assert st.n == 10, st.n

                        def step(t, n, b, first, last):
                            logits(t, n, b, first)
                            e.sums(v, t, n, b, first, e.G[0][b][:, :, :])
                        chunks(v, step)

        def edges_2(src_ap, dst_ap):
            with ExitStack() as ctx:
                e = Edges(ctx, 2, [(kv_tab, 128, "src"), (q2_tab, 64, "dst")], {"src": src_ap, "dst": dst_ap})
                with nc.Block() as block:
                    @block.sync
                    def _(sp):
                        chunks(sp, lambda t, n, b, first, last: e.load_indices(sp, t, n, b, first))

                    @block.gpsimd
                    def _(pool):
                        e.constants()
                        e.gathers(pool)

                    @block.scalar
                    def _(act):
                        wait(act, e.ready, e.N_READY)

                        def step(t, n, b, first, last):
                            e.factors(act, t, n, b, first)
                            e.store_rows(act, t, n, b, first)
                        chunks(act, step)
                        e.drain_stores(act)

                    @block.vector
                    def _(v):
                        wait(v, e.ready, e.N_READY)

                        def scores(t, n, b, first):
                            st = Steps(v, e.a_steps, t * 3)
                            for g in range(2):
                                wait(v, e.rows_in[g][b], (n + 1) * (16 * C))
                            st.then(nc.vector.tensor_tensor(e.T1[:, :, :], e.G[0][b][:, :, 0:64],
                                                            e.G[1][b][:, :, :], ALU.mult))
                            st.then(nc.vector.tensor_reduce(e.LG[:, :, 0:C].rearrange("p h j -> p j h"),
                                                            e.T1[:, :, :].rearrange("p j (h c) -> p j h c", c=CH),
                                                            AX.X, ALU.add))
                            st.then(nc.vector.tensor_scalar(e.LG[:, :, 0:C], e.LG[:, :, 0:C], 1.0 / D ** 0.5, -5.0,
                                                            ALU.mult, ALU.max))
                            if not first:
                                wait(v, e.exps_ready, t)
                            nc.vector.tensor_scalar(e.ARG[:, 1, :, :], e.LG[:, :, 0:C], 5.0, None, ALU.min)\
                              .then_inc(e.args_ready, 1)

                        def step(t, n, b, first, last):
                            scores(t, n, b, first)
                            e.sums(v, t, n, b, first, e.G[0][b][:, :, 64:128])
                        chunks(v, step)

        def edges_3():
            with ExitStack() as ctx:
                e = Edges(ctx, 3, [(rel_tab, 64, "rel")], {"rel": relidx})
                EW = sb("EW", [P, J], F32, ctx)
                ew_in = e.sem("ew_in")
                with nc.Block() as block:
                    @block.sync
                    def _(sp):
                        sp.dma_start(EW[:, :], ew).then_inc(ew_in, 16)
                        chunks(sp, lambda t, n, b, first, last: e.load_indices(sp, t, n, b, first))

                    @block.gpsimd
                    def _(pool):
                        e.constants()
                        e.gathers(pool)

                    @block.scalar
                    def _(act):
                        wait(act, e.ready, e.N_READY)

                        def step(t, n, b, first, last):
                            e.factors(act, t, n, b, first)
                            e.store_rows(act, t, n, b, first)
                        chunks(act, step)
                        e.drain_stores(act)

                    @block.vector
                    def _(v):
                        wait(v, e.ready, e.N_READY)
                        wait(v, ew_in, 16)

                        def step(t, n, b, first, last):
                            wait(v, e.rows_in[0][b], (n + 1) * (16 * C))
                            e.sums(v, t, n, b, first, e.G[0][b][:, :, :], EW[:, bass.ds(t * C, C)])
                        chunks(v, step)

        def edges_1(src_ap, dst_ap):
            with ExitStack() as ctx:
                e = Edges(ctx, 1, [(x1_tab, 64, "src"), (q1_tab, 128, "dst")], {"src": src_ap, "dst": dst_ap})
                EF, S9 = e.pair("EF", [P, C, 64]), e.pair("S9", [P, C, SH])
                XS = e.pair("XS", [P, C, SH, 64])
                XST = e.pair("XST", [P, 5, 512])
                EFT = sb("EFT", [P, 512], F32, ctx)
                HT = [[sb(f"HT{b}{a}", [P, 512], F32, ctx) for a in range(2)] for b in range(2)]
                WKV = e.pair("WKV", [P, 256])
                RW = e.pair("RW", [P, C, 256])
                CF = sb("CF", [P, 5, 256], F32, ctx)
                W1 = sb("W1", [P, P], F32, ctx)
                W2 = sb("W2", [P, 256], F32, ctx)
                B1 = sb("B1", [P, 1], F32, ctx)
                B2F = sb("B2F", [1, 5, 256], F32, ctx)
                B2 = [sb(f"B2{i}", [1, 256], BF16, ctx) for i in range(3)]
                ONEB = sb("ONEB", [1, P], BF16, ctx)
                RING = [e.bank(f"RING{i}") for i in range(3)]
                COLS = [e.bank(f"COLS{i}") for i in range(4)]
                xs_ready, staged, evacuated = e.sem("xs_ready"), e.sem("staged"), e.sem("evacuated")
                col_done, w_copied, col_used = e.sem("col_done"), e.sem("w_copied"), e.sem("col_used")
                w_in, parts = e.sem("w_in"), e.sem("parts")

                STAGES = 13

                def ring(q, b):
                    return (q + b) % 3

                def holder_before(q, b):
                    return next(d for d in range(1, STAGES + 1)
                                if ring((q - d) % STAGES, b if q >= d else 1 - b) == ring(q, b))

                with nc.Block() as block:
                    @block.sync
                    def _(sp):
                        wait(sp, parts, 1)
                        for ap, source in ((CF[:, 0:4, :], cfix[0:512, :].rearrange("(k p) n -> p k n", p=P)),
                                           (CF[0:64, 4, :], cfix[512:576, :]),
                                           (W2[0:64, 0:128], w2[:, 0:128]), (W2[64:128, 128:256], w2[:, 128:256]),
                                           (B1[:, :], b1), (B2F[:, 0, :], b2),
                                           (W1[0:64, :], w64[:, W_COLS["k_w1"][0]:W_COLS["v_w1"][1]]),
                                           (W1[64:128, :], w64[:, W_COLS["k_w1"][0]:W_COLS["v_w1"][1]])):
                            sp.dma_start(ap, source).then_inc(w_in, 16)

                        def step(t, n, b, first, last):
                            e.load_indices(sp, t, n, b, first)
                            if not first:
                                wait(sp, staged, t * STAGES - (2 * STAGES - 1))
                                wait(sp, xs_ready, (t - 1) * 2)
                            sp.dma_start(EF[b][:, :, :], row_view(ea64, t)).then_inc(e.attr_in[b], 16)
                            sp.dma_start(S9[b][:, :, :], row_view(ea9, t)).then_inc(e.attr_in[b], 16)
                        chunks(sp, step)

                    @block.gpsimd
                    def _(pool):
                        nc.gpsimd.memset(W2[:, :], 0.0).then_inc(parts, 1)
                        e.constants()

                        def rows(g, t, n, b):
                            tab, _, which = e.tables[g]
                            pool.sem_inc(parked, 1)
                            for col in range(C):
                                pool.indirect_dma_start(
                                    out=e.G[g][b][:, col, :], out_offset=None, in_=tab,
                                    in_offset=bass.IndirectOffsetOnAxis(ap=e.IDX[which][b][:, col:col + 1], axis=0),
                                ).then_inc(e.rows_in[g][b], 16)

                        def node_rows(t, n, b, first):
                            wait(pool, e.idx_in[b], (n + 1) * 32)
                            if not first:
                                wait(pool, xs_ready, (t - 1) * 2)
                            rows(0, t, n, b)

                        def step(t, n, b, first, last):
                            if first:
                                node_rows(0, 0, 0, True)
                                node_rows(1, 0, 1, True)
                            elif not last:
                                node_rows(t + 1, n + b, 1 - b, False)
                            wait(pool, e.idx_in[b], (n + 1) * 32)
                            if not first:
                                wait(pool, e.args_ready, t - 1)
                            rows(1, t, n, b)
                        chunks(pool, step)

                    @block.tensor
                    def _(pe):
                        wait(pe, w_in, 16 * 8)
                        wait(pe, parts, 8)

                        def free(t, q, b, first):
                            back = holder_before(q, b)
                            if not (first and q < back):
                                wait(pe, evacuated, t * STAGES + (q - back + 1))

                        def transposes(t, b, half, first):
                            for k in range(5):
                                q = (1, 8)[half] + k
                                rows = P if k < 4 else 64
                                free(t, q, b, first)
                                if k == 4:
                                    pe.sem_inc(parked, 1)
                                for c in range(4):
                                    last = nc.tensor.transpose(
                                        RING[ring(q, b)][0:rows, c * P:(c + 1) * P],
                                        XS[b][:, 4 * half + c, :, :].rearrange("p s f -> p (s f)")
                                        [:, k * P:k * P + rows], IDENT[:, :])
                                last.then_inc(staged, 1)

                        def columns(t, b, half, first):
                            wait(pe, evacuated, t * STAGES + (8 if half == 0 else STAGES))
                            for c in range(4):
                                col = 4 * half + c
                                if not (first and half == 0):
                                    wait(pe, col_used, t * C + (col - 3))
                                bank = COLS[col % 4]
                                for k in range(5):
                                    rows = P if k < 4 else 64
                                    nc.tensor.matmul(bank[:, 0:256], XST[half][0:rows, k, c * P:(c + 1) * P],
                                                     CF[0:rows, k, :], start=(k == 0), stop=(k == 4))
                                for part in range(3):
                                    nc.tensor.matmul(bank[:, 256:512], ONEB[:, :], B2[part][:, :],
                                                     start=(part == 0), stop=False)
                                nc.tensor.matmul(bank[:, 256:512],
                                                 HT[b][col % 2][:, (col // 2) * P:(col // 2 + 1) * P],
                                                 W2[:, :], start=False, stop=True).then_inc(col_done, 1)

                        def step(t, n, b, first, last):
                            wait(pe, e.attr_in[b], (n + 1) * 32)
                            free(t, 0, b, first)
                            for c in range(4):
                                ins = nc.tensor.transpose(RING[ring(0, b)][:, c * P:(c + 1) * P],
                                                          EF[b][:, 2 * c:2 * c + 2, :]
                                                          .rearrange("p j f -> p (j f)"), IDENT[:, :])
                            ins.then_inc(staged, 1)
                            wait(pe, xs_ready, t * 2 + 1)
                            transposes(t, b, 0, first)
                            for a in range(2):
                                free(t, 6 + a, b, first)
                                nc.tensor.matmul(RING[ring(6 + a, b)][:, :], W1[64 * a:64 * a + 64, :],
                                                 EFT[64 * a:64 * a + 64, :], start=True, stop=True)\
                                  .then_inc(staged, 1)
                            if not first:
                                columns(t - 1, 1 - b, 1, False)
                            wait(pe, xs_ready, t * 2 + 2)
                            transposes(t, b, 1, first)
                            columns(t, b, 0, first)

                        chunks(pe, step)
                        columns(NCH - 1, 1, 1, False)

                    @block.scalar
                    def _(act):
                        wait(act, w_in, 16 * 8)
                        wait(act, e.ready, e.N_READY)

                        def evacuate(t, q, b, out_ap, rows=P, func=ACT.Copy, **kw):
                            wait(act, staged, t * STAGES + (q + 1))
                            nc.scalar.activation(out_ap, RING[ring(q, b)][0:rows, :], func, **kw)\
                              .then_inc(evacuated, 1)

                        def half_transposes(t, b, half, first):
                            if not first:
                                wait(act, col_done, t * C - (4 if half == 0 else 0))
                            for k in range(5):
                                rows = P if k < 4 else 64
                                evacuate(t, (1, 8)[half] + k, b, XST[half][0:rows, k, :], rows)

                        def weights(t, col, early):
                            wait(act, col_done, t * C + (col + 1))
                            if not early:
                                wait(act, col_used, t * C + (col - 1))
                            nc.scalar.activation(WKV[col % 2][:, :], COLS[col % 4][:, 256:512], ACT.Copy)\
                              .then_inc(w_copied, 1)

                        def step(t, n, b, first, last):
                            if not first:
                                wait(act, staged, t * STAGES - (STAGES - 8))
                            evacuate(t, 0, b, EFT[:, :])
                            half_transposes(t, b, 0, first)
                            for a in range(2):
                                evacuate(t, 6 + a, b, HT[b][a][:, :], func=ACT.Relu, bias=B1[:, 0:1])
                            if not first:
                                for col in range(4, 8):
                                    weights(t - 1, col, False)
                            half_transposes(t, b, 1, first)
                            if not first:
                                e.factors(act, t - 1, before(n, b), 1 - b, False)
                            for col in range(4):
                                weights(t, col, first and col < 2)
                            if not first:
                                e.store_rows(act, t - 1, before(n, b), 1 - b, False)
                        chunks(act, step)
                        for col in range(4, 8):
                            weights(NCH - 1, col, False)
                        e.factors(act, NCH - 1, NCH // 2 - 1, 1, False)
                        e.store_rows(act, NCH - 1, NCH // 2 - 1, 1, False)
                        e.drain_stores(act)

                    @block.vector
                    def _(v):
                        wait(v, e.ready, e.N_READY)
                        wait(v, w_in, 16 * 8)
                        nc.vector.memset(ONEB[:, :], 1.0).then_inc(parts, 1)
                        nc.vector.tensor_copy(B2[0][:, :], B2F[:, 0, :]).then_inc(parts, 1)
                        wait(v, parts, 3)
                        nc.vector.tensor_tensor(B2F[:, 1, :], B2F[:, 0, :], B2[0][:, :], ALU.subtract)\
                          .then_inc(parts, 1)
                        wait(v, parts, 4)
                        nc.vector.tensor_copy(B2[1][:, :], B2F[:, 1, :]).then_inc(parts, 1)
                        wait(v, parts, 5)
                        nc.vector.tensor_tensor(B2F[:, 2, :], B2F[:, 1, :], B2[1][:, :], ALU.subtract)\
                          .then_inc(parts, 1)
                        wait(v, parts, 6)
                        nc.vector.tensor_copy(B2[2][:, :], B2F[:, 2, :]).then_inc(parts, 2)

                        def outer(t, n, b, first):
                            wait(v, e.rows_in[0][b], (n + 1) * (16 * C))
                            wait(v, e.attr_in[b], (n + 1) * 32)
                            for half in range(2):
                                if not first:
                                    wait(v, staged, t * STAGES - (2 * STAGES - (6, 13)[half]))
                                j = slice(4 * half, 4 * half + 4)
                                nc.vector.tensor_tensor(
                                    XS[b][:, j, :, :],
                                    e.G[0][b][:, j, :].unsqueeze(2).to_broadcast([P, 4, SH, 64]),
                                    S9[b][:, j, :].unsqueeze(3).to_broadcast([P, 4, SH, 64]), ALU.mult)\
                                  .then_inc(xs_ready, 1)

                        def products(t, n, b, first):
                            for col in range(C):
                                wait(v, w_copied, t * C + (col + 1))
                                nc.vector.tensor_tensor(RW[b][:, col, :], COLS[col % 4][:, 0:256],
                                                        WKV[col % 2][:, :], ALU.mult).then_inc(col_used, 1)

                        def logits(t, n, b, first):
                            st = Steps(v, e.a_steps, t * 7)
                            wait(v, e.rows_in[1][b], (n + 1) * (16 * C))
                            wait(v, col_used, (t + 1) * C)
                            st.then(nc.vector.tensor_tensor(e.T1[:, :, :], RW[b][:, :, 0:128], e.G[1][b][:, :, :],
                                                            ALU.mult))
                            if not first:
                                wait(v, e.args_ready, t)
                            e.breaks(st, t)
                            st.do(nc.vector.tensor_reduce(e.LG[:, :, 1:1 + C].rearrange("p h j -> p j h"),
                                                          e.T1[:, :, :].rearrange("p j (h c) -> p j h c", c=CH),
                                                          AX.X, ALU.add))
                            e.maxima(v, st, t, n, b, first)
                            assert st.n == 7, st.n

                        def step(t, n, b, first, last):
                            if first:
                                outer(0, 0, 0, True)
                                outer(1, 0, 1, True)
                            elif not last:
                                outer(t + 1, n + b, 1 - b, False)
                            if not first:
                                e.sums(v, t - 1, before(n, b), 1 - b, False, RW[1 - b][:, :, 128:256])
                            products(t, n, b, first)
                            logits(t, n, b, first)
                        chunks(v, step)
                        e.sums(v, NCH - 1, NCH // 2 - 1, 1, False, RW[1][:, :, 128:256])

        def finish_layer(layer):
            H, R, WD = HEADS[layer], SUMS[layer], ROW[layer]
            FE = H * CH
            has_weights = R > FE
            groups = H // 4
            GR = 64 + 4 * has_weights
            with ExitStack() as ctx:
                def s(name):
                    return phase_semaphore(name)

                def bank(name):
                    return ctx.enter_context(nc.psum_tensor(unique(name), [P, 512], F32))

                GN = sb("GN", [P, K, WD], F32, ctx)
                GC = sb("GC", [P, K, WD], F32, ctx)
                MX = sb("MX", [P, K, H], F32, ctx)
                Y = sb("Y", [P, K, 64], F32, ctx)
                SQ = sb("SQ", [P, K, 64], F32, ctx)
                AT = sb("AT", [P, K * P], F32, ctx)
                LROW = sb("LROW", [P, 3, GR], F32, ctx)
                CT = sb("CT", [P, 3, P], F32, ctx)
                CW = sb("CW", [P, 5, P], F32, ctx)
                CROW = sb("CROW", [P, WD], F32, ctx)
                NULL = sb("NULL", [1, WD], F32, ctx)
                SM = sb("SM", [P, 8, 64], F32, ctx)
                SN = sb("SN", [P, 6, K], F32, ctx)
                TP = [bank("TP0"), bank("TP1")]
                CP, CB, PB = bank("CP"), bank("CB"), bank("PB")
                PO = [bank("PO0"), bank("PO1")]
                dve, null_set, carried = s("dve"), s("null_set"), s("carried")
                rows_in, carry_in, stored = s("rows_in"), s("carry_in"), s("stored")
                c_rows, c_tp, c_arg, c_exp, c_sum, c_back, c_row = (s("c_rows"), s("c_tp"), s("c_arg"), s("c_exp"),
                                                                    s("c_sum"), s("c_back"), s("c_row"))
                merge_arg, merge_exp, agg_ready, agg_t, agg_c, agg_mm, agg_add = (
                    s("merge_arg"), s("merge_exp"), s("agg_ready"), s("agg_t"), s("agg_c"), s("agg_mm"), s("agg_add"))
                bn_part, bn_sum, bn_var, bn_sd = s("bn_part"), s("bn_sum"), s("bn_var"), s("bn_sd")
                ln_var, ln_sd, gelu_in, gelu_out, done = s("ln_var"), s("ln_sd"), s("gelu_in"), s("gelu_out"), s("done")
                tab = carry_tabs[layer]
                project_agg = layer in (1, 2)
                units = GROUPS
                N = slice(0, NP)

                with nc.Block() as block:
                    @block.gpsimd
                    def _(pool):
                        nc.gpsimd.memset(NULL[:, :], 0.0).then_inc(null_set, 1)
                        pool.wait_ge(null_set, 1)
                        nc.gpsimd.memset(NULL[:, R:WD], NEG).then_inc(null_set, 1)
                        for k in range(K):
                            pool.indirect_dma_start(
                                out=GN[N, k, :], out_offset=None, in_=scan_tabs[layer],
                                in_offset=bass.IndirectOffsetOnAxis(ap=END_AT[N, k:k + 1], axis=0),
                            ).then_inc(rows_in, 16)
                        pool.wait_ge(carried, 32)
                        for k in range(K):
                            pool.indirect_dma_start(
                                out=GC[N, k, :], out_offset=None, in_=tab,
                                in_offset=bass.IndirectOffsetOnAxis(ap=CARRY_AT[N, k:k + 1], axis=0),
                            ).then_inc(carry_in, 16)

                    @block.sync
                    def _(sp):
                        sp.wait_ge(null_set, 2)
                        sp.dma_start(tab[P:P + 1, :], NULL[:, :]).then_inc(carried, 16)
                        sp.wait_ge(c_row, groups)
                        sp.dma_start(tab[0:P, :], CROW[:, :]).then_inc(carried, 16)
                        sp.wait_ge(carried, 32)
                        if layer == 3:
                            sp.wait_ge(done, 1)
                            sp.dma_start(out.rearrange("(p k) f -> p k f", k=K), X[N, :, :]).then_inc(stored, 16)
                            sp.wait_ge(stored, 16)

                    @block.tensor
                    def _(pe):
                        for g in range(groups):
                            pe.wait_ge(c_rows, g + 1)
                            for n in range(3):
                                last = nc.tensor.transpose(CP[0:GR, n * P:(n + 1) * P], LROW[:, n, :], IDENT[:, :])
                            last.then_inc(c_tp, 1)
                            pe.wait_ge(c_sum, g + 1)
                            nc.tensor.transpose(CB[:, 0:GR], CW[0:GR, 3, :], IDENT[0:GR, 0:GR]).then_inc(c_back, 1)
                            nc.tensor.transpose(CB[:, P:P + GR], CW[0:GR, 0, :], IDENT[0:GR, 0:GR])\
                              .then_inc(c_back, 1)
                        if project_agg:
                            weights = WO_T[:, :] if layer == 1 else wcol("Wo")
                            pe.wait_ge(agg_ready, 1)
                            for u, (k0, m) in enumerate(units):
                                if u >= 2:
                                    pe.wait_ge(agg_c, u - 1)
                                for c in range(m):
                                    last = nc.tensor.transpose(TP[u % 2][0:FE, c * P:c * P + NP],
                                                               GN[N, k0 + c, 0:FE], IDENT[N, N])
                                last.then_inc(agg_t, 1)
                            for u, (k0, m) in enumerate(units):
                                pe.wait_ge(agg_c, u + 1)
                                if u >= 2:
                                    pe.wait_ge(agg_add, u - 1)
                                for c in range(m):
                                    last = nc.tensor.matmul(PO[u % 2][N, c * 64:c * 64 + 64],
                                                            AT[0:FE, (k0 + c) * P:(k0 + c) * P + NP], weights,
                                                            start=True, stop=True)
                                last.then_inc(agg_mm, 1)
                        if layer != 2:
                            for n in range(2):
                                pe.wait_ge(bn_part, n + 1)
                                nc.tensor.matmul(PB[:, n * 64:n * 64 + 64], ONES[N, :], SM[N, n, :], start=True,
                                                 stop=True).then_inc(bn_sum, 1)

                    @block.scalar
                    def _(act):
                        for g in range(groups):
                            act.wait_ge(c_arg, g + 1)
                            nc.scalar.activation(CW[0:GR, 1:3, :], CW[0:GR, 1:3, :], ACT.Exp).then_inc(c_exp, 1)
                        act.wait_ge(merge_arg, 1)
                        nc.scalar.activation(GN[N, :, R:WD], GN[N, :, R:WD], ACT.Exp).then_inc(merge_exp, 1)
                        nc.scalar.activation(GC[N, :, R:WD], GC[N, :, R:WD], ACT.Exp).then_inc(merge_exp, 1)
                        if project_agg:
                            for u, (k0, m) in enumerate(units):
                                act.wait_ge(agg_t, u + 1)
                                nc.scalar.activation(
                                    AT[0:FE, k0 * P:(k0 + m) * P].rearrange("p (k n) -> p k n", n=P)[:, :, N],
                                    TP[u % 2][0:FE, 0:m * P].rearrange("p (k n) -> p k n", n=P)[:, :, N], ACT.Copy)\
                                  .then_inc(agg_c, 1)
                        if layer != 2:
                            act.wait_ge(bn_var, 1)
                            nc.scalar.activation(SM[:, 3, :], SM[:, 3, :], ACT.Sqrt).then_inc(bn_sd, 1)
                        if layer == 0:
                            act.wait_ge(gelu_in, 1)
                            nc.scalar.activation(Y[N, :, :], Y[N, :, :], ACT.Gelu).then_inc(gelu_out, 1)
                        for n in range(2 if layer == 2 else 1):
                            act.wait_ge(ln_var, n + 1)
                            nc.scalar.activation(SN[N, 2, :], SN[N, 2, :], ACT.Sqrt).then_inc(ln_sd, 1)

                    @block.vector
                    def _(v):
                        st = Steps(v, dve)
                        nv = nc.vector
                        tt = nv.tensor_tensor
                        for g in range(groups):
                            last = SC[1][:, :, C:C + 1].rearrange("p r j -> p (r j)")
                            st.do(nv.tensor_copy(LROW[:, 0, 0:64], last[:, 64 * g:64 * g + 64]))
                            if has_weights:
                                st.do(nv.tensor_copy(LROW[:, 0, 64:68], last[:, FE + 4 * g:FE + 4 * g + 4]))
                            if layer < 2:
                                m = MS[1][:, 4 * g:4 * g + 4, C:C + 1]
                                st.do(nv.tensor_copy(LROW[:, 1, 0:64].rearrange("p (h c) -> p h c", c=CH),
                                                     m.to_broadcast([P, 4, CH])))
                                st.do(nv.tensor_copy(LROW[:, 1, 64:68], m.rearrange("p h j -> p (h j)")))
                            else:
                                st.do(nv.memset(LROW[:, 1, :], 0.0))
                            st.do(nv.tensor_copy(LROW[:, 2, :], PASS[:, 0:1].to_broadcast([P, GR])))
                            st.wait()
                            nv.tensor_scalar(SM[:, 7, 0:1], PASS[:, 0:1], 1.0, None, ALU.mult).then_inc(c_rows, 1)
                            v.wait_ge(c_tp, g + 1)
                            st.then(nv.tensor_copy(CT[0:GR, :, :], CP[0:GR, 0:3 * P]
                                                   .rearrange("p (n q) -> p n q", n=3)))
                            st.then(nv.tensor_tensor_scan(CW[0:GR, 0, :], CT[0:GR, 2, :], CT[0:GR, 1, :], NEG,
                                                          ALU.add, ALU.max))
                            st.do(nv.memset(CW[0:GR, 1, 0:1], NEG))
                            st.do(tt(CW[0:GR, 1, 1:P], CW[0:GR, 0, 0:P - 1], CW[0:GR, 0, 1:P], ALU.subtract))
                            st.do(tt(CW[0:GR, 2, :], CT[0:GR, 1, :], CW[0:GR, 0, :], ALU.subtract))
                            st.wait()
                            tt(CW[0:GR, 1, :], CW[0:GR, 1, :], CT[0:GR, 2, :], ALU.add).then_inc(c_arg, 1)
                            v.wait_ge(c_exp, g + 1)
                            st.then(tt(CW[0:GR, 4, :], CT[0:GR, 0, :], CW[0:GR, 2, :], ALU.mult))
                            nv.tensor_tensor_scan(CW[0:GR, 3, :], CW[0:GR, 1, :], CW[0:GR, 4, :], 0.0, ALU.mult,
                                                  ALU.add).then_inc(c_sum, 1)
                            v.wait_ge(c_back, 2 * g + 2)
                            st.do(nv.tensor_copy(CROW[:, 64 * g:64 * g + 64], CB[:, 0:64]))
                            if has_weights:
                                st.do(nv.tensor_copy(CROW[:, FE + 4 * g:FE + 4 * g + 4], CB[:, 64:68]))
                            st.wait()
                            nv.tensor_copy(CROW[:, R + 4 * g:R + 4 * g + 4], CB[:, P:P + 64:CH])\
                                .then_inc(c_row, 1)
                        v.wait_ge(rows_in, 16 * K)
                        v.wait_ge(carry_in, 16 * K)
                        st.then(tt(MX[N, :, :], GN[N, :, R:WD], GC[N, :, R:WD], ALU.max))
                        st.then(tt(GN[N, :, R:WD], GN[N, :, R:WD], MX[N, :, :], ALU.subtract))
                        tt(GC[N, :, R:WD], GC[N, :, R:WD], MX[N, :, :], ALU.subtract).then_inc(merge_arg, 1)
                        v.wait_ge(merge_exp, 2)
                        for G in (GN, GC):
                            fac = G[N, :, R:WD]
                            st.do(tt(G[N, :, 0:FE].rearrange("p k (h c) -> p k h c", c=CH),
                                     G[N, :, 0:FE].rearrange("p k (h c) -> p k h c", c=CH),
                                     fac.unsqueeze(3).to_broadcast([NP, K, H, CH]), ALU.mult))
                            if has_weights:
                                st.do(tt(G[N, :, FE:R], G[N, :, FE:R], fac, ALU.mult))
                        st.wait()
                        st.then(tt(GN[N, :, 0:R], GN[N, :, 0:R], GC[N, :, 0:R], ALU.add))
                        st.then(tt(GN[N, :, 0:R], GN[N, :, 0:R],
                                   HAS[N, :].unsqueeze(2).to_broadcast([NP, K, R]), ALU.mult))
                        if has_weights:
                            st.then(nv.tensor_scalar(GN[N, :, FE:R], GN[N, :, FE:R], 1.0 if layer == 2 else 1e-16,
                                                     None, ALU.add))
                            st.then(nv.reciprocal(MX[N, :, :], GN[N, :, FE:R]))
                            agg = GN[N, :, 0:FE].rearrange("p k (h c) -> p k h c", c=CH)
                            st.then(tt(agg, agg, MX[N, :, :].unsqueeze(3).to_broadcast([NP, K, H, CH]), ALU.mult))
                        if project_agg:
                            nv.tensor_scalar(SM[N, 7, 0:1], PASS[N, 0:1], 1.0, None, ALU.mult)\
                                .then_inc(agg_ready, 1)
                            for u, (k0, m) in enumerate(units):
                                v.wait_ge(agg_mm, u + 1)
                                tt(Y[N, k0:k0 + m, :], PO[u % 2][N, 0:m * 64].rearrange("p (k n) -> p k n", k=m),
                                   KEEP[N, k0:k0 + m, :], ALU.add).then_inc(agg_add, 1)
                            v.wait_ge(agg_add, len(units))
                            if layer == 2:
                                st.then(tt(Y[N, :, :], Y[N, :, :], over_nodes(vec("bo")), ALU.add))
                        elif layer == 0:
                            st.then(tt(Y[N, :, :], GN[N, :, 0:64], over_nodes(vec("bias0")), ALU.add))
                        else:
                            st.then(tt(Y[N, :, :], GN[N, :, 0:64], over_nodes(vec("bias3")), ALU.add))
                            st.then(nv.scalar_tensor_tensor(out=Y[N, :, :], in0=Y[N, :, :], scalar=0.0,
                                                            in1=KEEP[N, :, :], op0=ALU.max, op1=ALU.add))

                        def layer_norm(x_ap, turn):
                            st.then(nv.tensor_reduce(SN[N, 0, :], x_ap, AX.X, ALU.add))
                            st.then(nv.tensor_scalar(SN[N, 1, :], SN[N, 0, :], 1.0 / 64, None, ALU.mult))
                            st.then(tt(SQ[N, :, :], x_ap, SN[N, 1, :].unsqueeze(2).to_broadcast([NP, K, 64]),
                                       ALU.subtract))
                            st.then(tt(GC[N, :, 0:64], SQ[N, :, :], SQ[N, :, :], ALU.mult))
                            st.then(nv.tensor_reduce(SN[N, 3, :], GC[N, :, 0:64], AX.X, ALU.add))
                            nv.tensor_scalar(SN[N, 2, :], SN[N, 3, :], 1.0 / 64, 1e-5, ALU.mult, ALU.add)\
                                .then_inc(ln_var, 1)
                            v.wait_ge(ln_sd, turn)
                            st.then(nv.reciprocal(SN[N, 4, :], SN[N, 2, :]))
                            return SN[N, 4, :].unsqueeze(2).to_broadcast([NP, K, 64])

                        if layer == 2:
                            rs = layer_norm(Y[N, :, :], 1)
                            st.then(tt(SQ[N, :, :], SQ[N, :, :], rs, ALU.mult))
                            st.then(tt(SQ[N, :, :], SQ[N, :, :], over_nodes(vec("gamma2")), ALU.mult))
                            st.then(tt(SQ[N, :, :], SQ[N, :, :], over_nodes(vec("beta2")), ALU.add))
                            st.then(tt(Y[N, :, :], Y[N, :, :], SQ[N, :, :], ALU.add))
                        else:
                            nv.tensor_reduce(SM[N, 0, :], Y[N, :, :].rearrange("p k f -> p f k"), AX.X, ALU.add)\
                                .then_inc(bn_part, 1)
                            v.wait_ge(bn_sum, 1)
                            st.then(nv.tensor_scalar(SM[:, 2, :], PB[:, 0:64], 1.0 / NODES, None, ALU.mult))
                            st.then(tt(Y[N, :, :], Y[N, :, :], over_nodes(SM[:, 2, :]), ALU.subtract))
                            st.then(tt(SQ[N, :, :], Y[N, :, :], Y[N, :, :], ALU.mult))
                            nv.tensor_reduce(SM[N, 1, :], SQ[N, :, :].rearrange("p k f -> p f k"), AX.X, ALU.add)\
                                .then_inc(bn_part, 1)
                            v.wait_ge(bn_sum, 2)
                            nv.tensor_scalar(SM[:, 3, :], PB[:, 64:128], 1.0 / NODES, 1e-5, ALU.mult, ALU.add)\
                                .then_inc(bn_var, 1)
                            v.wait_ge(bn_sd, 1)
                            st.then(nv.reciprocal(SM[:, 4, :], SM[:, 3, :]))
                            st.then(tt(SM[:, 5, :], SM[:, 4, :], vec(f"gamma{layer}"), ALU.mult))
                            st.then(tt(Y[N, :, :], Y[N, :, :], over_nodes(SM[:, 5, :]), ALU.mult))
                            st.then(tt(Y[N, :, :], Y[N, :, :], over_nodes(vec(f"beta{layer}")), ALU.add))
                        if layer == 0:
                            tt(Y[N, :, :], Y[N, :, :], X[N, :, :], ALU.add).then_inc(gelu_in, 1)
                            v.wait_ge(gelu_out, 1)
                        st.then(tt(Y[N, :, :], Y[N, :, :], X[N, :, :], ALU.add))
                        rs = layer_norm(Y[N, :, :], 2 if layer == 2 else 1)
                        tt(X[N, :, :], SQ[N, :, :], rs, ALU.mult).then_inc(done, 1)

        end_phase()
        project(wcol("W_l", "W_r"), 128, vec("b_l", 2), [(xl_tab, 0, 64), (xr_tab, 64, 64)], None)
        end_phase()
        edges_0(src, dst_of_edges)
        end_phase()
        finish_layer(0)
        end_phase()
        project(wcol("Wq1", "W_self"), 192, vec("zero_q0", 3), [(q1_tab, 0, 128), (x1_tab, None, 64)], 128)
        end_phase()
        edges_1(src, dst_of_edges)
        end_phase()
        finish_layer(1)
        end_phase()
        project(wcol("Wk", "Wf"), 256, vec("bk", 4), [(kv_tab, 0, 128), (q2_tab, 128, 64)], 192)
        end_phase()
        edges_2(src, dst_of_edges)
        end_phase()
        finish_layer(2)
        end_phase()
        project_relations()
        end_phase()
        edges_3()
        end_phase()
        finish_layer(3)
        end_phase()


_VECS = ["L0_gnn_b_l", "L0_gnn_b_r", None, None, None, "L2_gnn_bk", "L2_gnn_bv", "L2_gnn_bq", "L2_gnn_bf",
         "L0_gnn_att", "L0_gnn_bias", "L0_gnn_gamma", "L0_gnn_beta", "L1_gnn_gamma", "L1_gnn_beta", "L2_gnn_bo",
         "L2_gnn_gamma", "L2_gnn_beta", "L3_gnn_bias", "L3_gnn_res_b", "L3_gnn_gamma", "L3_gnn_beta"]


def kernel(**inputs):
    import numpy as np
    import concourse.bacc as bacc
    from concourse.bass_utils import run_bass_kernel_spmd

    a = {k: np.asarray(v) for k, v in inputs.items()}
    f32 = np.float32

    def padded(v, rows):
        return np.concatenate([v, np.zeros((rows - v.shape[0],) + v.shape[1:], v.dtype)])

    dst = a["dst"].astype(np.int32)
    w64 = np.concatenate([a["L0_gnn_W_l"], a["L0_gnn_W_r"], a["L1_gnn_Wq"], a["L1_gnn_W_self"], a["L1_gnn_k_w1"],
                          a["L1_gnn_v_w1"], a["L2_gnn_Wk"], a["L2_gnn_Wv"], a["L2_gnn_Wq"], a["L2_gnn_Wf"],
                          a["L2_gnn_Wo"], a["L3_gnn_res_w"], a["L3_gnn_comp"]], axis=1)
    arrays = {
        "x": padded(a["x"], NPAD),
        "dst_shifted": np.concatenate([np.full(1, -1, np.int32), dst, np.full(EPAD - EDGES, NODES, np.int32)]),
        "src": padded(a["src"].astype(np.int32), EPAD).reshape(P, J),
        "ea16": padded(a["edge_attr_16"], EPAD),
        "ea64": padded(a["edge_attr_64"], EPAD),
        "ea9": padded(a["edge_attr_9"], EPAD),
        "etype": padded(a["edge_type_64"].astype(np.int32), EPAD).reshape(P, J),
        "ew": padded(a["edge_weight1"], EPAD).reshape(P, J),
        "w64": w64,
        "we": a["L0_gnn_W_e"],
        "cfix": np.concatenate([a["L1_gnn_Cqk"].transpose(1, 0, 2), a["L1_gnn_Cv"].transpose(1, 0, 2)], axis=2)
                .reshape(SH * 64, 256),
        "w2": np.concatenate([a["L1_gnn_k_w2"], a["L1_gnn_v_w2"]], axis=1),
        "b1": np.concatenate([a["L1_gnn_k_b1"], a["L1_gnn_v_b1"]]).reshape(P, 1),
        "b2": np.concatenate([a["L1_gnn_k_b2"], a["L1_gnn_v_b2"]]).reshape(1, 256),
        "wout": a["L1_gnn_W_out"],
        "vecs": np.concatenate([np.zeros(64, f32) if n is None else a[n].reshape(64) for n in _VECS])
                .reshape(1, V_ALL),
        "basis": a["L3_gnn_basis"],
    }
    nc = bacc.Bacc("TRN2", target_bir_lowering=False, num_devices=1)
    args = {}
    for name in arrays:
        arrays[name] = np.ascontiguousarray(arrays[name])
        args[name] = nc.dram_tensor(name, arrays[name].shape, mybir.dt.from_np(arrays[name].dtype),
                                    kind="ExternalInput").ap()
    out = nc.dram_tensor("out", (NODES, D), F32, kind="ExternalOutput").ap()
    graph_kernel(nc, out=out, **args)
    r = run_bass_kernel_spmd(nc, [arrays], core_ids=[0])
    return r.results[0]["out"]
```

```python
import concourse.bass as bass
from concourse import mybir
from contextlib import ExitStack

F32 = mybir.dt.float32
I32 = mybir.dt.int32
BF16 = mybir.dt.bfloat16
F32R = mybir.dt.float32r
ALU = mybir.AluOpType
ACT = mybir.ActivationFunctionType
AX = mybir.AxisListType

NODES, EDGES, D = 3125, 100000, 64
P = 128
K = 25
NP = NODES // K
NPAD = P * K
C = 8
J = 784
NCH = J // C
EPAD = P * J
RELS = 64
SH = 9
CH = 16
HEADS = [4, 8, 4, 4]
SUMS = [68, 136, 68, 64]
ROW = [s + h for s, h in zip(SUMS, HEADS)]
NEG = -1.0e30
MAGIC = 12582912.0
GROUPS = [(k, min(4, K - k)) for k in range(0, K, 4)]
assert NP * K == NODES and NCH % 2 == 0 and EPAD >= EDGES

W_COLS = {}
_at = 0
for _n, _w in (("W_l", 64), ("W_r", 64), ("Wq1", 128), ("W_self", 64), ("k_w1", 64), ("v_w1", 64), ("Wk", 64),
               ("Wv", 64), ("Wq2", 64), ("Wf", 64), ("Wo", 64), ("res_w", 64), ("comp", 64)):
    W_COLS[_n] = (_at, _at + _w)
    _at += _w
W_ALL = _at
V_NAMES = ["b_l", "b_r", "zero_q0", "zero_q1", "zero_s", "bk", "bv", "bq", "bf", "att", "bias0", "gamma0", "beta0",
           "gamma1", "beta1", "bo", "gamma2", "beta2", "bias3", "res_b", "gamma3", "beta3"]
V_AT = {n: i * 64 for i, n in enumerate(V_NAMES)}
V_ALL = 64 * len(V_NAMES)


def graph_kernel(nc, x, dst_shifted, src, ea16, ea64, ea9, etype, ew, w64, we, cfix, w2, b1, b2, wout, vecs, basis,
                 out):
    scratch = {}

    def dram(name, shape, dt=F32):
        scratch[name] = nc.dram_tensor(name, shape, dt, kind="Internal").ap()
        return scratch[name]

    xl_tab, xr_tab = dram("xl_tab", [NPAD, 64]), dram("xr_tab", [NPAD, 64])
    x1_tab, q1_tab = dram("x1_tab", [NPAD, 64]), dram("q1_tab", [NPAD, 128])
    kv_tab, q2_tab = dram("kv_tab", [NPAD, 128]), dram("q2_tab", [NPAD, 64])
    rel_tab = dram("rel_tab", [NPAD * RELS, 64])
    scan_tabs = [dram(f"scan{l}", [EPAD, ROW[l]]) for l in range(4)]
    carry_tabs = [dram(f"carry{l}", [P + 1, ROW[l]]) for l in range(4)]
    relidx = dram("relidx", [P, J], I32)
    spread = dram("spread", [EPAD, 64])
    dst_of_edges = dst_shifted[1:1 + EPAD].rearrange("(p j) -> p j", j=J)

    uses = {}

    def unique(name):
        uses[name] = uses.get(name, 0) + 1
        return name if uses[name] == 1 else f"{name}_{uses[name]}"

    top = ExitStack()
    with top:
        def sb(name, shape, dt=F32, ctx=top):
            return ctx.enter_context(nc.sbuf_tensor(unique(name), shape, dt))

        X = sb("X", [P, K, D])
        KEEP = sb("KEEP", [P, K, 64])
        W = sb("W", [64, W_ALL])
        VEC = sb("VEC", [P, V_ALL])
        WO_T = sb("WO_T", [P, 64])
        RESW_T = sb("RESW_T", [64, 64])
        COMP_T = sb("COMP_T", [64, 64])
        IDENT = sb("IDENT", [P, P])
        ONES = sb("ONES", [P, P])
        SAME = sb("SAME", [P, J])
        BREAK = sb("BREAK", [P, J])
        HAS = sb("HAS", [P, K])
        END_AT = sb("END_AT", [P, K], I32)
        START_AT = sb("START_AT", [P, K], I32)
        FIRST_DST = sb("FIRST_DST", [P, 1], I32)
        CARRY_AT = sb("CARRY_AT", [P, K], I32)
        PASS = sb("PASS", [P, 1])
        SC = [sb(f"SC{b}", [P, 136, 1 + C]) for b in range(2)]
        MS = [sb(f"MS{b}", [P, 8, 1 + C]) for b in range(2)]

        parked = top.enter_context(nc.semaphore("parked"))

        open_semaphores = []

        def end_phase():
            nc.clear_and_free_semaphores(list(open_semaphores))
            open_semaphores.clear()
            nc.all_engine_barrier()

        def phase_semaphore(name):
            sem = nc.alloc_semaphore(unique(name))
            open_semaphores.append(sem)
            return sem

        def vec(name, n=1):
            return VEC[:, V_AT[name]:V_AT[name] + 64 * n]

        def wcol(a, b=None):
            return W[:, W_COLS[a][0]:W_COLS[b or a][1]]

        def over_nodes(v, n=NP):
            return v[0:n, :].unsqueeze(1).to_broadcast([n, K, v.shape[1]])

        class Steps:

            def __init__(self, eng, sem, base=0):
                self.eng, self.sem, self.base, self.n = eng, sem, base, 0

            def do(self, ins):
                ins.then_inc(self.sem, 1)
                self.n += 1
                return ins

            def wait(self, back=0):
                self.eng.wait_ge(self.sem, self.base + (self.n - back))

            def then(self, ins):
                self.do(ins)
                self.wait()

        def chunks(eng, step, peeled=2):
            for t in range(peeled):
                step(t, t // 2, t % 2, t == 0, False)
            with eng.Fori(peeled // 2, NCH // 2 - 1) as n:
                step(n * 2, n, 0, False, False)
                step(n * 2 + 1, n, 1, False, False)
            step(NCH - 2, NCH // 2 - 1, 0, False, False)
            step(NCH - 1, NCH // 2 - 1, 1, False, True)

        def wait(eng, sem, value):
            if not isinstance(value, int) or value > 0:
                eng.wait_ge(sem, value)
                if eng is nc.sync and not isinstance(value, int):
                    eng.sem_inc(parked, 1)

        HB = 16
        with ExitStack() as ctx:
            def s(name):
                return phase_semaphore(name)

            DSTX = sb("DSTX", [P, 2, J], I32, ctx)
            TYPES = sb("TYPES", [P, 2, J], I32, ctx)
            RIDX = sb("RIDX", [P, J], I32, ctx)
            HI = sb("HI", [P, J], F32, ctx)
            LO = sb("LO", [P, J], F32, ctx)
            IOTA = sb("IOTA", [P, P], I32, ctx)
            IOTAF = sb("IOTAF", [P, P], F32, ctx)
            OH = [sb(f"OH{b}", [P, HB, P], BF16, ctx) for b in range(2)]
            OL = [sb(f"OL{b}", [P, HB, K], BF16, ctx) for b in range(2)]
            ZB = sb("ZB", [P, P], BF16, ctx)
            ZERO = sb("ZERO", [P, J // 7 * 8], F32, ctx)
            TRI = sb("TRI", [P, P], F32, ctx)
            ST = sb("ST", [P, 11, K], F32, ctx)
            COUNTS = ctx.enter_context(nc.psum_tensor(unique("COUNTS"), [P, 512], F32))
            PS = ctx.enter_context(nc.psum_tensor(unique("PS"), [P, 512], F32))
            PR = [ctx.enter_context(nc.psum_tensor(unique(f"PR{b}"), [P, 512], F32)) for b in range(2)]
            loaded, dst_in, types_in = s("loaded"), s("dst_in"), s("types_in")
            consts, dve, hot, hot_used, counted = s("consts"), s("dve"), s("hot"), s("hot_used"), s("counted")
            totals, offs, ridx_ready, ridx_out = s("totals"), s("offs"), s("ridx_ready"), s("ridx_out")
            zeroed, zeroed_out = s("zeroed"), s("zeroed_out")
            tposed, t_copied = s("tposed"), s("t_copied")
            with nc.Block() as block:
                @block.sync
                def _(sp):
                    sp.dma_start(DSTX[:, 0, :], dst_shifted[1:1 + EPAD].rearrange("(p j) -> p j", j=J))\
                      .then_inc(dst_in, 16)
                    sp.dma_start(DSTX[:, 1, :], dst_shifted[0:EPAD].rearrange("(p j) -> p j", j=J))\
                      .then_inc(dst_in, 16)
                    sp.dma_start(W[:, :], w64).then_inc(loaded, 16)
                    sp.dma_start(TYPES[:, 0, :], src).then_inc(types_in, 16)
                    sp.dma_start(TYPES[:, 1, :], etype).then_inc(types_in, 16)
                    sp.dma_start(X[:, :, :], x.rearrange("(p k) f -> p k f", k=K)).then_inc(loaded, 16)
                    sp.dma_start(VEC[:, :], vecs.to_broadcast([P, V_ALL])).then_inc(loaded, 16)
                    sp.dma_start(WO_T[:, :], wout).then_inc(loaded, 16)
                    sp.wait_ge(zeroed, 1)
                    spread_v = spread.rearrange("(p a m) f -> p a (m f)", a=56, m=14)
                    sp.dma_start(spread_v, ZERO[:, :].unsqueeze(1).to_broadcast([P, 56, 14 * 64]))\
                      .then_inc(zeroed_out, 16)
                    sp.wait_ge(zeroed_out, 16)
                    sp.wait_ge(ridx_ready, 1)
                    sp.dma_start(relidx, RIDX[:, :]).then_inc(ridx_out, 16)
                    sp.wait_ge(ridx_out, 16)
                    sp.wait_ge(loaded, 64)

                @block.gpsimd
                def _(pool):
                    nc.gpsimd.memset(ZERO[:, :], 0.0).then_inc(zeroed, 1)
                    nc.gpsimd.iota(IOTA[:, :], [[1, P]], base=0, channel_multiplier=0).then_inc(consts, 1)
                    nc.gpsimd.memset(IDENT[:, :], 0.0).then_inc(consts, 1)
                    nc.gpsimd.memset(ONES[:, :], 1.0).then_inc(consts, 1)
                    nc.gpsimd.memset(TRI[:, :], 1.0).then_inc(consts, 1)
                    nc.gpsimd.memset(ZB[:, :], 0.0).then_inc(consts, 1)
                    pool.wait_ge(consts, 5)
                    nc.gpsimd.affine_select(out=IDENT[:, :], in_=IDENT[:, :], compare_op=ALU.not_equal, fill=1.0,
                                            base=0, pattern=[[-1, P]], channel_multiplier=1).then_inc(consts, 1)
                    nc.gpsimd.affine_select(out=TRI[:, :], in_=TRI[:, :], compare_op=ALU.is_gt, fill=0.0,
                                            base=0, pattern=[[1, P]], channel_multiplier=-1).then_inc(consts, 1)

                @block.vector
                def _(v):
                    st = Steps(v, dve)
                    v.wait_ge(consts, 7)
                    st.do(nc.vector.tensor_copy(IOTAF[:, :], IOTA[:, :]))
                    v.wait_ge(dst_in, 32)
                    st.then(nc.vector.tensor_scalar(HI[:, :], DSTX[:, 0, :], 1.0 / K, -(K - 1) / 2 / K, ALU.mult,
                                                    ALU.add))
                    st.then(nc.vector.tensor_scalar(HI[:, :], HI[:, :], MAGIC, None, ALU.add))
                    st.then(nc.vector.tensor_scalar(HI[:, :], HI[:, :], -MAGIC, None, ALU.add))
                    st.then(nc.vector.scalar_tensor_tensor(out=LO[:, :], in0=HI[:, :], scalar=-float(K),
                                                           in1=DSTX[:, 0, :], op0=ALU.mult, op1=ALU.add))
                    def hots(t, b):
                        at = bass.ds(t * HB, HB)
                        nc.vector.tensor_tensor(OH[b][:, :, :], IOTAF[:, :].unsqueeze(1).to_broadcast([P, HB, P]),
                                                HI[:, at].unsqueeze(2).to_broadcast([P, HB, P]),
                                                ALU.is_equal).then_inc(hot, 1)
                        nc.vector.tensor_tensor(OL[b][:, :, :],
                                                IOTAF[:, 0:K].unsqueeze(1).to_broadcast([P, HB, K]),
                                                LO[:, at].unsqueeze(2).to_broadcast([P, HB, K]),
                                                ALU.is_equal).then_inc(hot, 1)

                    hots(0, 0)
                    hots(1, 1)
                    v.wait_ge(hot_used, 1)
                    hots(2, 0)
                    with v.Fori(1, J // HB // 2) as i:
                        v.wait_ge(hot_used, i * 2)
                        hots(i * 2 + 1, 1)
                        v.wait_ge(hot_used, i * 2 + 1)
                        hots(i * 2 + 2, 0)
                    st.do(nc.vector.tensor_tensor(SAME[:, :], DSTX[:, 0, :], DSTX[:, 1, :], ALU.is_equal))
                    st.do(nc.vector.tensor_tensor(ST[:, 0, 0:1], DSTX[:, 0, 0:1], DSTX[:, 0, J - 1:J],
                                                  ALU.is_equal))
                    st.wait()
                    st.do(nc.vector.tensor_scalar(BREAK[:, :], SAME[:, :], -1.0, -NEG, ALU.add, ALU.mult))
                    st.then(nc.vector.tensor_tensor(ST[:, 0, 0:1], ST[:, 0, 0:1], SAME[:, 0:1], ALU.mult))
                    st.do(nc.vector.tensor_scalar(PASS[:, :], ST[:, 0, 0:1], -1.0, -NEG, ALU.add, ALU.mult))
                    v.wait_ge(types_in, 32)
                    nc.vector.scalar_tensor_tensor(out=RIDX[:, :], in0=TYPES[:, 0, :], scalar=float(RELS),
                                                   in1=TYPES[:, 1, :], op0=ALU.mult, op1=ALU.add)\
                      .then_inc(ridx_ready, 1)
                    v.wait_ge(counted, 1)
                    st.then(nc.vector.tensor_copy(ST[:, 1, :], COUNTS[:, 0:K]))
                    st.then(nc.vector.tensor_tensor_scan(ST[:, 2, :], ONES[:, 0:K], ST[:, 1, :], 0.0, ALU.mult,
                                                         ALU.add))
                    nc.vector.tensor_copy(ST[:, 3, 0:1], ST[:, 2, K - 1:K]).then_inc(totals, 1)
                    v.wait_ge(offs, 1)
                    st.do(nc.vector.tensor_scalar(ST[:, 4, :], ST[:, 2, :], PS[:, 0:1], None, ALU.add))
                    st.do(nc.vector.tensor_scalar(HAS[:, :], ST[:, 1, :], 0.0, None, ALU.is_gt))
                    st.wait()
                    st.do(nc.vector.tensor_tensor(ST[:, 5, :], ST[:, 4, :], ST[:, 1, :], ALU.subtract))
                    st.then(nc.vector.tensor_scalar(ST[:, 6, :], ST[:, 4, :], -1.0, 0.0, ALU.add, ALU.max))
                    st.do(nc.vector.tensor_copy(END_AT[:, :], ST[:, 6, :]))
                    st.do(nc.vector.tensor_copy(FIRST_DST[:, :], DSTX[:, 0, 0:1]))
                    st.then(nc.vector.scalar_tensor_tensor(out=ST[:, 10, :], in0=ST[:, 5, :],
                                                           scalar=-float(EPAD), in1=HAS[:, :], op0=ALU.add,
                                                           op1=ALU.mult))
                    st.do(nc.vector.tensor_scalar(START_AT[:, :], ST[:, 10, :], float(EPAD), None, ALU.add))
                    st.then(nc.vector.tensor_scalar(ST[:, 7, :], ST[:, 6, :], 1.0 / J, -(J - 1) / 2 / J, ALU.mult,
                                                    ALU.add))
                    st.then(nc.vector.tensor_scalar(ST[:, 7, :], ST[:, 7, :], MAGIC, None, ALU.add))
                    st.then(nc.vector.tensor_scalar(ST[:, 7, :], ST[:, 7, :], -MAGIC, None, ALU.add))
                    st.then(nc.vector.scalar_tensor_tensor(out=ST[:, 8, :], in0=ST[:, 7, :], scalar=float(J),
                                                           in1=ST[:, 5, :], op0=ALU.mult, op1=ALU.is_gt))
                    st.then(nc.vector.tensor_tensor(ST[:, 8, :], ST[:, 8, :], HAS[:, :], ALU.mult))
                    st.then(nc.vector.scalar_tensor_tensor(out=ST[:, 9, :], in0=ST[:, 7, :], scalar=-1.0 - P,
                                                           in1=ST[:, 8, :], op0=ALU.add, op1=ALU.mult))
                    st.then(nc.vector.tensor_scalar(CARRY_AT[:, :], ST[:, 9, :], float(P), None, ALU.add))
                    for n in range(2):
                        v.wait_ge(tposed, n + 1)
                        nc.vector.tensor_copy((RESW_T, COMP_T)[n][:, :], PR[n][0:64, 0:64]).then_inc(t_copied, 1)

                @block.tensor
                def _(pe):
                    pe.wait_ge(consts, 7)
                    nc.tensor.matmul(COUNTS[:, 0:K], ZB[:, :], ZB[:, 0:K], start=True, stop=False)

                    def count(t, b):
                        pe.wait_ge(hot, t * 2 + 2)
                        for c in range(HB):
                            last = nc.tensor.matmul(COUNTS[:, 0:K], OH[b][:, c, :], OL[b][:, c, :], start=False,
                                                    stop=False)
                        last.then_inc(hot_used, 1)

                    count(0, 0)
                    with pe.Fori(0, J // HB // 2) as i:
                        count(i * 2 + 1, 1)
                        count(i * 2 + 2, 0)
                    nc.tensor.matmul(COUNTS[:, 0:K], ZB[:, :], ZB[:, 0:K], start=False, stop=True)\
                      .then_inc(counted, 1)
                    pe.wait_ge(totals, 1)
                    nc.tensor.matmul(PS[:, 0:1], TRI[:, :], ST[:, 3, 0:1], start=True, stop=True)\
                      .then_inc(offs, 1)
                    pe.wait_ge(loaded, 64)
                    nc.tensor.transpose(PR[0][0:64, 0:64], wcol("res_w"), IDENT[0:64, 0:64]).then_inc(tposed, 1)
                    nc.tensor.transpose(PR[1][0:64, 0:64], wcol("comp"), IDENT[0:64, 0:64]).then_inc(tposed, 1)

        def project(weights, n_out, biases, tables, keep, spread_at=None):
            per = 512 // n_out
            units = [(k, min(per, K - k)) for k in range(0, K, per)]
            with ExitStack() as ctx:
                def s(name):
                    return phase_semaphore(name)

                XT = sb("XT", [64, NPAD], F32, ctx)
                TAB = sb("TAB", [P, K, n_out], F32, ctx)
                PT = [ctx.enter_context(nc.psum_tensor(unique(f"PT{b}"), [P, 512], F32)) for b in range(2)]
                PO = [ctx.enter_context(nc.psum_tensor(unique(f"PO{b}"), [P, 512], F32)) for b in range(4)]
                scattered = s("scattered")
                t_done, t_copied, m_done, m_copied, stored = (s("t_done"), s("t_copied"), s("m_done"),
                                                              s("m_copied"), s("stored"))
                with nc.Block() as block:
                    @block.tensor
                    def _(pe):
                        for g, (k0, m) in enumerate(GROUPS):
                            if g >= 2:
                                pe.wait_ge(t_copied, g - 1)
                            for c in range(m):
                                last = nc.tensor.transpose(PT[g % 2][0:64, c * P:(c + 1) * P], X[:, k0 + c, :],
                                                           IDENT[:, :])
                            last.then_inc(t_done, 1)
                        for u, (k0, m) in enumerate(units):
                            pe.wait_ge(t_copied, min((k0 + m - 1) // 4 + 1, len(GROUPS)))
                            if u >= 4:
                                pe.wait_ge(m_copied, u - 3)
                            for c in range(m):
                                last = nc.tensor.matmul(PO[u % 4][:, c * n_out:(c + 1) * n_out],
                                                        XT[:, (k0 + c) * P:(k0 + c + 1) * P], weights,
                                                        start=True, stop=True)
                            last.then_inc(m_done, 1)

                    @block.scalar
                    def _(act):
                        for g, (k0, m) in enumerate(GROUPS):
                            act.wait_ge(t_done, g + 1)
                            nc.scalar.activation(XT[:, k0 * P:(k0 + m) * P], PT[g % 2][0:64, 0:m * P], ACT.Copy)\
                              .then_inc(t_copied, 1)

                    @block.vector
                    def _(v):
                        for u, (k0, m) in enumerate(units):
                            v.wait_ge(m_done, u + 1)
                            nc.vector.tensor_tensor(
                                TAB[:, k0:k0 + m, :],
                                PO[u % 4][:, 0:m * n_out].rearrange("p (k n) -> p k n", k=m),
                                biases.unsqueeze(1).to_broadcast([P, m, n_out]), ALU.add).then_inc(m_copied, 1)
                        if keep is not None:
                            v.wait_ge(m_copied, len(units))
                            nc.vector.tensor_copy(KEEP[:, :, :], TAB[:, :, keep:keep + 64])\
                              .then_inc(m_copied, 1)

                    @block.gpsimd
                    def _(pool):
                        if spread_at is not None:
                            pool.wait_ge(m_copied, len(units))
                            for k in range(K):
                                pool.indirect_dma_start(
                                    out=spread, in_=TAB[0:NP, k, spread_at:spread_at + 64], in_offset=None,
                                    out_offset=bass.IndirectOffsetOnAxis(ap=START_AT[0:NP, k:k + 1], axis=0),
                                    bounds_check=EPAD - 1, oob_is_err=False).then_inc(scattered, 16)
                            pool.wait_ge(scattered, 16 * K)

                    @block.sync
                    def _(sp):
                        sp.wait_ge(m_copied, len(units))
                        for tab, at, width in tables:
                            source = X[:, :, :] if at is None else TAB[:, :, at:at + width]
                            sp.dma_start(tab.rearrange("(p k) f -> p k f", k=K), source).then_inc(stored, 16)
                        sp.wait_ge(stored, 16 * len(tables))

        def project_relations():
            with ExitStack() as ctx:
                def s(name):
                    return phase_semaphore(name)

                XT = sb("XT", [64, NPAD], F32, ctx)
                XT2 = sb("XT2", [P, NPAD], F32R, ctx)
                XX = sb("XX", [P, K, 2, 64], F32, ctx)
                BASIS = sb("BASIS", [64, P, 64], F32, ctx)
                doubled = s("doubled")
                WHI = sb("WHI", [P, RELS, 64], F32R, ctx)
                WLO = sb("WLO", [P, RELS, 64], F32R, ctx)
                YS = [sb(f"YS{b}", [P, RELS * 64], F32, ctx) for b in range(2)]
                PT = [ctx.enter_context(nc.psum_tensor(unique(f"PT{b}"), [P, 512], F32)) for b in range(2)]
                PO = [ctx.enter_context(nc.psum_tensor(unique(f"PO{b}"), [P, 512], F32)) for b in range(6)]
                t_done, t_copied, t_split, m_done = s("t_done"), s("t_copied"), s("t_split"), s("m_done")
                act_copied, dve_copied = s("act_copied"), s("dve_copied")
                stored = [s("stored0"), s("stored1")]
                res_done, res_copied = s("res_done"), s("res_copied")
                basis_in, rel_w, rel_hi, rel_lo = s("basis_in"), s("rel_w"), s("rel_hi"), s("rel_lo")
                rel_v = rel_tab.rearrange("(p k r) f -> k p (r f)", k=K, r=RELS)
                whi, wlo = (w[:, :, :].rearrange("i r o -> i (r o)") for w in (WHI, WLO))

                def by_relation(bank):
                    return bank[:, :].rearrange("i (o r) -> i r o", o=8)

                with nc.Block() as block:
                    @block.gpsimd
                    def _(pool):
                        for a in range(2):
                            nc.gpsimd.tensor_copy(XX[:, :, a, :], X[:, :, :]).then_inc(doubled, 1)

                    @block.tensor
                    def _(pe):
                        pe.wait_ge(doubled, 2)
                        for g, (k0, m) in enumerate(GROUPS):
                            if g >= 2:
                                pe.wait_ge(t_split, g - 1)
                                pe.wait_ge(t_copied, 2 * g - 2)
                            for c in range(m):
                                last = nc.tensor.transpose(
                                    PT[g % 2][:, c * P:(c + 1) * P],
                                    XX[:, k0 + c, :, :].rearrange("p a f -> p (a f)"), IDENT[:, :])
                            last.then_inc(t_done, 1)
                        pe.wait_ge(basis_in, 32)
                        for g in range(8):
                            if g >= 4:
                                pe.wait_ge(rel_lo, g - 3)
                            for o in range(8):
                                last = nc.tensor.matmul(
                                    PO[g % 4][:, o * 64:o * 64 + 64],
                                    BASIS[:, :, 8 * g + o], COMP_T[:, :],
                                    start=True, stop=True)
                            last.then_inc(rel_w, 1)
                        pe.wait_ge(t_split, len(GROUPS))
                        for r in range(4):
                            ks = range(8 * r, min(8 * r + 8, K))
                            if r >= 2:
                                pe.wait_ge(res_copied, r - 1)
                            for c, k in enumerate(ks):
                                last = nc.tensor.matmul(PT[r % 2][:, c * 64:c * 64 + 64], XT[:, k * P:(k + 1) * P],
                                                        RESW_T[:, :], start=True, stop=True)
                            last.then_inc(res_done, 1)
                        pe.wait_ge(rel_lo, 8)
                        for u in range(K * 8):
                            k, g = u // 8, u % 8
                            if u >= 6:
                                w = u - 6
                                pe.wait_ge(act_copied if w % 2 == 0 else dve_copied, w // 2 + 1)
                            for n, w in enumerate((whi, wlo)):
                                last = nc.tensor.matmul(PO[u % 6][:, :], XT2[:, k * P:(k + 1) * P],
                                                        w[:, g * 512:(g + 1) * 512], start=(n == 0), stop=(n == 1))
                            last.then_inc(m_done, 1)

                    @block.scalar
                    def _(act):
                        for g, (k0, m) in enumerate(GROUPS):
                            act.wait_ge(t_done, g + 1)
                            nc.scalar.activation(XT[:, k0 * P:(k0 + m) * P], PT[g % 2][0:64, 0:m * P], ACT.Copy)\
                              .then_inc(t_copied, 1)
                            nc.scalar.activation(XT2[:, k0 * P:(k0 + m) * P], PT[g % 2][:, 0:m * P], ACT.Copy)\
                              .then_inc(t_copied, 1)
                        for g in range(8):
                            act.wait_ge(rel_w, g + 1)
                            nc.scalar.activation(WHI[:, :, 8 * g:8 * g + 8], by_relation(PO[g % 4]), ACT.Copy)\
                              .then_inc(rel_hi, 1)
                        for u in range(0, K * 8, 2):
                            k, g = u // 8, u % 8
                            act.wait_ge(m_done, u + 1)
                            if k >= 2 and g == 0:
                                act.wait_ge(stored[k % 2], 16 * (k // 2))
                            nc.scalar.activation(YS[k % 2][:, g * 512:(g + 1) * 512], PO[u % 6][:, :], ACT.Copy)\
                              .then_inc(act_copied, 1)

                    @block.vector
                    def _(v):
                        for g, (k0, m) in enumerate(GROUPS):
                            v.wait_ge(t_copied, 2 * g + 2)
                            lo = XT2[64:128, k0 * P:(k0 + m) * P]
                            nc.vector.tensor_tensor(lo, PT[g % 2][64:128, 0:m * P], lo.bitcast(F32),
                                                    ALU.subtract).then_inc(t_split, 1)
                        for g in range(8):
                            v.wait_ge(rel_hi, g + 1)
                            nc.vector.tensor_tensor(WLO[:, :, 8 * g:8 * g + 8], by_relation(PO[g % 4]),
                                                    WHI[:, :, 8 * g:8 * g + 8].bitcast(F32),
                                                    ALU.subtract).then_inc(rel_lo, 1)
                        for r in range(4):
                            m = min(8 * r + 8, K) - 8 * r
                            v.wait_ge(res_done, r + 1)
                            nc.vector.tensor_tensor(
                                KEEP[:, 8 * r:8 * r + m, :], PT[r % 2][:, 0:m * 64].rearrange("p (k n) -> p k n", k=m),
                                vec("res_b").unsqueeze(1).to_broadcast([P, m, 64]), ALU.add).then_inc(res_copied, 1)
                        v.wait_ge(res_copied, 4)
                        nc.vector.tensor_scalar(KEEP[:, :, :], KEEP[:, :, :], 0.0, None, ALU.max)\
                          .then_inc(res_copied, 1)
                        for u in range(1, K * 8, 2):
                            k, g = u // 8, u % 8
                            v.wait_ge(m_done, u + 1)
                            if k >= 2 and g == 1:
                                v.wait_ge(stored[k % 2], 16 * (k // 2))
                            nc.vector.tensor_copy(YS[k % 2][:, g * 512:(g + 1) * 512], PO[u % 6][:, :])\
                              .then_inc(dve_copied, 1)

                    @block.sync
                    def _(sp):
                        for a in range(2):
                            sp.dma_start(BASIS[:, 64 * a:64 * a + 64, :], basis).then_inc(basis_in, 16)
                        for k in range(K):
                            sp.wait_ge(act_copied, 4 * k + 4)
                            sp.wait_ge(dve_copied, 4 * k + 4)
                            sp.dma_start(rel_v[k, :, :], YS[k % 2][:, :]).then_inc(stored[k % 2], 16)
                        sp.wait_ge(stored[0], 16 * ((K + 1) // 2))
                        sp.wait_ge(stored[1], 16 * (K // 2))

        def row_view(tab, t):
            return tab.rearrange("(p j) f -> p j f", j=J)[:, bass.ds(t * C, C), :]

        def before(n, b):
            return n - (1 - b)

        class Edges:

            def __init__(self, ctx, layer, tables, indices):
                self.layer, self.tables, self.indices = layer, tables, indices
                self.H, self.R = HEADS[layer], SUMS[layer]
                self.FE = self.H * CH
                self.weights = self.R > self.FE
                self.running_max = layer < 2
                self.ctx = ctx
                self.N_READY = 9 if layer == 0 else 7
                H, R = self.H, self.R
                self.IDX = {n: self.pair(f"IDX_{n}", [P, C], I32) for n in indices}
                self.G = [self.pair(f"G{g}", [P, C, w]) for g, (_, w, _) in enumerate(tables)]
                self.MSG = sb("MSG", [P, R, 1 + C], F32, ctx)
                self.DEC = self.pair("DEC", [P, R, 1 + C])
                self.OUT = self.pair("OUT", [P, C, R + H])
                self.EX = self.pair("EX", [P, 2, H, C])
                self.ARG = sb("ARG", [P, 2, H, C], F32, ctx)
                self.LG = sb("LG", [P, H, 1 + C], F32, ctx)
                self.BR = sb("BR", [P, H, 1 + C], F32, ctx)
                self.T1 = sb("T1", [P, C, self.FE], F32, ctx)
                self.idx_in, self.attr_in, self.stored = (
                    [self.sem(f"{name}{b}") for b in range(2)] for name in ("idx_in", "attr_in", "stored"))
                self.rows_in = [[self.sem(f"rows{g}_in{b}") for b in range(2)] for g in range(len(tables))]
                self.ready, self.a_steps, self.b_steps = self.sem("ready"), self.sem("a_steps"), self.sem("b_steps")
                self.args_ready, self.exps_ready = self.sem("args_ready"), self.sem("exps_ready")
                self.decays_ready, self.scanned = self.sem("decays_ready"), self.sem("scanned")
                self.copied_out = self.sem("copied_out")
                if layer in (0, 2):
                    self.RAW = self.pair("RAW", [P, C, 64])
                    self.XI = self.pair("XI", [P, 64, 1 + C])
                    self.XE = self.pair("XE", [P, 64, 1 + C])
                    self.HOLD = self.pair("HOLD", [P, 64, 1 + C]) if layer == 0 else self.DEC
                    self.FIRST = sb("FIRST", [P, 64], F32, ctx)
                    self.raw_in = [self.sem(f"raw_in{b}") for b in range(2)]
                    self.raw_turned, self.held, self.expanded = (self.sem("raw_turned"), self.sem("held"),
                                                                 self.sem("expanded"))
                    self.x_steps, self.first_in = self.sem("x_steps"), self.sem("first_in")

            def sem(self, name):
                return phase_semaphore(name)

            def pair(self, name, shape, dt=F32):
                return [sb(f"{name}{b}", shape, dt, self.ctx) for b in range(2)]

            def bank(self, name):
                return self.ctx.enter_context(nc.psum_tensor(unique(name), [P, 512], F32))

            def constants(self):
                fills = [(SC[1][:, :, :], 0.0), (MS[1][:, :, :], NEG), (self.BR[:, :, :], NEG)]
                fills += [(self.DEC[b][:, :, :], 0.0) for b in range(2)]
                if self.layer == 0:
                    fills += [(self.HOLD[b][:, :, :], 0.0) for b in range(2)]
                fills += [(self.OUT[b][:, :, self.R:], 0.0) for b in range(2)]
                for ap, value in fills:
                    nc.gpsimd.memset(ap, value).then_inc(self.ready, 1)
                assert len(fills) == self.N_READY, len(fills)

            def first_rows(self, pool, table):
                pool.indirect_dma_start(out=self.FIRST[:, :], out_offset=None, in_=table,
                                        in_offset=bass.IndirectOffsetOnAxis(ap=FIRST_DST[:, 0:1], axis=0))\
                    .then_inc(self.first_in, 16)

            def load_spread(self, sp, t, n, b, first):
                if not first:
                    wait(sp, self.raw_turned, t - 1)
                sp.dma_start(self.RAW[b][:, :, :], row_view(spread, t)).then_inc(self.raw_in[b], 16)

            def turn(self, act, t, n, b, first):
                wait(act, self.raw_in[b], (n + 1) * 16)
                if not first:
                    wait(act, self.expanded, t - 1)
                nc.scalar.activation(self.XI[b][:, :, 1:1 + C], self.RAW[b][:, :, :].rearrange("p j f -> p f j"),
                                     ACT.Copy).then_inc(self.raw_turned, 1)
                if self.layer == 2:
                    self.same_factors(act, t, b, first)
                else:
                    act.sem_inc(parked, 1)
                    nc.scalar.activation(self.HOLD[b][:, :, 1:1 + C],
                                         SAME[:, bass.ds(t * C, C)].unsqueeze(1).to_broadcast([P, 64, C]),
                                         ACT.Copy).then_inc(self.held, 1)

            def expand(self, v, t, n, b, first):
                st = Steps(v, self.x_steps, t)
                if first:
                    wait(v, self.first_in, 16)
                    before_ = self.FIRST[:, :].unsqueeze(2)
                else:
                    before_ = self.XE[1 - b][:, :, C:C + 1]
                st.do(nc.vector.tensor_copy(self.XI[b][:, :, 0:1], before_))
                st.wait()
                wait(v, self.raw_turned, t + 1)
                if self.layer == 2:
                    wait(v, self.decays_ready, t + 1)
                else:
                    wait(v, self.held, t + 1)
                flat = lambda ap: ap.rearrange("p f j -> p (f j)")
                nc.vector.tensor_tensor_scan(flat(self.XE[b][:, :, :]), flat(self.HOLD[b][:, 0:64, :]),
                                             flat(self.XI[b][:, :, :]), 0.0, ALU.mult, ALU.add)\
                    .then_inc(self.expanded, 1)
                wait(v, self.expanded, t + 1)

            def gathers(self, pool):
                def step(t, n, b, first, last):
                    wait(pool, self.idx_in[b], (n + 1) * (16 * len(self.indices)))
                    if not first:
                        wait(pool, self.scanned, t - 1)
                    pool.sem_inc(parked, 1)
                    for c in range(C):
                        for g, (tab, _, which) in enumerate(self.tables):
                            pool.indirect_dma_start(
                                out=self.G[g][b][:, c, :], out_offset=None, in_=tab,
                                in_offset=bass.IndirectOffsetOnAxis(ap=self.IDX[which][b][:, c:c + 1], axis=0),
                            ).then_inc(self.rows_in[g][b], 16)
                chunks(pool, step)

            def load_indices(self, sp, t, n, b, first):
                if not first:
                    for g in range(len(self.tables)):
                        wait(sp, self.rows_in[g][b], n * (16 * C))
                for name, source in self.indices.items():
                    sp.dma_start(self.IDX[name][b][:, :], source[:, bass.ds(t * C, C)])\
                      .then_inc(self.idx_in[b], 16)

            def maxima(self, v, st, t, n, b, first):
                nc_v, H = nc.vector, self.H
                st.do(nc_v.tensor_copy(self.LG[:, :, 0:1], MS[1 - b][:, 0:H, C:C + 1]))
                st.wait()
                if not first:
                    wait(v, self.copied_out, (t - 1) * 2)
                flat = lambda ap: ap.rearrange("p h j -> p (h j)")
                st.then(nc_v.tensor_tensor_scan(flat(MS[b][:, 0:H, :]), flat(self.BR[:, :, :]),
                                                flat(self.LG[:, :, :]), 0.0, ALU.add, ALU.max))
                if not first:
                    wait(v, self.exps_ready, t)
                st.do(nc_v.tensor_tensor(self.ARG[:, 0, :, :], MS[b][:, 0:H, 0:C], MS[b][:, 0:H, 1:1 + C],
                                         ALU.subtract))
                st.then(nc_v.tensor_tensor(self.ARG[:, 1, :, :], self.LG[:, :, 1:1 + C], MS[b][:, 0:H, 1:1 + C],
                                           ALU.subtract))
                nc_v.tensor_tensor(self.ARG[:, 0, :, :], self.ARG[:, 0, :, :], self.BR[:, :, 1:1 + C], ALU.add)\
                    .then_inc(self.args_ready, 1)

            def breaks(self, st, t):
                st.do(nc.vector.tensor_scalar(self.BR[:, :, 1:1 + C],
                                              BREAK[:, bass.ds(t * C, C)].unsqueeze(1)
                                              .to_broadcast([P, self.H, C]), 1.0, None, ALU.mult))

            def sums(self, v, t, n, b, first, rows, weight=None):
                H, FE, R = self.H, self.FE, self.R
                st = Steps(v, self.b_steps, t * (3 if self.weights else 2))
                wait(v, self.decays_ready, (t + 1) * self.n_decays())
                if self.layer == 2:
                    wait(v, self.exps_ready, t + 1)
                if weight is None:
                    w = self.EX[b][:, 1, :, :].unsqueeze(2).to_broadcast([P, H, CH, C])
                    st.do(nc.vector.tensor_tensor(
                        self.MSG[:, 0:FE, 1:1 + C].rearrange("p (h c) j -> p h c j", c=CH),
                        rows.rearrange("p j (h c) -> p h c j", c=CH), w, ALU.mult))
                    st.do(nc.vector.tensor_copy(self.MSG[:, FE:R, 1:1 + C], self.EX[b][:, 1, :, :]))
                else:
                    st.do(nc.vector.tensor_tensor(self.MSG[:, :, 1:1 + C], rows.rearrange("p j f -> p f j"),
                                                  weight.unsqueeze(1).to_broadcast([P, FE, C]), ALU.mult))
                st.do(nc.vector.tensor_copy(self.MSG[:, :, 0:1], SC[1 - b][:, 0:R, C:C + 1]))
                st.wait()
                if not first:
                    wait(v, self.copied_out, (t - 1) * self.n_copies())
                flat = lambda ap: ap.rearrange("p r j -> p (r j)")
                nc.vector.tensor_tensor_scan(flat(SC[b][:, 0:R, :]), flat(self.DEC[b][:, :, :]),
                                             flat(self.MSG[:, :, :]), 0.0, ALU.mult, ALU.add)\
                    .then_inc(self.scanned, 1)
                wait(v, self.scanned, t + 1)

            def n_decays(self):
                return 2 if self.running_max else 1

            def n_copies(self):
                return 2 if self.running_max else 1

            def factors(self, act, t, n, b, first):
                H, FE, R = self.H, self.FE, self.R
                if self.layer != 3:
                    wait(act, self.args_ready, t + 1)
                if not first:
                    wait(act, self.scanned, t - 1)
                if self.running_max:
                    nc.scalar.activation(self.EX[b][:, :, :, :], self.ARG[:, :, :, :], ACT.Exp)\
                      .then_inc(self.exps_ready, 1)
                    wait(act, self.exps_ready, t + 1)
                    decay = self.EX[b][:, 0, :, :]
                    nc.scalar.activation(self.DEC[b][:, 0:FE, 1:1 + C].rearrange("p (h c) j -> p h c j", c=CH),
                                         decay.unsqueeze(2).to_broadcast([P, H, CH, C]), ACT.Copy)\
                      .then_inc(self.decays_ready, 1)
                    nc.scalar.activation(self.DEC[b][:, FE:R, 1:1 + C], decay, ACT.Copy)\
                      .then_inc(self.decays_ready, 1)
                    return
                if self.layer == 2:
                    nc.scalar.activation(self.EX[b][:, 1, :, :], self.ARG[:, 1, :, :], ACT.Exp)\
                      .then_inc(self.exps_ready, 1)
                else:
                    self.same_factors(act, t, b, first)

            def same_factors(self, act, t, b, first):
                if not first:
                    wait(act, self.scanned, t - 1)
                act.sem_inc(parked, 1)
                nc.scalar.activation(self.DEC[b][:, :, 1:1 + C],
                                     SAME[:, bass.ds(t * C, C)].unsqueeze(1).to_broadcast([P, self.R, C]),
                                     ACT.Copy)\
                  .then_inc(self.decays_ready, 1)

            def store_rows(self, act, t, n, b, early):
                R, H = self.R, self.H
                wait(act, self.scanned, t + 1)
                if not early:
                    wait(act, self.stored[b], n * 16)
                nc.scalar.activation(self.OUT[b][:, :, 0:R], SC[b][:, 0:R, 1:1 + C].rearrange("p r j -> p j r"),
                                     ACT.Copy).then_inc(self.copied_out, 1)
                if self.running_max:
                    nc.scalar.activation(self.OUT[b][:, :, R:R + H],
                                         MS[b][:, 0:H, 1:1 + C].rearrange("p r j -> p j r"), ACT.Copy)\
                      .then_inc(self.copied_out, 1)
                wait(act, self.copied_out, (t + 1) * self.n_copies())
                act.dma_start(row_view(scan_tabs[self.layer], t), self.OUT[b][:, :, :])\
                   .then_inc(self.stored[b], 16)

            def drain_stores(self, act):
                for b in range(2):
                    wait(act, self.stored[b], NCH // 2 * 16)

        def edges_0(src_ap):
            with ExitStack() as ctx:
                e = Edges(ctx, 0, [(xl_tab, 64, "src")], {"src": src_ap})
                ATTR = e.pair("ATTR", [P, C, 16])
                ATTR_T = sb("ATTR_T", [P, P], F32, ctx)
                WE8 = sb("WE8", [P, C, 64], F32, ctx)
                TR, PROJ = [e.bank("TR0"), e.bank("TR1")], [e.bank("PROJ0"), e.bank("PROJ1")]
                attr_t, attr_c, projected, we_in, cleared = (e.sem("attr_t"), e.sem("attr_c"), e.sem("projected"),
                                                             e.sem("we_in"), e.sem("cleared"))
                with nc.Block() as block:
                    @block.sync
                    def _(sp):
                        wait(sp, cleared, 1)
                        for c in range(C):
                            sp.dma_start(WE8[16 * c:16 * c + 16, c, :], we).then_inc(we_in, 16)

                        def step(t, n, b, first, last):
                            e.load_indices(sp, t, n, b, first)
                            e.load_spread(sp, t, n, b, first)
                            if not first:
                                wait(sp, attr_t, t - 1)
                            sp.dma_start(ATTR[b][:, :, :], row_view(ea16, t)).then_inc(e.attr_in[b], 16)
                        chunks(sp, step)

                    @block.gpsimd
                    def _(pool):
                        nc.gpsimd.memset(WE8[:, :, :], 0.0).then_inc(cleared, 1)
                        e.constants()
                        e.first_rows(pool, xr_tab)
                        e.gathers(pool)

                    @block.tensor
                    def _(pe):
                        wait(pe, we_in, 16 * C)

                        def step(t, n, b, first, last):
                            wait(pe, e.attr_in[b], (n + 1) * 16)
                            nc.tensor.transpose(TR[b][:, 0:P], ATTR[b][:, :, :].rearrange("p j f -> p (j f)"),
                                                IDENT[:, :]).then_inc(attr_t, 1)
                            wait(pe, attr_c, t + 1)
                            if not first:
                                wait(pe, e.args_ready, t - 1)
                            nc.tensor.matmul(PROJ[b][:, :], ATTR_T[:, :],
                                             WE8[:, :, :].rearrange("p j f -> p (j f)"), start=True, stop=True)\
                              .then_inc(projected, 1)
                        chunks(pe, step)

                    @block.scalar
                    def _(act):
                        wait(act, e.ready, e.N_READY)

                        def ahead(t, n, b, first):
                            e.turn(act, t, n, b, first)
                            wait(act, attr_t, t + 1)
                            if not first:
                                wait(act, projected, t)
                            nc.scalar.activation(ATTR_T[:, :], TR[b][:, 0:P], ACT.Copy).then_inc(attr_c, 1)

                        def step(t, n, b, first, last):
                            if first:
                                ahead(t, n, b, True)
                            e.factors(act, t, n, b, first)
                            if not last:
                                ahead(t + 1, n + b, 1 - b, False)
                            e.store_rows(act, t, n, b, first)
                        chunks(act, step)
                        e.drain_stores(act)

                    @block.vector
                    def _(v):
                        wait(v, e.ready, e.N_READY)

                        def logits(t, n, b, first):
                            T, LG = e.T1, e.LG
                            st = Steps(v, e.a_steps, t * 10)
                            wait(v, e.rows_in[0][b], (n + 1) * (16 * C))
                            st.then(nc.vector.tensor_tensor(T[:, :, :], e.G[0][b][:, :, :],
                                                            e.XE[b][:, :, 1:1 + C].rearrange("p f j -> p j f"),
                                                            ALU.add))
                            wait(v, projected, t + 1)
                            st.then(nc.vector.tensor_tensor(T[:, :, :], T[:, :, :],
                                                            PROJ[b][:, :].rearrange("p (j f) -> p j f", j=C),
                                                            ALU.add))
                            st.then(nc.vector.scalar_tensor_tensor(out=T[:, :, :], in0=T[:, :, :], scalar=0.2,
                                                                   in1=T[:, :, :], op0=ALU.mult, op1=ALU.max))
                            st.then(nc.vector.tensor_tensor(T[:, :, :], T[:, :, :],
                                                            vec("att").unsqueeze(1).to_broadcast([P, C, 64]),
                                                            ALU.mult))
                            if not first:
                                wait(v, e.args_ready, t)
                            e.breaks(st, t)
                            st.do(nc.vector.tensor_reduce(LG[:, :, 1:1 + C].rearrange("p h j -> p j h"),
                                                          T[:, :, :].rearrange("p j (h c) -> p j h c", c=CH),
                                                          AX.X, ALU.add))
                            e.maxima(v, st, t, n, b, first)
                            assert st.n == 10, st.n

                        def step(t, n, b, first, last):
                            e.expand(v, t, n, b, first)
                            logits(t, n, b, first)
                            e.sums(v, t, n, b, first, e.G[0][b][:, :, :])
                        chunks(v, step)

        def edges_2(src_ap):
            with ExitStack() as ctx:
                e = Edges(ctx, 2, [(kv_tab, 128, "src")], {"src": src_ap})
                with nc.Block() as block:
                    @block.sync
                    def _(sp):
                        def step(t, n, b, first, last):
                            e.load_indices(sp, t, n, b, first)
                            e.load_spread(sp, t, n, b, first)
                        chunks(sp, step)

                    @block.gpsimd
                    def _(pool):
                        e.constants()
                        e.first_rows(pool, q2_tab)
                        e.gathers(pool)

                    @block.scalar
                    def _(act):
                        wait(act, e.ready, e.N_READY)

                        def step(t, n, b, first, last):
                            if first:
                                e.turn(act, t, n, b, True)
                            e.factors(act, t, n, b, first)
                            if not last:
                                e.turn(act, t + 1, n + b, 1 - b, False)
                            e.store_rows(act, t, n, b, first)
                        chunks(act, step)
                        e.drain_stores(act)

                    @block.vector
                    def _(v):
                        wait(v, e.ready, e.N_READY)

                        def scores(t, n, b, first):
                            st = Steps(v, e.a_steps, t * 3)
                            wait(v, e.rows_in[0][b], (n + 1) * (16 * C))
                            st.then(nc.vector.tensor_tensor(e.T1[:, :, :], e.G[0][b][:, :, 0:64],
                                                            e.XE[b][:, :, 1:1 + C].rearrange("p f j -> p j f"),
                                                            ALU.mult))
                            st.then(nc.vector.tensor_reduce(e.LG[:, :, 0:C].rearrange("p h j -> p j h"),
                                                            e.T1[:, :, :].rearrange("p j (h c) -> p j h c", c=CH),
                                                            AX.X, ALU.add))
                            st.then(nc.vector.tensor_scalar(e.LG[:, :, 0:C], e.LG[:, :, 0:C], 1.0 / D ** 0.5, -5.0,
                                                            ALU.mult, ALU.max))
                            if not first:
                                wait(v, e.exps_ready, t)
                            nc.vector.tensor_scalar(e.ARG[:, 1, :, :], e.LG[:, :, 0:C], 5.0, None, ALU.min)\
                              .then_inc(e.args_ready, 1)

                        def step(t, n, b, first, last):
                            e.expand(v, t, n, b, first)
                            scores(t, n, b, first)
                            e.sums(v, t, n, b, first, e.G[0][b][:, :, 64:128])
                        chunks(v, step)

        def edges_3():
            with ExitStack() as ctx:
                e = Edges(ctx, 3, [(rel_tab, 64, "rel")], {"rel": relidx})
                EW = sb("EW", [P, J], F32, ctx)
                ew_in = e.sem("ew_in")
                with nc.Block() as block:
                    @block.sync
                    def _(sp):
                        sp.dma_start(EW[:, :], ew).then_inc(ew_in, 16)
                        chunks(sp, lambda t, n, b, first, last: e.load_indices(sp, t, n, b, first))

                    @block.gpsimd
                    def _(pool):
                        e.constants()
                        e.gathers(pool)

                    @block.scalar
                    def _(act):
                        wait(act, e.ready, e.N_READY)

                        def step(t, n, b, first, last):
                            e.factors(act, t, n, b, first)
                            e.store_rows(act, t, n, b, first)
                        chunks(act, step)
                        e.drain_stores(act)

                    @block.vector
                    def _(v):
                        wait(v, e.ready, e.N_READY)
                        wait(v, ew_in, 16)

                        def step(t, n, b, first, last):
                            wait(v, e.rows_in[0][b], (n + 1) * (16 * C))
                            e.sums(v, t, n, b, first, e.G[0][b][:, :, :], EW[:, bass.ds(t * C, C)])
                        chunks(v, step)

        def edges_1(src_ap, dst_ap):
            with ExitStack() as ctx:
                e = Edges(ctx, 1, [(x1_tab, 64, "src"), (q1_tab, 128, "dst")], {"src": src_ap, "dst": dst_ap})
                EF, S9 = e.pair("EF", [P, C, 64]), e.pair("S9", [P, C, SH])
                XS = sb("XS", [P, C, SH, 64], F32, ctx)
                XHI, XLO = e.pair("XHI", [P, 5, 512], F32R), e.pair("XLO", [P, 5, 512], F32R)
                EFT = sb("EFT", [P, 512], F32, ctx)
                HT = [[sb(f"HT{b}{a}", [P, 512], F32, ctx) for a in range(2)] for b in range(2)]
                WKV = e.pair("WKV", [P, 256])
                RW = e.pair("RW", [P, C, 256])
                CHI, CLO = sb("CHI", [P, 5, 256], F32R, ctx), sb("CLO", [P, 5, 256], F32R, ctx)
                CF = XS[:, :, :, :].rearrange("p j s f -> p (j s f)")[:, 0:5 * 256]\
                    .rearrange("p (k n) -> p k n", k=5)
                W1 = sb("W1", [P, P], F32, ctx)
                W2 = sb("W2", [P, 256], F32, ctx)
                B1 = sb("B1", [P, 1], F32, ctx)
                B2F = sb("B2F", [1, 5, 256], F32, ctx)
                B2 = [sb(f"B2{i}", [1, 256], BF16, ctx) for i in range(3)]
                B2R = sb("B2R", [3, 256], BF16, ctx)
                ONEB = sb("ONEB", [3, P], BF16, ctx)
                RING = [e.bank(f"RING{i}") for i in range(4)]
                COLS = [e.bank(f"COLS{i}") for i in range(4)]
                xs_ready, staged, evacuated = e.sem("xs_ready"), e.sem("staged"), e.sem("evacuated")
                col_done, w_copied, col_used = e.sem("col_done"), e.sem("w_copied"), e.sem("col_used")
                w_in, parts, b2_in, split, c_split = (e.sem("w_in"), e.sem("parts"), e.sem("b2_in"),
                                                      e.sem("split"), e.sem("c_split"))

                STAGES = 13

                def ring(q, b):
                    return (q + b) % 4

                def holder_before(q, b):
                    return next(d for d in range(1, STAGES + 1)
                                if ring((q - d) % STAGES, b if q >= d else 1 - b) == ring(q, b))

                def first_stage(half):
                    return (1, 8)[half]

                with nc.Block() as block:
                    @block.sync
                    def _(sp):
                        wait(sp, parts, 1)
                        for ap, source in ((CF[:, 0:4, :], cfix[0:512, :].rearrange("(k p) n -> p k n", p=P)),
                                           (CF[0:64, 4, :], cfix[512:576, :]),
                                           (W2[0:64, 0:128], w2[:, 0:128]), (W2[64:128, 128:256], w2[:, 128:256]),
                                           (B1[:, :], b1), (B2F[:, 0, :], b2),
                                           (W1[0:64, :], w64[:, W_COLS["k_w1"][0]:W_COLS["v_w1"][1]]),
                                           (W1[64:128, :], w64[:, W_COLS["k_w1"][0]:W_COLS["v_w1"][1]])):
                            sp.dma_start(ap, source).then_inc(w_in, 16)

                        wait(sp, parts, 8)
                        for i in range(3):
                            sp.dma_start(B2R[i:i + 1, :], B2[i][:, :]).then_inc(b2_in, 16)

                        def step(t, n, b, first, last):
                            e.load_indices(sp, t, n, b, first)
                            if not first:
                                wait(sp, staged, t * STAGES - (2 * STAGES - 1))
                                wait(sp, xs_ready, (t - 1) * 2)
                            sp.dma_start(EF[b][:, :, :], row_view(ea64, t)).then_inc(e.attr_in[b], 16)
                            sp.dma_start(S9[b][:, :, :], row_view(ea9, t)).then_inc(e.attr_in[b], 16)
                        chunks(sp, step)

                    @block.gpsimd
                    def _(pool):
                        nc.gpsimd.memset(W2[:, :], 0.0).then_inc(parts, 1)
                        e.constants()

                        def rows(g, t, n, b):
                            tab, _, which = e.tables[g]
                            pool.sem_inc(parked, 1)
                            for col in range(C):
                                pool.indirect_dma_start(
                                    out=e.G[g][b][:, col, :], out_offset=None, in_=tab,
                                    in_offset=bass.IndirectOffsetOnAxis(ap=e.IDX[which][b][:, col:col + 1], axis=0),
                                ).then_inc(e.rows_in[g][b], 16)

                        def node_rows(t, n, b, first):
                            wait(pool, e.idx_in[b], (n + 1) * 32)
                            if not first:
                                wait(pool, xs_ready, (t - 1) * 2)
                            rows(0, t, n, b)

                        def step(t, n, b, first, last):
                            if first:
                                node_rows(0, 0, 0, True)
                                node_rows(1, 0, 1, True)
                            elif not last:
                                node_rows(t + 1, n + b, 1 - b, False)
                            wait(pool, e.idx_in[b], (n + 1) * 32)
                            if not first:
                                wait(pool, e.args_ready, t - 1)
                            rows(1, t, n, b)
                        chunks(pool, step)

                    @block.tensor
                    def _(pe):
                        wait(pe, w_in, 16 * 8)
                        wait(pe, b2_in, 48)
                        wait(pe, c_split, 2)

                        def free(t, q, b, first):
                            back = holder_before(q, b)
                            if first and q < back:
                                return
                            old, tt = (q - back) % STAGES, t if q >= back else t - 1
                            if old in (0, 6, 7):
                                wait(pe, evacuated, tt * STAGES + (old + 1))
                            else:
                                wait(pe, split, tt * 10 + (old if old < 6 else old - 2))

                        def transposes(t, b, half, first):
                            for k in range(5):
                                q = first_stage(half) + k
                                rows = P if k < 4 else 64
                                free(t, q, b, first)
                                if k == 4:
                                    pe.sem_inc(parked, 1)
                                for c in range(4):
                                    last = nc.tensor.transpose(
                                        RING[ring(q, b)][0:rows, c * P:(c + 1) * P],
                                        XS[:, 4 * half + c, :, :].rearrange("p s f -> p (s f)")
                                        [:, k * P:k * P + rows], IDENT[:, :])
                                last.then_inc(staged, 1)

                        def columns(t, b, half, first):
                            wait(pe, split, t * 10 + 5 * (half + 1))
                            wait(pe, evacuated, t * STAGES + 8)
                            for c in range(4):
                                col = 4 * half + c
                                if not (first and half == 0):
                                    wait(pe, col_used, t * C + (col - 3))
                                bank = COLS[col % 4]
                                for k in range(5):
                                    rows = P if k < 4 else 64
                                    hi, lo = (a[half][0:rows, k, c * P:(c + 1) * P] for a in (XHI, XLO))
                                    nc.tensor.matmul(bank[:, 0:256], hi, CHI[0:rows, k, :], start=(k == 0),
                                                     stop=False)
                                    nc.tensor.matmul(bank[:, 0:256], hi, CLO[0:rows, k, :], start=False,
                                                     stop=False)
                                    nc.tensor.matmul(bank[:, 0:256], lo, CHI[0:rows, k, :], start=False,
                                                     stop=(k == 4))
                                nc.tensor.matmul(bank[:, 256:512], ONEB[:, :], B2R[:, :], start=True, stop=False)
                                nc.tensor.matmul(bank[:, 256:512],
                                                 HT[b][col % 2][:, (col // 2) * P:(col // 2 + 1) * P],
                                                 W2[:, :], start=False, stop=True).then_inc(col_done, 1)

                        def step(t, n, b, first, last):
                            wait(pe, e.attr_in[b], (n + 1) * 32)
                            free(t, 0, b, first)
                            for c in range(4):
                                ins = nc.tensor.transpose(RING[ring(0, b)][:, c * P:(c + 1) * P],
                                                          EF[b][:, 2 * c:2 * c + 2, :]
                                                          .rearrange("p j f -> p (j f)"), IDENT[:, :])
                            ins.then_inc(staged, 1)
                            wait(pe, xs_ready, t * 2 + 1)
                            transposes(t, b, 0, first)
                            for a in range(2):
                                free(t, 6 + a, b, first)
                                nc.tensor.matmul(RING[ring(6 + a, b)][:, :], W1[64 * a:64 * a + 64, :],
                                                 EFT[64 * a:64 * a + 64, :], start=True, stop=True)\
                                  .then_inc(staged, 1)
                            if not first:
                                columns(t - 1, 1 - b, 1, False)
                            wait(pe, xs_ready, t * 2 + 2)
                            transposes(t, b, 1, first)
                            columns(t, b, 0, first)

                        chunks(pe, step)
                        columns(NCH - 1, 1, 1, False)

                    @block.scalar
                    def _(act):
                        wait(act, w_in, 16 * 8)
                        wait(act, e.ready, e.N_READY)

                        def evacuate(t, q, b, out_ap, rows=P, func=ACT.Copy, **kw):
                            wait(act, staged, t * STAGES + (q + 1))
                            nc.scalar.activation(out_ap, RING[ring(q, b)][0:rows, :], func, **kw)\
                              .then_inc(evacuated, 1)

                        def half_transposes(t, b, half, first):
                            if not first:
                                wait(act, col_done, t * C - (4 if half == 0 else 0))
                            for k in range(5):
                                rows = P if k < 4 else 64
                                evacuate(t, first_stage(half) + k, b, XHI[half][0:rows, k, :], rows)

                        def weights(t, col, early):
                            wait(act, col_done, t * C + (col + 1))
                            if not early:
                                wait(act, col_used, t * C + (col - 1))
                            nc.scalar.activation(WKV[col % 2][:, :], COLS[col % 4][:, 256:512], ACT.Copy)\
                              .then_inc(w_copied, 1)

                        def step(t, n, b, first, last):
                            if not first:
                                wait(act, staged, t * STAGES - (STAGES - 8))
                            evacuate(t, 0, b, EFT[:, :])
                            half_transposes(t, b, 0, first)
                            for a in range(2):
                                evacuate(t, 6 + a, b, HT[b][a][:, :], func=ACT.Relu, bias=B1[:, 0:1])
                            if not isinstance(t, int) or t >= 2:
                                e.store_rows(act, t - 2, n - 1, b, False)
                            if not first:
                                for col in range(4, 8):
                                    weights(t - 1, col, False)
                            half_transposes(t, b, 1, first)
                            if not first:
                                e.factors(act, t - 1, before(n, b), 1 - b, False)
                            for col in range(4):
                                weights(t, col, first and col < 2)
                        chunks(act, step, 4)
                        e.store_rows(act, NCH - 2, NCH // 2 - 1, 0, False)
                        for col in range(4, 8):
                            weights(NCH - 1, col, False)
                        e.factors(act, NCH - 1, NCH // 2 - 1, 1, False)
                        e.store_rows(act, NCH - 1, NCH // 2 - 1, 1, False)
                        e.drain_stores(act)

                    @block.vector
                    def _(v):
                        wait(v, e.ready, e.N_READY)
                        wait(v, w_in, 16 * 8)
                        nc.vector.memset(ONEB[:, :], 1.0).then_inc(parts, 1)
                        nc.vector.tensor_copy(B2[0][:, :], B2F[:, 0, :]).then_inc(parts, 1)
                        wait(v, parts, 3)
                        nc.vector.tensor_tensor(B2F[:, 1, :], B2F[:, 0, :], B2[0][:, :], ALU.subtract)\
                          .then_inc(parts, 1)
                        wait(v, parts, 4)
                        nc.vector.tensor_copy(B2[1][:, :], B2F[:, 1, :]).then_inc(parts, 1)
                        wait(v, parts, 5)
                        nc.vector.tensor_tensor(B2F[:, 2, :], B2F[:, 1, :], B2[1][:, :], ALU.subtract)\
                          .then_inc(parts, 1)
                        wait(v, parts, 6)
                        nc.vector.tensor_copy(B2[2][:, :], B2F[:, 2, :]).then_inc(parts, 2)

                        nc.vector.tensor_copy(CHI[:, 0:4, :], CF[:, 0:4, :]).then_inc(parts, 1)
                        nc.vector.tensor_copy(CHI[0:64, 4, :], CF[0:64, 4, :]).then_inc(parts, 1)
                        wait(v, parts, 10)
                        nc.vector.tensor_tensor(CLO[:, 0:4, :], CF[:, 0:4, :], CHI[:, 0:4, :].bitcast(F32),
                                                ALU.subtract).then_inc(c_split, 1)
                        nc.vector.tensor_tensor(CLO[0:64, 4, :], CF[0:64, 4, :], CHI[0:64, 4, :].bitcast(F32),
                                                ALU.subtract).then_inc(c_split, 1)
                        wait(v, c_split, 2)

                        def outer(t, n, b, first, half):
                            if half == 0:
                                wait(v, e.rows_in[0][b], (n + 1) * (16 * C))
                                wait(v, e.attr_in[b], (n + 1) * 32)
                            if not first:
                                wait(v, staged, t * STAGES - (STAGES - (6, 13)[half]))
                            j = slice(4 * half, 4 * half + 4)
                            nc.vector.tensor_tensor(
                                XS[:, j, :, :],
                                e.G[0][b][:, j, :].unsqueeze(2).to_broadcast([P, 4, SH, 64]),
                                S9[b][:, j, :].unsqueeze(3).to_broadcast([P, 4, SH, 64]), ALU.mult)\
                              .then_inc(xs_ready, 1)

                        def lows(t, b, half, first):
                            if not first:
                                wait(v, col_done, t * C - (4 if half == 0 else 0))
                            for k in range(5):
                                q = first_stage(half) + k
                                rows = P if k < 4 else 64
                                wait(v, evacuated, t * STAGES + (q + 1))
                                nc.vector.tensor_tensor(XLO[half][0:rows, k, :], RING[ring(q, b)][0:rows, :],
                                                        XHI[half][0:rows, k, :].bitcast(F32), ALU.subtract)\
                                  .then_inc(split, 1)

                        def products(t, b, cols):
                            for col in cols:
                                wait(v, w_copied, t * C + (col + 1))
                                nc.vector.tensor_tensor(RW[b][:, col, :], COLS[col % 4][:, 0:256],
                                                        WKV[col % 2][:, :], ALU.mult).then_inc(col_used, 1)

                        def logits(t, n, b, first):
                            st = Steps(v, e.a_steps, t * 7)
                            wait(v, e.rows_in[1][b], (n + 1) * (16 * C))
                            wait(v, col_used, (t + 1) * C)
                            st.then(nc.vector.tensor_tensor(e.T1[:, :, :], RW[b][:, :, 0:128], e.G[1][b][:, :, :],
                                                            ALU.mult))
                            if not first:
                                wait(v, e.args_ready, t)
                            e.breaks(st, t)
                            st.do(nc.vector.tensor_reduce(e.LG[:, :, 1:1 + C].rearrange("p h j -> p j h"),
                                                          e.T1[:, :, :].rearrange("p j (h c) -> p j h c", c=CH),
                                                          AX.X, ALU.add))
                            e.maxima(v, st, t, n, b, first)
                            assert st.n == 7, st.n

                        def step(t, n, b, first, last):
                            if first:
                                for half in range(2):
                                    outer(0, 0, 0, True, half)
                            lows(t, b, 0, first)
                            if not isinstance(t, int) or t >= 2:
                                e.sums(v, t - 2, n - 1, b, False, RW[b][:, :, 128:256])
                            if not first:
                                products(t - 1, 1 - b, range(4, 8))
                            if not last:
                                outer(t + 1, n + b, 1 - b, False, 0)
                            lows(t, b, 1, first)
                            if not first:
                                logits(t - 1, before(n, b), 1 - b, False)
                            if not last:
                                outer(t + 1, n + b, 1 - b, False, 1)
                            products(t, b, range(4))
                        chunks(v, step, 4)
                        end = NCH - 1
                        e.sums(v, end - 1, NCH // 2 - 1, 0, False, RW[0][:, :, 128:256])
                        products(end, 1, range(4, 8))
                        logits(end, NCH // 2 - 1, 1, False)
                        e.sums(v, end, NCH // 2 - 1, 1, False, RW[1][:, :, 128:256])

        def finish_layer(layer):
            H, R, WD = HEADS[layer], SUMS[layer], ROW[layer]
            FE = H * CH
            has_weights = R > FE
            groups = H // 4
            GR = 64 + 4 * has_weights
            with ExitStack() as ctx:
                def s(name):
                    return phase_semaphore(name)

                def bank(name):
                    return ctx.enter_context(nc.psum_tensor(unique(name), [P, 512], F32))

                GN = sb("GN", [P, K, WD], F32, ctx)
                GC = sb("GC", [P, K, WD], F32, ctx)
                MX = sb("MX", [P, K, H], F32, ctx)
                Y = sb("Y", [P, K, 64], F32, ctx)
                SQ = sb("SQ", [P, K, 64], F32, ctx)
                AT = sb("AT", [P, K * P], F32, ctx)
                LROW = sb("LROW", [P, 3, GR], F32, ctx)
                CT = sb("CT", [P, 3, P], F32, ctx)
                CW = sb("CW", [P, 5, P], F32, ctx)
                CROW = sb("CROW", [P, WD], F32, ctx)
                NULL = sb("NULL", [1, WD], F32, ctx)
                SM = sb("SM", [P, 8, 64], F32, ctx)
                SN = sb("SN", [P, 6, K], F32, ctx)
                TP = [bank("TP0"), bank("TP1")]
                CP, CB, PB = bank("CP"), bank("CB"), bank("PB")
                PO = [bank("PO0"), bank("PO1")]
                dve, null_set, carried = s("dve"), s("null_set"), s("carried")
                rows_in, carry_in, stored = s("rows_in"), s("carry_in"), s("stored")
                c_rows, c_tp, c_arg, c_exp, c_sum, c_back, c_row = (s("c_rows"), s("c_tp"), s("c_arg"), s("c_exp"),
                                                                    s("c_sum"), s("c_back"), s("c_row"))
                merge_arg, merge_exp, agg_ready, agg_t, agg_c, agg_mm, agg_add = (
                    s("merge_arg"), s("merge_exp"), s("agg_ready"), s("agg_t"), s("agg_c"), s("agg_mm"), s("agg_add"))
                bn_part, bn_sum, bn_var, bn_sd = s("bn_part"), s("bn_sum"), s("bn_var"), s("bn_sd")
                ln_var, ln_sd, gelu_in, gelu_out, done = s("ln_var"), s("ln_sd"), s("gelu_in"), s("gelu_out"), s("done")
                tab = carry_tabs[layer]
                project_agg = layer in (1, 2)
                units = GROUPS
                N = slice(0, NP)

                with nc.Block() as block:
                    @block.gpsimd
                    def _(pool):
                        nc.gpsimd.memset(NULL[:, :], 0.0).then_inc(null_set, 1)
                        pool.wait_ge(null_set, 1)
                        nc.gpsimd.memset(NULL[:, R:WD], NEG).then_inc(null_set, 1)
                        for k in range(K):
                            pool.indirect_dma_start(
                                out=GN[N, k, :], out_offset=None, in_=scan_tabs[layer],
                                in_offset=bass.IndirectOffsetOnAxis(ap=END_AT[N, k:k + 1], axis=0),
                            ).then_inc(rows_in, 16)
                        pool.wait_ge(carried, 32)
                        for k in range(K):
                            pool.indirect_dma_start(
                                out=GC[N, k, :], out_offset=None, in_=tab,
                                in_offset=bass.IndirectOffsetOnAxis(ap=CARRY_AT[N, k:k + 1], axis=0),
                            ).then_inc(carry_in, 16)

                    @block.sync
                    def _(sp):
                        sp.wait_ge(null_set, 2)
                        sp.dma_start(tab[P:P + 1, :], NULL[:, :]).then_inc(carried, 16)
                        sp.wait_ge(c_row, groups)
                        sp.dma_start(tab[0:P, :], CROW[:, :]).then_inc(carried, 16)
                        sp.wait_ge(carried, 32)
                        if layer == 3:
                            sp.wait_ge(done, 1)
                            sp.dma_start(out.rearrange("(p k) f -> p k f", k=K), X[N, :, :]).then_inc(stored, 16)
                            sp.wait_ge(stored, 16)

                    @block.tensor
                    def _(pe):
                        for g in range(groups):
                            pe.wait_ge(c_rows, g + 1)
                            for n in range(3):
                                last = nc.tensor.transpose(CP[0:GR, n * P:(n + 1) * P], LROW[:, n, :], IDENT[:, :])
                            last.then_inc(c_tp, 1)
                            pe.wait_ge(c_sum, g + 1)
                            nc.tensor.transpose(CB[:, 0:GR], CW[0:GR, 3, :], IDENT[0:GR, 0:GR]).then_inc(c_back, 1)
                            nc.tensor.transpose(CB[:, P:P + GR], CW[0:GR, 0, :], IDENT[0:GR, 0:GR])\
                              .then_inc(c_back, 1)
                        if project_agg:
                            weights = WO_T[:, :] if layer == 1 else wcol("Wo")
                            pe.wait_ge(agg_ready, 1)
                            for u, (k0, m) in enumerate(units):
                                if u >= 2:
                                    pe.wait_ge(agg_c, u - 1)
                                for c in range(m):
                                    last = nc.tensor.transpose(TP[u % 2][0:FE, c * P:c * P + NP],
                                                               GN[N, k0 + c, 0:FE], IDENT[N, N])
                                last.then_inc(agg_t, 1)
                            for u, (k0, m) in enumerate(units):
                                pe.wait_ge(agg_c, u + 1)
                                if u >= 2:
                                    pe.wait_ge(agg_add, u - 1)
                                for c in range(m):
                                    last = nc.tensor.matmul(PO[u % 2][N, c * 64:c * 64 + 64],
                                                            AT[0:FE, (k0 + c) * P:(k0 + c) * P + NP], weights,
                                                            start=True, stop=True)
                                last.then_inc(agg_mm, 1)
                        if layer != 2:
                            for n in range(2):
                                pe.wait_ge(bn_part, n + 1)
                                nc.tensor.matmul(PB[:, n * 64:n * 64 + 64], ONES[N, :], SM[N, n, :], start=True,
                                                 stop=True).then_inc(bn_sum, 1)

                    @block.scalar
                    def _(act):
                        for g in range(groups):
                            act.wait_ge(c_arg, g + 1)
                            nc.scalar.activation(CW[0:GR, 1:3, :], CW[0:GR, 1:3, :], ACT.Exp).then_inc(c_exp, 1)
                        act.wait_ge(merge_arg, 1)
                        nc.scalar.activation(GN[N, :, R:WD], GN[N, :, R:WD], ACT.Exp).then_inc(merge_exp, 1)
                        nc.scalar.activation(GC[N, :, R:WD], GC[N, :, R:WD], ACT.Exp).then_inc(merge_exp, 1)
                        if project_agg:
                            for u, (k0, m) in enumerate(units):
                                act.wait_ge(agg_t, u + 1)
                                nc.scalar.activation(
                                    AT[0:FE, k0 * P:(k0 + m) * P].rearrange("p (k n) -> p k n", n=P)[:, :, N],
                                    TP[u % 2][0:FE, 0:m * P].rearrange("p (k n) -> p k n", n=P)[:, :, N], ACT.Copy)\
                                  .then_inc(agg_c, 1)
                        if layer != 2:
                            act.wait_ge(bn_var, 1)
                            nc.scalar.activation(SM[:, 3, :], SM[:, 3, :], ACT.Sqrt).then_inc(bn_sd, 1)
                        if layer == 0:
                            act.wait_ge(gelu_in, 1)
                            nc.scalar.activation(Y[N, :, :], Y[N, :, :], ACT.Gelu).then_inc(gelu_out, 1)
                        for n in range(2 if layer == 2 else 1):
                            act.wait_ge(ln_var, n + 1)
                            nc.scalar.activation(SN[N, 2, :], SN[N, 2, :], ACT.Sqrt).then_inc(ln_sd, 1)

                    @block.vector
                    def _(v):
                        st = Steps(v, dve)
                        nv = nc.vector
                        tt = nv.tensor_tensor
                        for g in range(groups):
                            last = SC[1][:, :, C:C + 1].rearrange("p r j -> p (r j)")
                            st.do(nv.tensor_copy(LROW[:, 0, 0:64], last[:, 64 * g:64 * g + 64]))
                            if has_weights:
                                st.do(nv.tensor_copy(LROW[:, 0, 64:68], last[:, FE + 4 * g:FE + 4 * g + 4]))
                            if layer < 2:
                                m = MS[1][:, 4 * g:4 * g + 4, C:C + 1]
                                st.do(nv.tensor_copy(LROW[:, 1, 0:64].rearrange("p (h c) -> p h c", c=CH),
                                                     m.to_broadcast([P, 4, CH])))
                                st.do(nv.tensor_copy(LROW[:, 1, 64:68], m.rearrange("p h j -> p (h j)")))
                            else:
                                st.do(nv.memset(LROW[:, 1, :], 0.0))
                            st.do(nv.tensor_copy(LROW[:, 2, :], PASS[:, 0:1].to_broadcast([P, GR])))
                            st.wait()
                            nv.tensor_scalar(SM[:, 7, 0:1], PASS[:, 0:1], 1.0, None, ALU.mult).then_inc(c_rows, 1)
                            v.wait_ge(c_tp, g + 1)
                            st.then(nv.tensor_copy(CT[0:GR, :, :], CP[0:GR, 0:3 * P]
                                                   .rearrange("p (n q) -> p n q", n=3)))
                            st.then(nv.tensor_tensor_scan(CW[0:GR, 0, :], CT[0:GR, 2, :], CT[0:GR, 1, :], NEG,
                                                          ALU.add, ALU.max))
                            st.do(nv.memset(CW[0:GR, 1, 0:1], NEG))
                            st.do(tt(CW[0:GR, 1, 1:P], CW[0:GR, 0, 0:P - 1], CW[0:GR, 0, 1:P], ALU.subtract))
                            st.do(tt(CW[0:GR, 2, :], CT[0:GR, 1, :], CW[0:GR, 0, :], ALU.subtract))
                            st.wait()
                            tt(CW[0:GR, 1, :], CW[0:GR, 1, :], CT[0:GR, 2, :], ALU.add).then_inc(c_arg, 1)
                            v.wait_ge(c_exp, g + 1)
                            st.then(tt(CW[0:GR, 4, :], CT[0:GR, 0, :], CW[0:GR, 2, :], ALU.mult))
                            nv.tensor_tensor_scan(CW[0:GR, 3, :], CW[0:GR, 1, :], CW[0:GR, 4, :], 0.0, ALU.mult,
                                                  ALU.add).then_inc(c_sum, 1)
                            v.wait_ge(c_back, 2 * g + 2)
                            st.do(nv.tensor_copy(CROW[:, 64 * g:64 * g + 64], CB[:, 0:64]))
                            if has_weights:
                                st.do(nv.tensor_copy(CROW[:, FE + 4 * g:FE + 4 * g + 4], CB[:, 64:68]))
                            st.wait()
                            nv.tensor_copy(CROW[:, R + 4 * g:R + 4 * g + 4], CB[:, P:P + 64:CH])\
                                .then_inc(c_row, 1)
                        v.wait_ge(rows_in, 16 * K)
                        v.wait_ge(carry_in, 16 * K)
                        st.then(tt(MX[N, :, :], GN[N, :, R:WD], GC[N, :, R:WD], ALU.max))
                        st.then(tt(GN[N, :, R:WD], GN[N, :, R:WD], MX[N, :, :], ALU.subtract))
                        tt(GC[N, :, R:WD], GC[N, :, R:WD], MX[N, :, :], ALU.subtract).then_inc(merge_arg, 1)
                        v.wait_ge(merge_exp, 2)
                        for G in (GN, GC):
                            fac = G[N, :, R:WD]
                            st.do(tt(G[N, :, 0:FE].rearrange("p k (h c) -> p k h c", c=CH),
                                     G[N, :, 0:FE].rearrange("p k (h c) -> p k h c", c=CH),
                                     fac.unsqueeze(3).to_broadcast([NP, K, H, CH]), ALU.mult))
                            if has_weights:
                                st.do(tt(G[N, :, FE:R], G[N, :, FE:R], fac, ALU.mult))
                        st.wait()
                        st.then(tt(GN[N, :, 0:R], GN[N, :, 0:R], GC[N, :, 0:R], ALU.add))
                        st.then(tt(GN[N, :, 0:R], GN[N, :, 0:R],
                                   HAS[N, :].unsqueeze(2).to_broadcast([NP, K, R]), ALU.mult))
                        if has_weights:
                            st.then(nv.tensor_scalar(GN[N, :, FE:R], GN[N, :, FE:R], 1.0 if layer == 2 else 1e-16,
                                                     None, ALU.add))
                            st.then(nv.reciprocal(MX[N, :, :], GN[N, :, FE:R]))
                            agg = GN[N, :, 0:FE].rearrange("p k (h c) -> p k h c", c=CH)
                            st.then(tt(agg, agg, MX[N, :, :].unsqueeze(3).to_broadcast([NP, K, H, CH]), ALU.mult))
                        if project_agg:
                            nv.tensor_scalar(SM[N, 7, 0:1], PASS[N, 0:1], 1.0, None, ALU.mult)\
                                .then_inc(agg_ready, 1)
                            for u, (k0, m) in enumerate(units):
                                v.wait_ge(agg_mm, u + 1)
                                tt(Y[N, k0:k0 + m, :], PO[u % 2][N, 0:m * 64].rearrange("p (k n) -> p k n", k=m),
                                   KEEP[N, k0:k0 + m, :], ALU.add).then_inc(agg_add, 1)
                            v.wait_ge(agg_add, len(units))
                            if layer == 2:
                                st.then(tt(Y[N, :, :], Y[N, :, :], over_nodes(vec("bo")), ALU.add))
                        elif layer == 0:
                            st.then(tt(Y[N, :, :], GN[N, :, 0:64], over_nodes(vec("bias0")), ALU.add))
                        else:
                            st.then(tt(Y[N, :, :], GN[N, :, 0:64], over_nodes(vec("bias3")), ALU.add))
                            st.then(nv.scalar_tensor_tensor(out=Y[N, :, :], in0=Y[N, :, :], scalar=0.0,
                                                            in1=KEEP[N, :, :], op0=ALU.max, op1=ALU.add))

                        def layer_norm(x_ap, turn):
                            st.then(nv.tensor_reduce(SN[N, 0, :], x_ap, AX.X, ALU.add))
                            st.then(nv.tensor_scalar(SN[N, 1, :], SN[N, 0, :], 1.0 / 64, None, ALU.mult))
                            st.then(tt(SQ[N, :, :], x_ap, SN[N, 1, :].unsqueeze(2).to_broadcast([NP, K, 64]),
                                       ALU.subtract))
                            st.then(tt(GC[N, :, 0:64], SQ[N, :, :], SQ[N, :, :], ALU.mult))
                            st.then(nv.tensor_reduce(SN[N, 3, :], GC[N, :, 0:64], AX.X, ALU.add))
                            nv.tensor_scalar(SN[N, 2, :], SN[N, 3, :], 1.0 / 64, 1e-5, ALU.mult, ALU.add)\
                                .then_inc(ln_var, 1)
                            v.wait_ge(ln_sd, turn)
                            st.then(nv.reciprocal(SN[N, 4, :], SN[N, 2, :]))
                            return SN[N, 4, :].unsqueeze(2).to_broadcast([NP, K, 64])

                        if layer == 2:
                            rs = layer_norm(Y[N, :, :], 1)
                            st.then(tt(SQ[N, :, :], SQ[N, :, :], rs, ALU.mult))
                            st.then(tt(SQ[N, :, :], SQ[N, :, :], over_nodes(vec("gamma2")), ALU.mult))
                            st.then(tt(SQ[N, :, :], SQ[N, :, :], over_nodes(vec("beta2")), ALU.add))
                            st.then(tt(Y[N, :, :], Y[N, :, :], SQ[N, :, :], ALU.add))
                        else:
                            nv.tensor_reduce(SM[N, 0, :], Y[N, :, :].rearrange("p k f -> p f k"), AX.X, ALU.add)\
                                .then_inc(bn_part, 1)
                            v.wait_ge(bn_sum, 1)
                            st.then(nv.tensor_scalar(SM[:, 2, :], PB[:, 0:64], 1.0 / NODES, None, ALU.mult))
                            st.then(tt(Y[N, :, :], Y[N, :, :], over_nodes(SM[:, 2, :]), ALU.subtract))
                            st.then(tt(SQ[N, :, :], Y[N, :, :], Y[N, :, :], ALU.mult))
                            nv.tensor_reduce(SM[N, 1, :], SQ[N, :, :].rearrange("p k f -> p f k"), AX.X, ALU.add)\
                                .then_inc(bn_part, 1)
                            v.wait_ge(bn_sum, 2)
                            nv.tensor_scalar(SM[:, 3, :], PB[:, 64:128], 1.0 / NODES, 1e-5, ALU.mult, ALU.add)\
                                .then_inc(bn_var, 1)
                            v.wait_ge(bn_sd, 1)
                            st.then(nv.reciprocal(SM[:, 4, :], SM[:, 3, :]))
                            st.then(tt(SM[:, 5, :], SM[:, 4, :], vec(f"gamma{layer}"), ALU.mult))
                            st.then(tt(Y[N, :, :], Y[N, :, :], over_nodes(SM[:, 5, :]), ALU.mult))
                            st.then(tt(Y[N, :, :], Y[N, :, :], over_nodes(vec(f"beta{layer}")), ALU.add))
                        if layer == 0:
                            tt(Y[N, :, :], Y[N, :, :], X[N, :, :], ALU.add).then_inc(gelu_in, 1)
                            v.wait_ge(gelu_out, 1)
                        st.then(tt(Y[N, :, :], Y[N, :, :], X[N, :, :], ALU.add))
                        rs = layer_norm(Y[N, :, :], 2 if layer == 2 else 1)
                        tt(X[N, :, :], SQ[N, :, :], rs, ALU.mult).then_inc(done, 1)

        end_phase()
        project(wcol("W_l", "W_r"), 128, vec("b_l", 2), [(xl_tab, 0, 64), (xr_tab, 64, 64)], None, 64)
        end_phase()
        edges_0(src)
        end_phase()
        finish_layer(0)
        end_phase()
        project(wcol("Wq1", "W_self"), 192, vec("zero_q0", 3), [(q1_tab, 0, 128), (x1_tab, None, 64)], 128)
        end_phase()
        edges_1(src, dst_of_edges)
        end_phase()
        finish_layer(1)
        end_phase()
        project(wcol("Wk", "Wf"), 256, vec("bk", 4), [(kv_tab, 0, 128), (q2_tab, 128, 64)], 192,
                128)
        end_phase()
        edges_2(src)
        end_phase()
        finish_layer(2)
        end_phase()
        project_relations()
        end_phase()
        edges_3()
        end_phase()
        finish_layer(3)
        end_phase()


_VECS = ["L0_gnn_b_l", "L0_gnn_b_r", None, None, None, "L2_gnn_bk", "L2_gnn_bv", "L2_gnn_bq", "L2_gnn_bf",
         "L0_gnn_att", "L0_gnn_bias", "L0_gnn_gamma", "L0_gnn_beta", "L1_gnn_gamma", "L1_gnn_beta", "L2_gnn_bo",
         "L2_gnn_gamma", "L2_gnn_beta", "L3_gnn_bias", "L3_gnn_res_b", "L3_gnn_gamma", "L3_gnn_beta"]


def kernel(**inputs):
    import numpy as np
    import concourse.bacc as bacc
    from concourse.bass_utils import run_bass_kernel_spmd

    a = {k: np.asarray(v) for k, v in inputs.items()}
    f32 = np.float32

    def padded(v, rows):
        return np.concatenate([v, np.zeros((rows - v.shape[0],) + v.shape[1:], v.dtype)])

    dst = a["dst"].astype(np.int32)
    w64 = np.concatenate([a["L0_gnn_W_l"], a["L0_gnn_W_r"], a["L1_gnn_Wq"], a["L1_gnn_W_self"], a["L1_gnn_k_w1"],
                          a["L1_gnn_v_w1"], a["L2_gnn_Wk"], a["L2_gnn_Wv"], a["L2_gnn_Wq"], a["L2_gnn_Wf"],
                          a["L2_gnn_Wo"], a["L3_gnn_res_w"], a["L3_gnn_comp"]], axis=1)
    arrays = {
        "x": padded(a["x"], NPAD),
        "dst_shifted": np.concatenate([np.full(1, -1, np.int32), dst, np.full(EPAD - EDGES, NODES, np.int32)]),
        "src": padded(a["src"].astype(np.int32), EPAD).reshape(P, J),
        "ea16": padded(a["edge_attr_16"], EPAD),
        "ea64": padded(a["edge_attr_64"], EPAD),
        "ea9": padded(a["edge_attr_9"], EPAD),
        "etype": padded(a["edge_type_64"].astype(np.int32), EPAD).reshape(P, J),
        "ew": padded(a["edge_weight1"], EPAD).reshape(P, J),
        "w64": w64,
        "we": a["L0_gnn_W_e"],
        "cfix": np.concatenate([a["L1_gnn_Cqk"].transpose(1, 0, 2), a["L1_gnn_Cv"].transpose(1, 0, 2)], axis=2)
                .reshape(SH * 64, 256),
        "w2": np.concatenate([a["L1_gnn_k_w2"], a["L1_gnn_v_w2"]], axis=1),
        "b1": np.concatenate([a["L1_gnn_k_b1"], a["L1_gnn_v_b1"]]).reshape(P, 1),
        "b2": np.concatenate([a["L1_gnn_k_b2"], a["L1_gnn_v_b2"]]).reshape(1, 256),
        "wout": a["L1_gnn_W_out"],
        "vecs": np.concatenate([np.zeros(64, f32) if n is None else a[n].reshape(64) for n in _VECS])
                .reshape(1, V_ALL),
        "basis": a["L3_gnn_basis"],
    }
    nc = bacc.Bacc("TRN2", target_bir_lowering=False, num_devices=1)
    args = {}
    for name in arrays:
        arrays[name] = np.ascontiguousarray(arrays[name])
        args[name] = nc.dram_tensor(name, arrays[name].shape, mybir.dt.from_np(arrays[name].dtype),
                                    kind="ExternalInput").ap()
    out = nc.dram_tensor("out", (NODES, D), F32, kind="ExternalOutput").ap()
    graph_kernel(nc, out=out, **args)
    r = run_bass_kernel_spmd(nc, [arrays], core_ids=[0])
    return r.results[0]["out"]
```

```python
import concourse.bass as bass
from concourse import mybir
from contextlib import ExitStack

F32 = mybir.dt.float32
I32 = mybir.dt.int32
BF16 = mybir.dt.bfloat16
F32R = mybir.dt.float32r
ALU = mybir.AluOpType
ACT = mybir.ActivationFunctionType
AX = mybir.AxisListType

NODES, EDGES, D = 3125, 100000, 64
P = 128
K = 25
NP = NODES // K
NPAD = P * K
C = 8
J = 784
NCH = J // C
EPAD = P * J
RELS = 64
SH = 9
CH = 16
HEADS = [4, 8, 4, 4]
SUMS = [68, 136, 68, 64]
ROW = [s + h for s, h in zip(SUMS, HEADS)]
NEG = -1.0e30
GROUPS = [(k, min(4, K - k)) for k in range(0, K, 4)]
assert NP * K == NODES and NCH % 2 == 0 and EPAD >= EDGES

W_COLS = {}
_at = 0
for _n, _w in (("W_l", 64), ("W_r", 64), ("Wq1", 128), ("W_self", 64), ("k_w1", 64), ("v_w1", 64), ("Wk", 64),
               ("Wv", 64), ("Wq2", 64), ("Wf", 64), ("Wo", 64), ("res_w", 64), ("comp", 64)):
    W_COLS[_n] = (_at, _at + _w)
    _at += _w
W_ALL = _at
V_NAMES = ["b_l", "b_r", "zero_q0", "zero_q1", "zero_s", "bk", "bv", "bq", "bf", "att", "bias0", "gamma0", "beta0",
           "gamma1", "beta1", "bo", "gamma2", "beta2", "bias3", "res_b", "gamma3", "beta3"]
V_AT = {n: i * 64 for i, n in enumerate(V_NAMES)}
V_ALL = 64 * len(V_NAMES)


def graph_kernel(nc, x, dst_shifted, src, ea16, ea64, ea9, etype, ew, w64, we, cfix, w2, b1, b2, wout, vecs, basis,
                 out):
    scratch = {}

    def dram(name, shape, dt=F32):
        scratch[name] = nc.dram_tensor(name, shape, dt, kind="Internal").ap()
        return scratch[name]

    xl_tab, xr_tab = dram("xl_tab", [NPAD, 64]), dram("xr_tab", [NPAD, 64])
    x1_tab, q1_tab = dram("x1_tab", [NPAD, 64]), dram("q1_tab", [NPAD, 128])
    kv_tab, q2_tab = dram("kv_tab", [NPAD, 128]), dram("q2_tab", [NPAD, 64])
    rel_tab = dram("rel_tab", [NPAD * RELS, 64])
    scan_tabs = [dram(f"scan{l}", [EPAD, ROW[l]]) for l in range(4)]
    carry_tabs = [dram(f"carry{l}", [NPAD, ROW[l]]) for l in range(4)]
    relidx = dram("relidx", [P, J], I32)
    spread = dram("spread", [EPAD, 64])
    dst_of_edges = dst_shifted[1:1 + EPAD].rearrange("(p j) -> p j", j=J)

    uses = {}

    def unique(name):
        uses[name] = uses.get(name, 0) + 1
        return name if uses[name] == 1 else f"{name}_{uses[name]}"

    top = ExitStack()
    with top:
        def sb(name, shape, dt=F32, ctx=top):
            return ctx.enter_context(nc.sbuf_tensor(unique(name), shape, dt))

        X = sb("X", [P, K, D])
        KEEP = sb("KEEP", [P, K, 64])
        W = sb("W", [64, W_ALL])
        VEC = sb("VEC", [P, V_ALL])
        WO_T = sb("WO_T", [P, 64])
        RESW_T = sb("RESW_T", [64, 64])
        COMP_T = sb("COMP_T", [64, 64])
        IDENT = sb("IDENT", [P, P])
        ONES = sb("ONES", [P, P])
        SAME = sb("SAME", [P, J])
        BREAK = sb("BREAK", [P, J])
        HAS = sb("HAS", [P, K])
        END_AT = sb("END_AT", [P, K], I32)
        START_AT = sb("START_AT", [P, K], I32)
        FIRST_DST = sb("FIRST_DST", [P, 1], I32)
        CARRY_AT = sb("CARRY_AT", [P, 1], I32)
        PASS = sb("PASS", [P, 1])
        SC = [sb(f"SC{b}", [P, 136, 1 + C]) for b in range(2)]
        MS = [sb(f"MS{b}", [P, 8, 1 + C]) for b in range(2)]

        parked = top.enter_context(nc.semaphore("parked"))

        open_semaphores = []

        def end_phase():
            nc.clear_and_free_semaphores(list(open_semaphores))
            open_semaphores.clear()
            nc.all_engine_barrier()

        def phase_semaphore(name):
            sem = nc.alloc_semaphore(unique(name))
            open_semaphores.append(sem)
            return sem

        def vec(name, n=1):
            return VEC[:, V_AT[name]:V_AT[name] + 64 * n]

        def wcol(a, b=None):
            return W[:, W_COLS[a][0]:W_COLS[b or a][1]]

        def over_nodes(v, n=NP):
            return v[0:n, :].unsqueeze(1).to_broadcast([n, K, v.shape[1]])

        class Steps:

            def __init__(self, eng, sem, base=0):
                self.eng, self.sem, self.base, self.n = eng, sem, base, 0

            def do(self, ins):
                ins.then_inc(self.sem, 1)
                self.n += 1
                return ins

            def wait(self, back=0):
                self.eng.wait_ge(self.sem, self.base + (self.n - back))

            def then(self, ins):
                self.do(ins)
                self.wait()

        def chunks(eng, step, peeled=2):
            for t in range(peeled):
                step(t, t // 2, t % 2, t == 0, False)
            with eng.Fori(peeled // 2, NCH // 2 - 1) as n:
                step(n * 2, n, 0, False, False)
                step(n * 2 + 1, n, 1, False, False)
            step(NCH - 2, NCH // 2 - 1, 0, False, False)
            step(NCH - 1, NCH // 2 - 1, 1, False, True)

        def wait(eng, sem, value):
            if not isinstance(value, int) or value > 0:
                eng.wait_ge(sem, value)
                if eng is nc.sync and not isinstance(value, int):
                    eng.sem_inc(parked, 1)

        SEGS = 2 * P
        SEG = EPAD // SEGS
        KT = K + 1
        NULL = sb("NULL", [P, sum(ROW)], F32)
        blanks = ExitStack()
        ZERO = sb("ZERO", [P, 14 * 64], F32, blanks)
        BLANKS = J // 56
        spread_zeroed = top.enter_context(nc.semaphore("spread_zeroed"))
        carries_nulled = top.enter_context(nc.semaphore("carries_nulled"))
        segments = dst_shifted[0:EPAD].rearrange("(q s) -> q s", s=SEG)
        with ExitStack() as ctx:
            def s(name):
                return phase_semaphore(name)

            DSTX = sb("DSTX", [P, 2, J], I32, ctx)
            NEXT = sb("NEXT", [P, 2], I32, ctx)
            TYPES = sb("TYPES", [P, 2, J], I32, ctx)
            RIDX = sb("RIDX", [P, J], I32, ctx)
            TH = sb("TH", [P, KT], I32, ctx)
            FIRSTS = sb("FIRSTS", [P, 2], F32, ctx)
            FD = sb("FD", [P, P, 2], F32, ctx)
            CMP = sb("CMP", [P, SEGS * 13], F32, ctx)
            AT_SEG = sb("AT_SEG", [P, KT], I32, ctx)
            GS = sb("GS", [P, KT, SEG], I32, ctx)
            ST = sb("ST", [P, 6, KT], F32, ctx)
            FB = ctx.enter_context(nc.psum_tensor(unique("FB"), [P, 512], F32))
            PR = [ctx.enter_context(nc.psum_tensor(unique(f"PR{b}"), [P, 512], F32)) for b in range(2)]
            loaded, dst_in, types_in = s("loaded"), s("dst_in"), s("types_in")
            consts, dve, diagonal, firsts_out = s("consts"), s("dve"), s("diagonal"), s("firsts_out")
            seg_known, ridx_ready, ridx_out = s("seg_known"), s("ridx_ready"), s("ridx_out")
            PARTS = [(0, 7), (7, 13), (13, 20), (20, KT)]
            seg_in = [s(f"seg_in{i}") for i in range(len(PARTS))]
            zeroed, nulled = s("zeroed"), s("nulled")
            tposed, t_copied = s("tposed"), s("t_copied")
            with nc.Block() as block:
                @block.sync
                def _(sp):
                    sp.dma_start(DSTX[:, 0, :], dst_shifted[1:1 + EPAD].rearrange("(p j) -> p j", j=J))\
                      .then_inc(dst_in, 16)
                    sp.dma_start(DSTX[:, 1, :], dst_shifted[0:EPAD].rearrange("(p j) -> p j", j=J))\
                      .then_inc(dst_in, 16)
                    sp.dma_start(NEXT[:, :], dst_shifted[1 + J:1 + J + EPAD].rearrange("(p j) -> p j", j=J)[:, 0:2])\
                      .then_inc(dst_in, 16)
                    sp.dma_start(W[:, :], w64).then_inc(loaded, 16)
                    sp.dma_start(TYPES[:, 0, :], src).then_inc(types_in, 16)
                    sp.dma_start(TYPES[:, 1, :], etype).then_inc(types_in, 16)
                    sp.dma_start(X[:, :, :], x.rearrange("(p k) f -> p k f", k=K)).then_inc(loaded, 16)
                    sp.dma_start(VEC[:, :], vecs.to_broadcast([P, V_ALL])).then_inc(loaded, 16)
                    sp.dma_start(WO_T[:, :], wout).then_inc(loaded, 16)
                    sp.wait_ge(zeroed, 1)

                    def blank_spread(pieces):
                        for a in pieces:
                            sp.dma_start(spread.rearrange("(p a m) f -> p a (m f)", a=BLANKS, m=56)[:, a, :]
                                         .rearrange("p (r f) -> p r f", r=4),
                                         ZERO[:, :].unsqueeze(1).to_broadcast([P, 4, 14 * 64]))\
                              .then_inc(spread_zeroed, 16)

                    blank_spread(range(3))
                    for part, (k0, k1) in enumerate(PARTS):
                        sp.wait_ge(seg_in[part], 16 * (k1 - k0))
                        blank_spread(range(3 + 2 * part, 5 + 2 * part))
                    blank_spread(range(3 + 2 * len(PARTS), BLANKS))
                    sp.wait_ge(nulled, 8)
                    for l in range(4):
                        sp.dma_start(carry_tabs[l].rearrange("(p k) f -> p k f", k=K),
                                     NULL[:, sum(ROW[:l]):sum(ROW[:l + 1])].unsqueeze(1)
                                     .to_broadcast([P, K, ROW[l]])).then_inc(carries_nulled, 16)
                    sp.wait_ge(ridx_ready, 1)
                    sp.dma_start(relidx, RIDX[:, :]).then_inc(ridx_out, 16)
                    sp.wait_ge(ridx_out, 16)
                    sp.wait_ge(loaded, 64)

                @block.gpsimd
                def _(pool):
                    nc.gpsimd.memset(ONES[:, :], 1.0).then_inc(consts, 1)
                    nc.gpsimd.memset(IDENT[:, :], 0.0).then_inc(consts, 1)
                    nc.gpsimd.iota(TH[:, :], [[1, KT]], base=0, channel_multiplier=K).then_inc(consts, 1)
                    pool.wait_ge(consts, 3)
                    nc.gpsimd.affine_select(out=IDENT[:, :], in_=IDENT[:, :], compare_op=ALU.not_equal, fill=1.0,
                                            base=0, pattern=[[-1, P]], channel_multiplier=1).then_inc(consts, 1)
                    nc.gpsimd.memset(ZERO[:, :], 0.0).then_inc(zeroed, 1)
                    for l in range(4):
                        at = sum(ROW[:l])
                        nc.gpsimd.memset(NULL[:, at:at + SUMS[l]], 0.0).then_inc(nulled, 1)
                        nc.gpsimd.memset(NULL[:, at + SUMS[l]:at + ROW[l]], NEG).then_inc(nulled, 1)
                    for part, (k0, k1) in enumerate(PARTS):
                        pool.wait_ge(seg_known, part // 2 + 1)
                        for k in range(k0, k1):
                            pool.indirect_dma_start(
                                out=GS[:, k, :], out_offset=None, in_=segments,
                                in_offset=bass.IndirectOffsetOnAxis(ap=AT_SEG[:, k:k + 1], axis=0),
                            ).then_inc(seg_in[part], 16)

                @block.vector
                def _(v):
                    st = Steps(v, dve)
                    v.wait_ge(dst_in, 48)
                    st.then(nc.vector.tensor_copy(FIRSTS[:, :],
                                                  DSTX[:, 1, :].rearrange("p (c s) -> p c s", s=SEG)[:, :, 0]))
                    v.wait_ge(consts, 4)
                    nc.vector.tensor_tensor(FD[:, :, :], IDENT[:, :].unsqueeze(2).to_broadcast([P, P, 2]),
                                            FIRSTS[:, :].unsqueeze(1).to_broadcast([P, P, 2]), ALU.mult)\
                      .then_inc(diagonal, 1)
                    v.wait_ge(firsts_out, 1)
                    for half in range(2):
                        ks = slice(13 * half, 13 * half + 13)
                        below = CMP[:, 0:13 * SEGS].rearrange("p (k q) -> p k q", q=SEGS)
                        st.then(nc.vector.tensor_tensor(below,
                                                        FB[:, 0:SEGS].unsqueeze(1).to_broadcast([P, 13, SEGS]),
                                                        TH[:, ks].unsqueeze(2).to_broadcast([P, 13, SEGS]),
                                                        ALU.is_lt))
                        st.then(nc.vector.tensor_reduce(ST[:, 0, ks], below, AX.X, ALU.add))
                        nc.vector.tensor_scalar(AT_SEG[:, ks], ST[:, 0, ks], -1.0, None, ALU.add)\
                          .then_inc(seg_known, 1)
                    st.do(nc.vector.tensor_tensor(SAME[:, :], DSTX[:, 0, :], DSTX[:, 1, :], ALU.is_equal))
                    st.do(nc.vector.tensor_tensor(ST[:, 5, 0:1], DSTX[:, 0, 0:1], DSTX[:, 0, J - 1:J],
                                                  ALU.is_equal))
                    st.wait()
                    st.do(nc.vector.tensor_scalar(BREAK[:, :], SAME[:, :], -1.0, -NEG, ALU.add, ALU.mult))
                    st.then(nc.vector.tensor_tensor(ST[:, 5, 0:1], ST[:, 5, 0:1], SAME[:, 0:1], ALU.mult))
                    st.do(nc.vector.tensor_scalar(PASS[:, :], ST[:, 5, 0:1], -1.0, -NEG, ALU.add, ALU.mult))
                    v.wait_ge(types_in, 32)
                    nc.vector.scalar_tensor_tensor(out=RIDX[:, :], in0=TYPES[:, 0, :], scalar=float(RELS),
                                                   in1=TYPES[:, 1, :], op0=ALU.mult, op1=ALU.add)\
                      .then_inc(ridx_ready, 1)
                    for part, (k0, k1) in enumerate(PARTS):
                        v.wait_ge(seg_in[part], 16 * (k1 - k0))
                        below = CMP[:, 0:(k1 - k0) * SEG].rearrange("p (k q) -> p k q", q=SEG)
                        st.then(nc.vector.tensor_tensor(below, GS[:, k0:k1, :],
                                                        TH[:, k0:k1].unsqueeze(2).to_broadcast([P, k1 - k0, SEG]),
                                                        ALU.is_lt))
                        st.then(nc.vector.tensor_reduce(ST[:, 1, k0:k1], below, AX.X, ALU.add))
                    st.then(nc.vector.scalar_tensor_tensor(out=ST[:, 2, :], in0=ST[:, 0, :], scalar=float(SEG),
                                                           in1=ST[:, 1, :], op0=ALU.mult, op1=ALU.add))
                    st.do(nc.vector.tensor_tensor(HAS[:, :], ST[:, 2, 1:KT], ST[:, 2, 0:K], ALU.is_gt))
                    st.do(nc.vector.tensor_scalar(END_AT[:, :], ST[:, 2, 1:KT], -float(SEG + 2), 0.0, ALU.add,
                                                  ALU.max))
                    st.do(nc.vector.tensor_copy(FIRST_DST[:, :], DSTX[:, 0, 0:1]))
                    st.wait()
                    st.then(nc.vector.scalar_tensor_tensor(out=ST[:, 3, 0:K], in0=ST[:, 2, 0:K],
                                                           scalar=-float(EPAD + SEG + 1), in1=HAS[:, :],
                                                           op0=ALU.add, op1=ALU.mult))
                    st.do(nc.vector.tensor_scalar(START_AT[:, :], ST[:, 3, 0:K], float(EPAD), None, ALU.add))
                    st.then(nc.vector.tensor_tensor(ST[:, 4, 0:1], DSTX[:, 0, 0:1], NEXT[:, 0:1], ALU.not_equal))
                    st.then(nc.vector.tensor_tensor(ST[:, 4, 1:2], ST[:, 4, 0:1], SAME[:, 0:1], ALU.mult))
                    st.then(nc.vector.scalar_tensor_tensor(out=ST[:, 4, 2:3], in0=DSTX[:, 0, 0:1],
                                                           scalar=-float(NPAD), in1=ST[:, 4, 1:2], op0=ALU.add,
                                                           op1=ALU.mult))
                    st.then(nc.vector.tensor_scalar(CARRY_AT[:, :], ST[:, 4, 2:3], float(NPAD), None, ALU.add))
                    for n in range(2):
                        v.wait_ge(tposed, n + 1)
                        nc.vector.tensor_copy((RESW_T, COMP_T)[n][:, :], PR[n][0:64, 0:64]).then_inc(t_copied, 1)

                @block.tensor
                def _(pe):
                    pe.wait_ge(diagonal, 1)
                    nc.tensor.matmul(FB[:, 0:SEGS], ONES[:, :], FD[:, :, :].rearrange("p q c -> p (q c)"),
                                     start=True, stop=True).then_inc(firsts_out, 1)
                    pe.wait_ge(loaded, 64)
                    nc.tensor.transpose(PR[0][0:64, 0:64], wcol("res_w"), IDENT[0:64, 0:64]).then_inc(tposed, 1)
                    nc.tensor.transpose(PR[1][0:64, 0:64], wcol("comp"), IDENT[0:64, 0:64]).then_inc(tposed, 1)

        def project(weights, n_out, biases, tables, keep, spread_at=None):
            per = 512 // n_out
            units = [(k, min(per, K - k)) for k in range(0, K, per)]
            with ExitStack() as ctx:
                def s(name):
                    return phase_semaphore(name)

                XT = sb("XT", [64, NPAD], F32, ctx)
                TAB = sb("TAB", [P, K, n_out], F32, ctx)
                PT = [ctx.enter_context(nc.psum_tensor(unique(f"PT{b}"), [P, 512], F32)) for b in range(2)]
                PO = [ctx.enter_context(nc.psum_tensor(unique(f"PO{b}"), [P, 512], F32)) for b in range(4)]
                scattered = s("scattered")
                t_done, t_copied, m_done, m_copied, stored = (s("t_done"), s("t_copied"), s("m_done"),
                                                              s("m_copied"), s("stored"))
                with nc.Block() as block:
                    @block.tensor
                    def _(pe):
                        for g, (k0, m) in enumerate(GROUPS):
                            if g >= 2:
                                pe.wait_ge(t_copied, g - 1)
                            for c in range(m):
                                last = nc.tensor.transpose(PT[g % 2][0:64, c * P:(c + 1) * P], X[:, k0 + c, :],
                                                           IDENT[:, :])
                            last.then_inc(t_done, 1)
                        for u, (k0, m) in enumerate(units):
                            pe.wait_ge(t_copied, min((k0 + m - 1) // 4 + 1, len(GROUPS)))
                            if u >= 4:
                                pe.wait_ge(m_copied, u - 3)
                            for c in range(m):
                                last = nc.tensor.matmul(PO[u % 4][:, c * n_out:(c + 1) * n_out],
                                                        XT[:, (k0 + c) * P:(k0 + c + 1) * P], weights,
                                                        start=True, stop=True)
                            last.then_inc(m_done, 1)

                    @block.scalar
                    def _(act):
                        for g, (k0, m) in enumerate(GROUPS):
                            act.wait_ge(t_done, g + 1)
                            nc.scalar.activation(XT[:, k0 * P:(k0 + m) * P], PT[g % 2][0:64, 0:m * P], ACT.Copy)\
                              .then_inc(t_copied, 1)

                    @block.vector
                    def _(v):
                        for u, (k0, m) in enumerate(units):
                            v.wait_ge(m_done, u + 1)
                            nc.vector.tensor_tensor(
                                TAB[:, k0:k0 + m, :],
                                PO[u % 4][:, 0:m * n_out].rearrange("p (k n) -> p k n", k=m),
                                biases.unsqueeze(1).to_broadcast([P, m, n_out]), ALU.add).then_inc(m_copied, 1)
                        if keep is not None:
                            v.wait_ge(m_copied, len(units))
                            nc.vector.tensor_copy(KEEP[:, :, :], TAB[:, :, keep:keep + 64])\
                              .then_inc(m_copied, 1)

                    @block.gpsimd
                    def _(pool):
                        if spread_at is not None:
                            pool.wait_ge(spread_zeroed, 16 * BLANKS)
                            for k in range(K):
                                pool.wait_ge(m_copied, k // per + 1)
                                pool.indirect_dma_start(
                                    out=spread, in_=TAB[0:NP, k, spread_at:spread_at + 64], in_offset=None,
                                    out_offset=bass.IndirectOffsetOnAxis(ap=START_AT[0:NP, k:k + 1], axis=0),
                                    bounds_check=EPAD - 1, oob_is_err=False).then_inc(scattered, 16)
                            pool.wait_ge(scattered, 16 * K)

                    @block.sync
                    def _(sp):
                        for tab, at, width in tables:
                            if at is None:
                                sp.dma_start(tab.rearrange("(p k) f -> p k f", k=K), X[:, :, :])\
                                  .then_inc(stored, 16)
                        made = [(tab, at, width) for tab, at, width in tables if at is not None]
                        k0 = 0
                        for ready in (len(units) // 2, len(units)):
                            sp.wait_ge(m_copied, ready)
                            k1 = min(ready * per, K)
                            for tab, at, width in made:
                                sp.dma_start(tab.rearrange("(p k) f -> p k f", k=K)[:, k0:k1, :],
                                             TAB[:, k0:k1, at:at + width]).then_inc(stored, 16)
                            k0 = k1
                        sp.wait_ge(stored, 16 * (len(tables) + len(made)))
                        sp.wait_ge(spread_zeroed, 16 * BLANKS)

        def project_relations():
            with ExitStack() as ctx:
                def s(name):
                    return phase_semaphore(name)

                XT = sb("XT", [64, NPAD], F32, ctx)
                XT2 = sb("XT2", [P, NPAD], F32R, ctx)
                XX = sb("XX", [P, K, 2, 64], F32, ctx)
                BASIS = sb("BASIS", [64, P, 64], F32, ctx)
                doubled = s("doubled")
                WHI = sb("WHI", [P, RELS, 64], F32R, ctx)
                WLO = sb("WLO", [P, RELS, 64], F32R, ctx)
                YS = [sb(f"YS{b}", [P, RELS * 64], F32, ctx) for b in range(2)]
                PT = [ctx.enter_context(nc.psum_tensor(unique(f"PT{b}"), [P, 512], F32)) for b in range(2)]
                PO = [ctx.enter_context(nc.psum_tensor(unique(f"PO{b}"), [P, 512], F32)) for b in range(6)]
                t_done, t_copied, t_split, m_done = s("t_done"), s("t_copied"), s("t_split"), s("m_done")
                act_copied, dve_copied = s("act_copied"), s("dve_copied")
                stored = [s("stored0"), s("stored1")]
                res_done, res_copied = s("res_done"), s("res_copied")
                basis_in, rel_w, rel_hi, rel_lo = s("basis_in"), s("rel_w"), s("rel_hi"), s("rel_lo")
                rel_v = rel_tab.rearrange("(p k r) f -> k p (r f)", k=K, r=RELS)
                whi, wlo = (w[:, :, :].rearrange("i r o -> i (r o)") for w in (WHI, WLO))

                def by_relation(bank):
                    return bank[:, :].rearrange("i (o r) -> i r o", o=8)

                with nc.Block() as block:
                    @block.gpsimd
                    def _(pool):
                        for a in range(2):
                            nc.gpsimd.tensor_copy(XX[:, :, a, :], X[:, :, :]).then_inc(doubled, 1)

                    @block.tensor
                    def _(pe):
                        pe.wait_ge(doubled, 2)
                        for g, (k0, m) in enumerate(GROUPS):
                            if g >= 2:
                                pe.wait_ge(t_split, g - 1)
                                pe.wait_ge(t_copied, 2 * g - 2)
                            for c in range(m):
                                last = nc.tensor.transpose(
                                    PT[g % 2][:, c * P:(c + 1) * P],
                                    XX[:, k0 + c, :, :].rearrange("p a f -> p (a f)"), IDENT[:, :])
                            last.then_inc(t_done, 1)
                        pe.wait_ge(basis_in, 32)
                        for g in range(8):
                            if g >= 4:
                                pe.wait_ge(rel_lo, g - 3)
                            for o in range(8):
                                last = nc.tensor.matmul(
                                    PO[g % 4][:, o * 64:o * 64 + 64],
                                    BASIS[:, :, 8 * g + o], COMP_T[:, :],
                                    start=True, stop=True)
                            last.then_inc(rel_w, 1)
                        pe.wait_ge(t_split, len(GROUPS))
                        for r in range(4):
                            ks = range(8 * r, min(8 * r + 8, K))
                            if r >= 2:
                                pe.wait_ge(res_copied, r - 1)
                            for c, k in enumerate(ks):
                                last = nc.tensor.matmul(PT[r % 2][:, c * 64:c * 64 + 64], XT[:, k * P:(k + 1) * P],
                                                        RESW_T[:, :], start=True, stop=True)
                            last.then_inc(res_done, 1)
                        pe.wait_ge(rel_lo, 8)
                        for u in range(K * 8):
                            k, g = u // 8, u % 8
                            if u >= 6:
                                w = u - 6
                                pe.wait_ge(act_copied if w % 2 == 0 else dve_copied, w // 2 + 1)
                            for n, w in enumerate((whi, wlo)):
                                last = nc.tensor.matmul(PO[u % 6][:, :], XT2[:, k * P:(k + 1) * P],
                                                        w[:, g * 512:(g + 1) * 512], start=(n == 0), stop=(n == 1))
                            last.then_inc(m_done, 1)

                    @block.scalar
                    def _(act):
                        for g, (k0, m) in enumerate(GROUPS):
                            act.wait_ge(t_done, g + 1)
                            nc.scalar.activation(XT[:, k0 * P:(k0 + m) * P], PT[g % 2][0:64, 0:m * P], ACT.Copy)\
                              .then_inc(t_copied, 1)
                            nc.scalar.activation(XT2[:, k0 * P:(k0 + m) * P], PT[g % 2][:, 0:m * P], ACT.Copy)\
                              .then_inc(t_copied, 1)
                        for g in range(8):
                            act.wait_ge(rel_w, g + 1)
                            nc.scalar.activation(WHI[:, :, 8 * g:8 * g + 8], by_relation(PO[g % 4]), ACT.Copy)\
                              .then_inc(rel_hi, 1)
                        for u in range(0, K * 8, 2):
                            k, g = u // 8, u % 8
                            act.wait_ge(m_done, u + 1)
                            if k >= 2 and g == 0:
                                act.wait_ge(stored[k % 2], 16 * (k // 2))
                            nc.scalar.activation(YS[k % 2][:, g * 512:(g + 1) * 512], PO[u % 6][:, :], ACT.Copy)\
                              .then_inc(act_copied, 1)

                    @block.vector
                    def _(v):
                        for g, (k0, m) in enumerate(GROUPS):
                            v.wait_ge(t_copied, 2 * g + 2)
                            lo = XT2[64:128, k0 * P:(k0 + m) * P]
                            nc.vector.tensor_tensor(lo, PT[g % 2][64:128, 0:m * P], lo.bitcast(F32),
                                                    ALU.subtract).then_inc(t_split, 1)
                        for g in range(8):
                            v.wait_ge(rel_hi, g + 1)
                            nc.vector.tensor_tensor(WLO[:, :, 8 * g:8 * g + 8], by_relation(PO[g % 4]),
                                                    WHI[:, :, 8 * g:8 * g + 8].bitcast(F32),
                                                    ALU.subtract).then_inc(rel_lo, 1)
                        for r in range(4):
                            m = min(8 * r + 8, K) - 8 * r
                            v.wait_ge(res_done, r + 1)
                            nc.vector.tensor_tensor(
                                KEEP[:, 8 * r:8 * r + m, :], PT[r % 2][:, 0:m * 64].rearrange("p (k n) -> p k n", k=m),
                                vec("res_b").unsqueeze(1).to_broadcast([P, m, 64]), ALU.add).then_inc(res_copied, 1)
                        v.wait_ge(res_copied, 4)
                        nc.vector.tensor_scalar(KEEP[:, :, :], KEEP[:, :, :], 0.0, None, ALU.max)\
                          .then_inc(res_copied, 1)
                        for u in range(1, K * 8, 2):
                            k, g = u // 8, u % 8
                            v.wait_ge(m_done, u + 1)
                            if k >= 2 and g == 1:
                                v.wait_ge(stored[k % 2], 16 * (k // 2))
                            nc.vector.tensor_copy(YS[k % 2][:, g * 512:(g + 1) * 512], PO[u % 6][:, :])\
                              .then_inc(dve_copied, 1)

                    @block.sync
                    def _(sp):
                        for a in range(2):
                            sp.dma_start(BASIS[:, 64 * a:64 * a + 64, :], basis).then_inc(basis_in, 16)
                        for k in range(K):
                            sp.wait_ge(act_copied, 4 * k + 4)
                            sp.wait_ge(dve_copied, 4 * k + 4)
                            sp.dma_start(rel_v[k, :, :], YS[k % 2][:, :]).then_inc(stored[k % 2], 16)
                        sp.wait_ge(stored[0], 16 * ((K + 1) // 2))
                        sp.wait_ge(stored[1], 16 * (K // 2))

        def row_view(tab, t):
            return tab.rearrange("(p j) f -> p j f", j=J)[:, bass.ds(t * C, C), :]

        def before(n, b):
            return n - (1 - b)

        class Edges:

            def __init__(self, ctx, layer, tables, indices):
                self.layer, self.tables, self.indices = layer, tables, indices
                self.H, self.R = HEADS[layer], SUMS[layer]
                self.FE = self.H * CH
                self.weights = self.R > self.FE
                self.running_max = layer < 2
                self.ctx = ctx
                self.N_READY = 9 if layer == 0 else 7
                H, R = self.H, self.R
                self.IDX = {n: self.pair(f"IDX_{n}", [P, C], I32) for n in indices}
                self.G = [self.pair(f"G{g}", [P, C, w]) for g, (_, w, _) in enumerate(tables)]
                self.MSG = sb("MSG", [P, R, 1 + C], F32, ctx)
                self.DEC = self.pair("DEC", [P, R, 1 + C])
                self.OUT = self.pair("OUT", [P, C, R + H])
                self.EX = self.pair("EX", [P, 2, H, C])
                self.ARG = sb("ARG", [P, 2, H, C], F32, ctx)
                self.LG = sb("LG", [P, H, 1 + C], F32, ctx)
                self.BR = sb("BR", [P, H, 1 + C], F32, ctx)
                self.T1 = sb("T1", [P, C, self.FE], F32, ctx)
                self.idx_in, self.attr_in, self.stored = (
                    [self.sem(f"{name}{b}") for b in range(2)] for name in ("idx_in", "attr_in", "stored"))
                self.rows_in = [[self.sem(f"rows{g}_in{b}") for b in range(2)] for g in range(len(tables))]
                self.ready, self.a_steps, self.b_steps = self.sem("ready"), self.sem("a_steps"), self.sem("b_steps")
                self.args_ready, self.exps_ready = self.sem("args_ready"), self.sem("exps_ready")
                self.decays_ready, self.scanned = self.sem("decays_ready"), self.sem("scanned")
                self.copied_out = self.sem("copied_out")
                if layer in (0, 2):
                    self.RAW = self.pair("RAW", [P, C, 64])
                    self.XI = self.pair("XI", [P, 64, 1 + C])
                    self.XE = self.pair("XE", [P, 64, 1 + C])
                    self.HOLD = self.pair("HOLD", [P, 64, 1 + C]) if layer == 0 else self.DEC
                    self.FIRST = sb("FIRST", [P, 64], F32, ctx)
                    self.raw_in = [self.sem(f"raw_in{b}") for b in range(2)]
                    self.raw_turned, self.held, self.expanded = (self.sem("raw_turned"), self.sem("held"),
                                                                 self.sem("expanded"))
                    self.x_steps, self.first_in = self.sem("x_steps"), self.sem("first_in")

            def sem(self, name):
                return phase_semaphore(name)

            def pair(self, name, shape, dt=F32):
                return [sb(f"{name}{b}", shape, dt, self.ctx) for b in range(2)]

            def bank(self, name):
                return self.ctx.enter_context(nc.psum_tensor(unique(name), [P, 512], F32))

            def constants(self):
                fills = [(SC[1][:, :, :], 0.0), (MS[1][:, :, :], NEG), (self.BR[:, :, :], NEG)]
                fills += [(self.DEC[b][:, :, :], 0.0) for b in range(2)]
                if self.layer == 0:
                    fills += [(self.HOLD[b][:, :, :], 0.0) for b in range(2)]
                fills += [(self.OUT[b][:, :, self.R:], 0.0) for b in range(2)]
                for ap, value in fills:
                    nc.gpsimd.memset(ap, value).then_inc(self.ready, 1)
                assert len(fills) == self.N_READY, len(fills)

            def first_rows(self, pool, table):
                pool.indirect_dma_start(out=self.FIRST[:, :], out_offset=None, in_=table,
                                        in_offset=bass.IndirectOffsetOnAxis(ap=FIRST_DST[:, 0:1], axis=0))\
                    .then_inc(self.first_in, 16)

            def load_spread(self, sp, t, n, b, first):
                if not first:
                    wait(sp, self.raw_turned, t - 1)
                sp.dma_start(self.RAW[b][:, :, :], row_view(spread, t)).then_inc(self.raw_in[b], 16)

            def turn(self, act, t, n, b, first):
                wait(act, self.raw_in[b], (n + 1) * 16)
                if not first:
                    wait(act, self.expanded, t - 1)
                nc.scalar.activation(self.XI[b][:, :, 1:1 + C], self.RAW[b][:, :, :].rearrange("p j f -> p f j"),
                                     ACT.Copy).then_inc(self.raw_turned, 1)
                if self.layer == 2:
                    self.same_factors(act, t, b, first)
                else:
                    act.sem_inc(parked, 1)
                    nc.scalar.activation(self.HOLD[b][:, :, 1:1 + C],
                                         SAME[:, bass.ds(t * C, C)].unsqueeze(1).to_broadcast([P, 64, C]),
                                         ACT.Copy).then_inc(self.held, 1)

            def expand(self, v, t, n, b, first):
                st = Steps(v, self.x_steps, t)
                if first:
                    wait(v, self.first_in, 16)
                    before_ = self.FIRST[:, :].unsqueeze(2)
                else:
                    before_ = self.XE[1 - b][:, :, C:C + 1]
                st.do(nc.vector.tensor_copy(self.XI[b][:, :, 0:1], before_))
                st.wait()
                wait(v, self.raw_turned, t + 1)
                if self.layer == 2:
                    wait(v, self.decays_ready, t + 1)
                else:
                    wait(v, self.held, t + 1)
                flat = lambda ap: ap.rearrange("p f j -> p (f j)")
                nc.vector.tensor_tensor_scan(flat(self.XE[b][:, :, :]), flat(self.HOLD[b][:, 0:64, :]),
                                             flat(self.XI[b][:, :, :]), 0.0, ALU.mult, ALU.add)\
                    .then_inc(self.expanded, 1)
                wait(v, self.expanded, t + 1)

            def gathers(self, pool):
                def step(t, n, b, first, last):
                    wait(pool, self.idx_in[b], (n + 1) * (16 * len(self.indices)))
                    if not first:
                        wait(pool, self.scanned, t - 1)
                    pool.sem_inc(parked, 1)
                    for c in range(C):
                        for g, (tab, _, which) in enumerate(self.tables):
                            pool.indirect_dma_start(
                                out=self.G[g][b][:, c, :], out_offset=None, in_=tab,
                                in_offset=bass.IndirectOffsetOnAxis(ap=self.IDX[which][b][:, c:c + 1], axis=0),
                            ).then_inc(self.rows_in[g][b], 16)
                chunks(pool, step)

            def load_indices(self, sp, t, n, b, first):
                if not first:
                    for g in range(len(self.tables)):
                        wait(sp, self.rows_in[g][b], n * (16 * C))
                for name, source in self.indices.items():
                    sp.dma_start(self.IDX[name][b][:, :], source[:, bass.ds(t * C, C)])\
                      .then_inc(self.idx_in[b], 16)

            def maxima(self, v, st, t, n, b, first):
                nc_v, H = nc.vector, self.H
                st.do(nc_v.tensor_copy(self.LG[:, :, 0:1], MS[1 - b][:, 0:H, C:C + 1]))
                st.wait()
                if not first:
                    wait(v, self.copied_out, (t - 1) * 2)
                flat = lambda ap: ap.rearrange("p h j -> p (h j)")
                st.then(nc_v.tensor_tensor_scan(flat(MS[b][:, 0:H, :]), flat(self.BR[:, :, :]),
                                                flat(self.LG[:, :, :]), 0.0, ALU.add, ALU.max))
                if not first:
                    wait(v, self.exps_ready, t)
                st.do(nc_v.tensor_tensor(self.ARG[:, 0, :, :], MS[b][:, 0:H, 0:C], MS[b][:, 0:H, 1:1 + C],
                                         ALU.subtract))
                st.then(nc_v.tensor_tensor(self.ARG[:, 1, :, :], self.LG[:, :, 1:1 + C], MS[b][:, 0:H, 1:1 + C],
                                           ALU.subtract))
                nc_v.tensor_tensor(self.ARG[:, 0, :, :], self.ARG[:, 0, :, :], self.BR[:, :, 1:1 + C], ALU.add)\
                    .then_inc(self.args_ready, 1)

            def breaks(self, st, t):
                st.do(nc.vector.tensor_scalar(self.BR[:, :, 1:1 + C],
                                              BREAK[:, bass.ds(t * C, C)].unsqueeze(1)
                                              .to_broadcast([P, self.H, C]), 1.0, None, ALU.mult))

            def sums(self, v, t, n, b, first, rows, weight=None):
                H, FE, R = self.H, self.FE, self.R
                st = Steps(v, self.b_steps, t * (3 if self.weights else 2))
                wait(v, self.decays_ready, (t + 1) * self.n_decays())
                if self.layer == 2:
                    wait(v, self.exps_ready, t + 1)
                if weight is None:
                    w = self.EX[b][:, 1, :, :].unsqueeze(2).to_broadcast([P, H, CH, C])
                    st.do(nc.vector.tensor_tensor(
                        self.MSG[:, 0:FE, 1:1 + C].rearrange("p (h c) j -> p h c j", c=CH),
                        rows.rearrange("p j (h c) -> p h c j", c=CH), w, ALU.mult))
                    st.do(nc.vector.tensor_copy(self.MSG[:, FE:R, 1:1 + C], self.EX[b][:, 1, :, :]))
                else:
                    st.do(nc.vector.tensor_tensor(self.MSG[:, :, 1:1 + C], rows.rearrange("p j f -> p f j"),
                                                  weight.unsqueeze(1).to_broadcast([P, FE, C]), ALU.mult))
                st.do(nc.vector.tensor_copy(self.MSG[:, :, 0:1], SC[1 - b][:, 0:R, C:C + 1]))
                st.wait()
                if not first:
                    wait(v, self.copied_out, (t - 1) * self.n_copies())
                flat = lambda ap: ap.rearrange("p r j -> p (r j)")
                nc.vector.tensor_tensor_scan(flat(SC[b][:, 0:R, :]), flat(self.DEC[b][:, :, :]),
                                             flat(self.MSG[:, :, :]), 0.0, ALU.mult, ALU.add)\
                    .then_inc(self.scanned, 1)
                wait(v, self.scanned, t + 1)

            def n_decays(self):
                return 2 if self.running_max else 1

            def n_copies(self):
                return 2 if self.running_max else 1

            def factors(self, act, t, n, b, first):
                H, FE, R = self.H, self.FE, self.R
                if self.layer != 3:
                    wait(act, self.args_ready, t + 1)
                if not first:
                    wait(act, self.scanned, t - 1)
                if self.running_max:
                    nc.scalar.activation(self.EX[b][:, :, :, :], self.ARG[:, :, :, :], ACT.Exp)\
                      .then_inc(self.exps_ready, 1)
                    wait(act, self.exps_ready, t + 1)
                    decay = self.EX[b][:, 0, :, :]
                    nc.scalar.activation(self.DEC[b][:, 0:FE, 1:1 + C].rearrange("p (h c) j -> p h c j", c=CH),
                                         decay.unsqueeze(2).to_broadcast([P, H, CH, C]), ACT.Copy)\
                      .then_inc(self.decays_ready, 1)
                    nc.scalar.activation(self.DEC[b][:, FE:R, 1:1 + C], decay, ACT.Copy)\
                      .then_inc(self.decays_ready, 1)
                    return
                if self.layer == 2:
                    nc.scalar.activation(self.EX[b][:, 1, :, :], self.ARG[:, 1, :, :], ACT.Exp)\
                      .then_inc(self.exps_ready, 1)
                else:
                    self.same_factors(act, t, b, first)

            def same_factors(self, act, t, b, first):
                if not first:
                    wait(act, self.scanned, t - 1)
                act.sem_inc(parked, 1)
                nc.scalar.activation(self.DEC[b][:, :, 1:1 + C],
                                     SAME[:, bass.ds(t * C, C)].unsqueeze(1).to_broadcast([P, self.R, C]),
                                     ACT.Copy)\
                  .then_inc(self.decays_ready, 1)

            def store_rows(self, act, t, n, b, early):
                R, H = self.R, self.H
                wait(act, self.scanned, t + 1)
                if not early:
                    wait(act, self.stored[b], n * 16)
                nc.scalar.activation(self.OUT[b][:, :, 0:R], SC[b][:, 0:R, 1:1 + C].rearrange("p r j -> p j r"),
                                     ACT.Copy).then_inc(self.copied_out, 1)
                if self.running_max:
                    nc.scalar.activation(self.OUT[b][:, :, R:R + H],
                                         MS[b][:, 0:H, 1:1 + C].rearrange("p r j -> p j r"), ACT.Copy)\
                      .then_inc(self.copied_out, 1)
                wait(act, self.copied_out, (t + 1) * self.n_copies())
                act.dma_start(row_view(scan_tabs[self.layer], t), self.OUT[b][:, :, :])\
                   .then_inc(self.stored[b], 16)

            def drain_stores(self, act):
                for b in range(2):
                    wait(act, self.stored[b], NCH // 2 * 16)

        def edges_0(src_ap):
            with ExitStack() as ctx:
                e = Edges(ctx, 0, [(xl_tab, 64, "src")], {"src": src_ap})
                ATTR = e.pair("ATTR", [P, C, 16])
                ATTR_T = sb("ATTR_T", [P, P], F32, ctx)
                WE8 = sb("WE8", [P, C, 64], F32, ctx)
                TR, PROJ = [e.bank("TR0"), e.bank("TR1")], [e.bank("PROJ0"), e.bank("PROJ1")]
                attr_t, attr_c, projected, we_in, cleared = (e.sem("attr_t"), e.sem("attr_c"), e.sem("projected"),
                                                             e.sem("we_in"), e.sem("cleared"))
                with nc.Block() as block:
                    @block.sync
                    def _(sp):
                        wait(sp, cleared, 1)
                        for c in range(C):
                            sp.dma_start(WE8[16 * c:16 * c + 16, c, :], we).then_inc(we_in, 16)

                        def step(t, n, b, first, last):
                            e.load_indices(sp, t, n, b, first)
                            e.load_spread(sp, t, n, b, first)
                            if not first:
                                wait(sp, attr_t, t - 1)
                            sp.dma_start(ATTR[b][:, :, :], row_view(ea16, t)).then_inc(e.attr_in[b], 16)
                        chunks(sp, step)

                    @block.gpsimd
                    def _(pool):
                        nc.gpsimd.memset(WE8[:, :, :], 0.0).then_inc(cleared, 1)
                        e.constants()
                        e.first_rows(pool, xr_tab)
                        e.gathers(pool)

                    @block.tensor
                    def _(pe):
                        wait(pe, we_in, 16 * C)

                        def step(t, n, b, first, last):
                            wait(pe, e.attr_in[b], (n + 1) * 16)
                            nc.tensor.transpose(TR[b][:, 0:P], ATTR[b][:, :, :].rearrange("p j f -> p (j f)"),
                                                IDENT[:, :]).then_inc(attr_t, 1)
                            wait(pe, attr_c, t + 1)
                            if not first:
                                wait(pe, e.args_ready, t - 1)
                            nc.tensor.matmul(PROJ[b][:, :], ATTR_T[:, :],
                                             WE8[:, :, :].rearrange("p j f -> p (j f)"), start=True, stop=True)\
                              .then_inc(projected, 1)
                        chunks(pe, step)

                    @block.scalar
                    def _(act):
                        wait(act, e.ready, e.N_READY)

                        def ahead(t, n, b, first):
                            e.turn(act, t, n, b, first)
                            wait(act, attr_t, t + 1)
                            if not first:
                                wait(act, projected, t)
                            nc.scalar.activation(ATTR_T[:, :], TR[b][:, 0:P], ACT.Copy).then_inc(attr_c, 1)

                        def step(t, n, b, first, last):
                            if first:
                                ahead(t, n, b, True)
                            e.factors(act, t, n, b, first)
                            if not last:
                                ahead(t + 1, n + b, 1 - b, False)
                            e.store_rows(act, t, n, b, first)
                        chunks(act, step)
                        e.drain_stores(act)

                    @block.vector
                    def _(v):
                        wait(v, e.ready, e.N_READY)

                        def logits(t, n, b, first):
                            T, LG = e.T1, e.LG
                            st = Steps(v, e.a_steps, t * 10)
                            wait(v, e.rows_in[0][b], (n + 1) * (16 * C))
                            st.then(nc.vector.tensor_tensor(T[:, :, :], e.G[0][b][:, :, :],
                                                            e.XE[b][:, :, 1:1 + C].rearrange("p f j -> p j f"),
                                                            ALU.add))
                            wait(v, projected, t + 1)
                            st.then(nc.vector.tensor_tensor(T[:, :, :], T[:, :, :],
                                                            PROJ[b][:, :].rearrange("p (j f) -> p j f", j=C),
                                                            ALU.add))
                            st.then(nc.vector.scalar_tensor_tensor(out=T[:, :, :], in0=T[:, :, :], scalar=0.2,
                                                                   in1=T[:, :, :], op0=ALU.mult, op1=ALU.max))
                            st.then(nc.vector.tensor_tensor(T[:, :, :], T[:, :, :],
                                                            vec("att").unsqueeze(1).to_broadcast([P, C, 64]),
                                                            ALU.mult))
                            if not first:
                                wait(v, e.args_ready, t)
                            e.breaks(st, t)
                            st.do(nc.vector.tensor_reduce(LG[:, :, 1:1 + C].rearrange("p h j -> p j h"),
                                                          T[:, :, :].rearrange("p j (h c) -> p j h c", c=CH),
                                                          AX.X, ALU.add))
                            e.maxima(v, st, t, n, b, first)
                            assert st.n == 10, st.n

                        def step(t, n, b, first, last):
                            e.expand(v, t, n, b, first)
                            logits(t, n, b, first)
                            e.sums(v, t, n, b, first, e.G[0][b][:, :, :])
                        chunks(v, step)

        def edges_2(src_ap):
            with ExitStack() as ctx:
                e = Edges(ctx, 2, [(kv_tab, 128, "src")], {"src": src_ap})
                with nc.Block() as block:
                    @block.sync
                    def _(sp):
                        def step(t, n, b, first, last):
                            e.load_indices(sp, t, n, b, first)
                            e.load_spread(sp, t, n, b, first)
                        chunks(sp, step)

                    @block.gpsimd
                    def _(pool):
                        e.constants()
                        e.first_rows(pool, q2_tab)
                        e.gathers(pool)

                    @block.scalar
                    def _(act):
                        wait(act, e.ready, e.N_READY)

                        def step(t, n, b, first, last):
                            if first:
                                e.turn(act, t, n, b, True)
                            e.factors(act, t, n, b, first)
                            if not last:
                                e.turn(act, t + 1, n + b, 1 - b, False)
                            e.store_rows(act, t, n, b, first)
                        chunks(act, step)
                        e.drain_stores(act)

                    @block.vector
                    def _(v):
                        wait(v, e.ready, e.N_READY)

                        def scores(t, n, b, first):
                            st = Steps(v, e.a_steps, t * 3)
                            wait(v, e.rows_in[0][b], (n + 1) * (16 * C))
                            st.then(nc.vector.tensor_tensor(e.T1[:, :, :], e.G[0][b][:, :, 0:64],
                                                            e.XE[b][:, :, 1:1 + C].rearrange("p f j -> p j f"),
                                                            ALU.mult))
                            st.then(nc.vector.tensor_reduce(e.LG[:, :, 0:C].rearrange("p h j -> p j h"),
                                                            e.T1[:, :, :].rearrange("p j (h c) -> p j h c", c=CH),
                                                            AX.X, ALU.add))
                            st.then(nc.vector.tensor_scalar(e.LG[:, :, 0:C], e.LG[:, :, 0:C], 1.0 / D ** 0.5, -5.0,
                                                            ALU.mult, ALU.max))
                            if not first:
                                wait(v, e.exps_ready, t)
                            nc.vector.tensor_scalar(e.ARG[:, 1, :, :], e.LG[:, :, 0:C], 5.0, None, ALU.min)\
                              .then_inc(e.args_ready, 1)

                        def step(t, n, b, first, last):
                            e.expand(v, t, n, b, first)
                            scores(t, n, b, first)
                            e.sums(v, t, n, b, first, e.G[0][b][:, :, 64:128])
                        chunks(v, step)

        def edges_3():
            with ExitStack() as ctx:
                e = Edges(ctx, 3, [(rel_tab, 64, "rel")], {"rel": relidx})
                EW = sb("EW", [P, J], F32, ctx)
                ew_in = e.sem("ew_in")
                with nc.Block() as block:
                    @block.sync
                    def _(sp):
                        sp.dma_start(EW[:, :], ew).then_inc(ew_in, 16)
                        chunks(sp, lambda t, n, b, first, last: e.load_indices(sp, t, n, b, first))

                    @block.gpsimd
                    def _(pool):
                        e.constants()
                        e.gathers(pool)

                    @block.scalar
                    def _(act):
                        wait(act, e.ready, e.N_READY)

                        def step(t, n, b, first, last):
                            e.factors(act, t, n, b, first)
                            e.store_rows(act, t, n, b, first)
                        chunks(act, step)
                        e.drain_stores(act)

                    @block.vector
                    def _(v):
                        wait(v, e.ready, e.N_READY)
                        wait(v, ew_in, 16)

                        def step(t, n, b, first, last):
                            wait(v, e.rows_in[0][b], (n + 1) * (16 * C))
                            e.sums(v, t, n, b, first, e.G[0][b][:, :, :], EW[:, bass.ds(t * C, C)])
                        chunks(v, step)

        def edges_1(src_ap, dst_ap):
            with ExitStack() as ctx:
                e = Edges(ctx, 1, [(x1_tab, 64, "src"), (q1_tab, 128, "dst")], {"src": src_ap, "dst": dst_ap})
                EF, S9 = e.pair("EF", [P, C, 64]), e.pair("S9", [P, C, SH + 1])
                XS = sb("XS", [P, C, SH + 1, 64], F32, ctx)
                XHI, XLO = e.pair("XHI", [P, 5, 512], F32R), e.pair("XLO", [P, 4, 512], F32R)
                EFT = sb("EFT", [P, 512], F32, ctx)
                HT = sb("HT", [P, 2, 512], F32, ctx)
                HHI, HLO = e.pair("HHI", [P, 2, 512], F32R), e.pair("HLO", [P, 2, 512], F32R)
                WKV = [sb(f"WKV{i}", [P, 256], F32, ctx) for i in range(4)]
                RW = e.pair("RW", [P, C, 256])
                CHI, CLO = sb("CHI", [P, 5, 256], F32R, ctx), sb("CLO", [P, 5, 256], F32R, ctx)
                CF = XS[:, :, :, :].rearrange("p j s f -> p (j s f)")[:, 0:5 * 256]\
                    .rearrange("p (k n) -> p k n", k=5)
                W1 = sb("W1", [P, P], F32, ctx)
                W2 = sb("W2", [P, 256], F32, ctx)
                W2HI, W2LO = sb("W2HI", [P, 256], F32R, ctx), sb("W2LO", [P, 256], F32R, ctx)
                B1 = sb("B1", [P, 1], F32, ctx)
                B2F = sb("B2F", [1, 5, 256], F32, ctx)
                B2 = [sb(f"B2{i}", [1, 256], BF16, ctx) for i in range(3)]
                B2R = sb("B2R", [3, 256], BF16, ctx)
                ONEB = sb("ONEB", [3, P], BF16, ctx)
                RING = [e.bank(f"RING{i}") for i in range(4)]
                COLS = [e.bank(f"COLS{i}") for i in range(4)]
                xs_ready, staged, evacuated = e.sem("xs_ready"), e.sem("staged"), e.sem("evacuated")
                col_done, w_copied, col_used = e.sem("col_done"), e.sem("w_copied"), e.sem("col_used")
                hidden_hi, hidden_split = e.sem("hidden_hi"), e.sem("hidden_split")
                w_in, parts, b2_in, split, c_split = (e.sem("w_in"), e.sem("parts"), e.sem("b2_in"),
                                                      e.sem("split"), e.sem("c_split"))

                STAGES = 13

                def ring(q, b):
                    return (q + b) % 4

                def holder_before(q, b):
                    return next(d for d in range(1, STAGES + 1)
                                if ring((q - d) % STAGES, b if q >= d else 1 - b) == ring(q, b))

                def first_stage(half):
                    return (1, 8)[half]

                with nc.Block() as block:
                    @block.sync
                    def _(sp):
                        wait(sp, parts, 1)
                        for ap, source in ((CF[:, 0:4, :], cfix[0:512, :].rearrange("(k p) n -> p k n", p=P)),
                                           (CF[0:64, 4, :], cfix[512:576, :]),
                                           (CF[64:128, 4, :], cfix[512:576, :]),
                                           (W2[0:64, 0:128], w2[:, 0:128]), (W2[64:128, 128:256], w2[:, 128:256]),
                                           (B1[:, :], b1), (B2F[:, 0, :], b2),
                                           (W1[0:64, :], w64[:, W_COLS["k_w1"][0]:W_COLS["v_w1"][1]]),
                                           (W1[64:128, :], w64[:, W_COLS["k_w1"][0]:W_COLS["v_w1"][1]])):
                            sp.dma_start(ap, source).then_inc(w_in, 16)

                        wait(sp, parts, 8)
                        for i in range(3):
                            sp.dma_start(B2R[i:i + 1, :], B2[i][:, :]).then_inc(b2_in, 16)

                        def step(t, n, b, first, last):
                            e.load_indices(sp, t, n, b, first)
                            if not first:
                                wait(sp, staged, t * STAGES - (2 * STAGES - 1))
                                wait(sp, xs_ready, (t - 1) * 2)
                            sp.dma_start(EF[b][:, :, :], row_view(ea64, t)).then_inc(e.attr_in[b], 16)
                            sp.dma_start(S9[b][:, :, :], row_view(ea9, t)).then_inc(e.attr_in[b], 16)
                        chunks(sp, step)

                    @block.gpsimd
                    def _(pool):
                        nc.gpsimd.memset(W2[:, :], 0.0).then_inc(parts, 1)
                        e.constants()

                        def rows(g, t, n, b):
                            tab, _, which = e.tables[g]
                            pool.sem_inc(parked, 1)
                            for col in range(C):
                                pool.indirect_dma_start(
                                    out=e.G[g][b][:, col, :], out_offset=None, in_=tab,
                                    in_offset=bass.IndirectOffsetOnAxis(ap=e.IDX[which][b][:, col:col + 1], axis=0),
                                ).then_inc(e.rows_in[g][b], 16)

                        def node_rows(t, n, b, first):
                            wait(pool, e.idx_in[b], (n + 1) * 32)
                            if not first:
                                wait(pool, xs_ready, (t - 1) * 2)
                            rows(0, t, n, b)

                        def step(t, n, b, first, last):
                            if first:
                                node_rows(0, 0, 0, True)
                                node_rows(1, 0, 1, True)
                            elif not last:
                                node_rows(t + 1, n + b, 1 - b, False)
                            wait(pool, e.idx_in[b], (n + 1) * 32)
                            if not first:
                                wait(pool, e.args_ready, t - 1)
                            rows(1, t, n, b)
                        chunks(pool, step)

                    @block.tensor
                    def _(pe):
                        wait(pe, w_in, 16 * 9)
                        wait(pe, b2_in, 48)
                        wait(pe, c_split, 2)

                        def free(t, q, b, first):
                            back = holder_before(q, b)
                            if first and q < back:
                                return
                            old, tt = (q - back) % STAGES, t if q >= back else t - 1
                            if old in (0, 6, 7):
                                wait(pe, evacuated, tt * STAGES + (old + 1))
                            else:
                                wait(pe, split, tt * 10 + (old if old < 6 else old - 2))

                        def transposes(t, b, half, first):
                            for k in range(5):
                                q = first_stage(half) + k
                                free(t, q, b, first)
                                for c in range(4):
                                    last = nc.tensor.transpose(
                                        RING[ring(q, b)][:, c * P:(c + 1) * P],
                                        XS[:, 4 * half + c, :, :].rearrange("p s f -> p (s f)")
                                        [:, k * P:(k + 1) * P], IDENT[:, :])
                                last.then_inc(staged, 1)

                        def columns(t, b, half, first):
                            wait(pe, split, t * 10 + 5 * (half + 1))
                            wait(pe, hidden_split, t * 2 + 2)
                            for c in range(4):
                                col = 4 * half + c
                                if not (first and half == 0):
                                    wait(pe, col_used, t * C + (col - 3))
                                bank = COLS[col % 4]
                                for k in range(5):
                                    hi = XHI[half][:, k, c * P:(c + 1) * P]
                                    nc.tensor.matmul(bank[:, 0:256], hi, CHI[:, k, :], start=(k == 0),
                                                     stop=False)
                                    nc.tensor.matmul(bank[:, 0:256], hi, CLO[:, k, :], start=False,
                                                     stop=(k == 4))
                                    if k < 4:
                                        nc.tensor.matmul(bank[:, 0:256], XLO[half][:, k, c * P:(c + 1) * P],
                                                         CHI[:, k, :], start=False, stop=False)
                                nc.tensor.matmul(bank[:, 256:512], ONEB[:, :], B2R[:, :], start=True, stop=False)
                                edges_ = slice((col // 2) * P, (col // 2 + 1) * P)
                                for h, w in ((HHI, W2HI), (HHI, W2LO), (HLO, W2HI)):
                                    last = nc.tensor.matmul(bank[:, 256:512], h[b][:, col % 2, edges_], w[:, :],
                                                            start=False, stop=(h is HLO))
                                last.then_inc(col_done, 1)

                        def step(t, n, b, first, last):
                            wait(pe, e.attr_in[b], (n + 1) * 32)
                            free(t, 0, b, first)
                            for c in range(4):
                                ins = nc.tensor.transpose(RING[ring(0, b)][:, c * P:(c + 1) * P],
                                                          EF[b][:, 2 * c:2 * c + 2, :]
                                                          .rearrange("p j f -> p (j f)"), IDENT[:, :])
                            ins.then_inc(staged, 1)
                            wait(pe, xs_ready, t * 2 + 1)
                            transposes(t, b, 0, first)
                            for a in range(2):
                                free(t, 6 + a, b, first)
                                nc.tensor.matmul(RING[ring(6 + a, b)][:, :], W1[64 * a:64 * a + 64, :],
                                                 EFT[64 * a:64 * a + 64, :], start=True, stop=True)\
                                  .then_inc(staged, 1)
                            if not first:
                                columns(t - 1, 1 - b, 1, False)
                            wait(pe, xs_ready, t * 2 + 2)
                            transposes(t, b, 1, first)
                            columns(t, b, 0, first)

                        chunks(pe, step)
                        columns(NCH - 1, 1, 1, False)

                    @block.scalar
                    def _(act):
                        wait(act, w_in, 16 * 9)
                        wait(act, e.ready, e.N_READY)

                        def evacuate(t, q, b, out_ap, func=ACT.Copy, **kw):
                            wait(act, staged, t * STAGES + (q + 1))
                            nc.scalar.activation(out_ap, RING[ring(q, b)][:, :], func, **kw)\
                              .then_inc(evacuated, 1)

                        def half_transposes(t, b, half, first):
                            if not first:
                                wait(act, col_done, t * C - (4 if half == 0 else 0))
                            for k in range(5):
                                evacuate(t, first_stage(half) + k, b, XHI[half][:, k, :])

                        def weights(t, col, early):
                            wait(act, col_done, t * C + (col + 1))
                            if not early:
                                wait(act, col_used, t * C + (col - 3))
                            nc.scalar.activation(WKV[col % 4][:, :], COLS[col % 4][:, 256:512], ACT.Copy)\
                              .then_inc(w_copied, 1)

                        def step(t, n, b, first, last):
                            if not first:
                                wait(act, staged, t * STAGES - (STAGES - 8))
                            evacuate(t, 0, b, EFT[:, :])
                            half_transposes(t, b, 0, first)
                            if not first:
                                wait(act, hidden_split, t * 2)
                            for a in range(2):
                                evacuate(t, 6 + a, b, HT[:, a, :], func=ACT.Relu, bias=B1[:, 0:1])
                            if not isinstance(t, int) or t >= 2:
                                e.store_rows(act, t - 2, n - 1, b, False)
                            for a in range(2):
                                if not first:
                                    weights(t - 1, 4 + a, False)
                                wait(act, evacuated, t * STAGES + (7 + a))
                                nc.scalar.activation(HHI[b][:, a, :], HT[:, a, :], ACT.Copy)\
                                  .then_inc(hidden_hi, 1)
                            if not first:
                                for col in range(6, 8):
                                    weights(t - 1, col, False)
                            half_transposes(t, b, 1, first)
                            if not first:
                                e.factors(act, t - 1, before(n, b), 1 - b, False)
                            for col in range(4):
                                weights(t, col, first)
                        chunks(act, step, 4)
                        e.store_rows(act, NCH - 2, NCH // 2 - 1, 0, False)
                        for col in range(4, 8):
                            weights(NCH - 1, col, False)
                        e.factors(act, NCH - 1, NCH // 2 - 1, 1, False)
                        e.store_rows(act, NCH - 1, NCH // 2 - 1, 1, False)
                        e.drain_stores(act)

                    @block.vector
                    def _(v):
                        wait(v, e.ready, e.N_READY)
                        wait(v, w_in, 16 * 9)
                        nc.vector.memset(ONEB[:, :], 1.0).then_inc(parts, 1)
                        nc.vector.tensor_copy(B2[0][:, :], B2F[:, 0, :]).then_inc(parts, 1)
                        wait(v, parts, 3)
                        nc.vector.tensor_tensor(B2F[:, 1, :], B2F[:, 0, :], B2[0][:, :], ALU.subtract)\
                          .then_inc(parts, 1)
                        wait(v, parts, 4)
                        nc.vector.tensor_copy(B2[1][:, :], B2F[:, 1, :]).then_inc(parts, 1)
                        wait(v, parts, 5)
                        nc.vector.tensor_tensor(B2F[:, 2, :], B2F[:, 1, :], B2[1][:, :], ALU.subtract)\
                          .then_inc(parts, 1)
                        wait(v, parts, 6)
                        nc.vector.tensor_copy(B2[2][:, :], B2F[:, 2, :]).then_inc(parts, 2)

                        nc.vector.tensor_copy(CHI[:, :, :], CF).then_inc(parts, 1)
                        nc.vector.tensor_copy(W2HI[:, :], W2[:, :]).then_inc(parts, 1)
                        wait(v, parts, 10)
                        nc.vector.tensor_tensor(CLO[:, :, :], CF, CHI[:, :, :].bitcast(F32), ALU.subtract)\
                          .then_inc(c_split, 1)
                        nc.vector.tensor_tensor(W2LO[:, :], W2[:, :], W2HI[:, :].bitcast(F32), ALU.subtract)\
                          .then_inc(c_split, 1)
                        wait(v, c_split, 2)

                        def outer(t, n, b, first, half):
                            if half == 0:
                                wait(v, e.rows_in[0][b], (n + 1) * (16 * C))
                                wait(v, e.attr_in[b], (n + 1) * 32)
                            if not first:
                                wait(v, staged, t * STAGES - (STAGES - (6, 13)[half]))
                            j = slice(4 * half, 4 * half + 4)
                            nc.vector.tensor_tensor(
                                XS[:, j, :, :],
                                e.G[0][b][:, j, :].unsqueeze(2).to_broadcast([P, 4, SH + 1, 64]),
                                S9[b][:, j, :].unsqueeze(3).to_broadcast([P, 4, SH + 1, 64]), ALU.mult)\
                              .then_inc(xs_ready, 1)

                        def lows(t, b, half, first):
                            if not first:
                                wait(v, col_done, t * C - (4 if half == 0 else 0))
                            for k in range(5):
                                q = first_stage(half) + k
                                rows = slice(0, P) if k < 4 else slice(64, P)
                                hi = XHI[half][rows, k, :]
                                wait(v, evacuated, t * STAGES + (q + 1))
                                nc.vector.tensor_tensor(XLO[half][:, k, :] if k < 4 else hi,
                                                        RING[ring(q, b)][rows, :], hi.bitcast(F32),
                                                        ALU.subtract).then_inc(split, 1)

                        def hidden_low(t, b, a):
                            wait(v, hidden_hi, t * 2 + (a + 1))
                            nc.vector.tensor_tensor(HLO[b][:, a, :], HT[:, a, :], HHI[b][:, a, :].bitcast(F32),
                                                    ALU.subtract).then_inc(hidden_split, 1)

                        def products(t, b, cols):
                            for col in cols:
                                wait(v, w_copied, t * C + (col + 1))
                                nc.vector.tensor_tensor(RW[b][:, col, :], COLS[col % 4][:, 0:256],
                                                        WKV[col % 4][:, :], ALU.mult).then_inc(col_used, 1)

                        def logits(t, n, b, first):
                            st = Steps(v, e.a_steps, t * 7)
                            wait(v, e.rows_in[1][b], (n + 1) * (16 * C))
                            wait(v, col_used, (t + 1) * C)
                            st.then(nc.vector.tensor_tensor(e.T1[:, :, :], RW[b][:, :, 0:128], e.G[1][b][:, :, :],
                                                            ALU.mult))
                            if not first:
                                wait(v, e.args_ready, t)
                            e.breaks(st, t)
                            st.do(nc.vector.tensor_reduce(e.LG[:, :, 1:1 + C].rearrange("p h j -> p j h"),
                                                          e.T1[:, :, :].rearrange("p j (h c) -> p j h c", c=CH),
                                                          AX.X, ALU.add))
                            e.maxima(v, st, t, n, b, first)
                            assert st.n == 7, st.n

                        def step(t, n, b, first, last):
                            if first:
                                for half in range(2):
                                    outer(0, 0, 0, True, half)
                            lows(t, b, 0, first)
                            if not isinstance(t, int) or t >= 2:
                                e.sums(v, t - 2, n - 1, b, False, RW[b][:, :, 128:256])
                            if not last:
                                outer(t + 1, n + b, 1 - b, False, 0)
                            for a in range(2):
                                if not first:
                                    products(t - 1, 1 - b, range(4 + 2 * a, 6 + 2 * a))
                                hidden_low(t, b, a)
                            lows(t, b, 1, first)
                            if not first:
                                logits(t - 1, before(n, b), 1 - b, False)
                            if not last:
                                outer(t + 1, n + b, 1 - b, False, 1)
                            products(t, b, range(4))
                        chunks(v, step, 4)
                        end = NCH - 1
                        e.sums(v, end - 1, NCH // 2 - 1, 0, False, RW[0][:, :, 128:256])
                        products(end, 1, range(4, 8))
                        logits(end, NCH // 2 - 1, 1, False)
                        e.sums(v, end, NCH // 2 - 1, 1, False, RW[1][:, :, 128:256])

        def finish_layer(layer):
            H, R, WD = HEADS[layer], SUMS[layer], ROW[layer]
            FE = H * CH
            has_weights = R > FE
            groups = H // 4
            GR = 64 + 4 * has_weights
            with ExitStack() as ctx:
                def s(name):
                    return phase_semaphore(name)

                def bank(name):
                    return ctx.enter_context(nc.psum_tensor(unique(name), [P, 512], F32))

                GN = sb("GN", [P, K, WD], F32, ctx)
                GC = sb("GC", [P, K, WD], F32, ctx)
                MX = sb("MX", [P, K, H], F32, ctx)
                Y = sb("Y", [P, K, 64], F32, ctx)
                SQ = sb("SQ", [P, K, 64], F32, ctx)
                AT = sb("AT", [P, K * P], F32, ctx)
                LROW = sb("LROW", [P, 3, GR], F32, ctx)
                CT = sb("CT", [P, 3, P], F32, ctx)
                CW = sb("CW", [P, 5, P], F32, ctx)
                CS = sb("CS", [P, 2, 1 + P], F32, ctx)
                CROW = sb("CROW", [P, WD], F32, ctx)
                SM = sb("SM", [P, 8, 64], F32, ctx)
                SN = sb("SN", [P, 6, K], F32, ctx)
                TP = [bank("TP0"), bank("TP1")]
                CP, CB, PB = bank("CP"), bank("CB"), bank("PB")
                PO = [bank("PO0"), bank("PO1")]
                dve, carried = s("dve"), s("carried")
                rows_in, carry_in, stored = s("rows_in"), s("carry_in"), s("stored")
                c_rows, c_tp, c_arg, c_exp, c_sum, c_back, c_row = (s("c_rows"), s("c_tp"), s("c_arg"), s("c_exp"),
                                                                    s("c_sum"), s("c_back"), s("c_row"))
                merge_arg, merge_exp, agg_ready, agg_t, agg_c, agg_mm, agg_add = (
                    s("merge_arg"), s("merge_exp"), s("agg_ready"), s("agg_t"), s("agg_c"), s("agg_mm"), s("agg_add"))
                bn_part, bn_sum, bn_var, bn_sd = s("bn_part"), s("bn_sum"), s("bn_var"), s("bn_sd")
                ln_var, ln_sd, gelu_in, gelu_out, done = s("ln_var"), s("ln_sd"), s("gelu_in"), s("gelu_out"), s("done")
                tab = carry_tabs[layer]
                project_agg = layer in (1, 2)
                units = GROUPS
                N = slice(0, NP)

                with nc.Block() as block:
                    @block.gpsimd
                    def _(pool):
                        for k in range(K):
                            pool.indirect_dma_start(
                                out=GN[N, k, :], out_offset=None, in_=scan_tabs[layer],
                                in_offset=bass.IndirectOffsetOnAxis(ap=END_AT[N, k:k + 1], axis=0),
                            ).then_inc(rows_in, 16)
                            if k == 12:
                                pool.wait_ge(carries_nulled, 16 * 4)
                                pool.wait_ge(c_row, groups)
                                pool.indirect_dma_start(
                                    out=tab, in_=CROW[:, :], in_offset=None,
                                    out_offset=bass.IndirectOffsetOnAxis(ap=CARRY_AT[:, 0:1], axis=0),
                                    bounds_check=NPAD - 1, oob_is_err=False).then_inc(carried, 16)

                    @block.sync
                    def _(sp):
                        sp.wait_ge(carried, 16)
                        sp.dma_start(GC[:, :, :], tab.rearrange("(p k) f -> p k f", k=K)).then_inc(carry_in, 16)
                        if layer == 3:
                            sp.wait_ge(done, 1)
                            sp.dma_start(out.rearrange("(p k) f -> p k f", k=K), X[N, :, :]).then_inc(stored, 16)
                            sp.wait_ge(stored, 16)

                    @block.tensor
                    def _(pe):
                        for g in range(groups):
                            pe.wait_ge(c_rows, g + 1)
                            for n in range(3):
                                last = nc.tensor.transpose(CP[0:GR, n * P:(n + 1) * P], LROW[:, n, :], IDENT[:, :])
                            last.then_inc(c_tp, 1)
                            pe.wait_ge(c_sum, g + 1)
                            nc.tensor.transpose(CB[:, 0:GR], CS[0:GR, 0, 0:P], IDENT[0:GR, 0:GR]).then_inc(c_back, 1)
                            nc.tensor.transpose(CB[:, P:P + GR], CS[0:GR, 1, 0:P], IDENT[0:GR, 0:GR])\
                              .then_inc(c_back, 1)
                        if project_agg:
                            weights = WO_T[:, :] if layer == 1 else wcol("Wo")
                            pe.wait_ge(agg_ready, 1)
                            for u, (k0, m) in enumerate(units):
                                if u >= 2:
                                    pe.wait_ge(agg_c, u - 1)
                                for c in range(m):
                                    last = nc.tensor.transpose(TP[u % 2][0:FE, c * P:c * P + NP],
                                                               GN[N, k0 + c, 0:FE], IDENT[N, N])
                                last.then_inc(agg_t, 1)
                            for u, (k0, m) in enumerate(units):
                                pe.wait_ge(agg_c, u + 1)
                                if u >= 2:
                                    pe.wait_ge(agg_add, u - 1)
                                for c in range(m):
                                    last = nc.tensor.matmul(PO[u % 2][N, c * 64:c * 64 + 64],
                                                            AT[0:FE, (k0 + c) * P:(k0 + c) * P + NP], weights,
                                                            start=True, stop=True)
                                last.then_inc(agg_mm, 1)
                        if layer != 2:
                            for n in range(2):
                                pe.wait_ge(bn_part, n + 1)
                                nc.tensor.matmul(PB[:, n * 64:n * 64 + 64], ONES[N, :], SM[N, n, :], start=True,
                                                 stop=True).then_inc(bn_sum, 1)

                    @block.scalar
                    def _(act):
                        for g in range(groups):
                            act.wait_ge(c_arg, g + 1)
                            nc.scalar.activation(CW[0:GR, 1:3, :], CW[0:GR, 1:3, :], ACT.Exp).then_inc(c_exp, 1)
                        act.wait_ge(merge_arg, 1)
                        nc.scalar.activation(GN[N, :, R:WD], GN[N, :, R:WD], ACT.Exp).then_inc(merge_exp, 1)
                        nc.scalar.activation(GC[N, :, R:WD], GC[N, :, R:WD], ACT.Exp).then_inc(merge_exp, 1)
                        if project_agg:
                            for u, (k0, m) in enumerate(units):
                                act.wait_ge(agg_t, u + 1)
                                nc.scalar.activation(
                                    AT[0:FE, k0 * P:(k0 + m) * P].rearrange("p (k n) -> p k n", n=P)[:, :, N],
                                    TP[u % 2][0:FE, 0:m * P].rearrange("p (k n) -> p k n", n=P)[:, :, N], ACT.Copy)\
                                  .then_inc(agg_c, 1)
                        if layer != 2:
                            act.wait_ge(bn_var, 1)
                            nc.scalar.activation(SM[:, 3, :], SM[:, 3, :], ACT.Sqrt).then_inc(bn_sd, 1)
                        if layer == 0:
                            act.wait_ge(gelu_in, 1)
                            nc.scalar.activation(Y[N, :, :], Y[N, :, :], ACT.Gelu).then_inc(gelu_out, 1)
                        for n in range(2 if layer == 2 else 1):
                            act.wait_ge(ln_var, n + 1)
                            nc.scalar.activation(SN[N, 2, :], SN[N, 2, :], ACT.Sqrt).then_inc(ln_sd, 1)

                    @block.vector
                    def _(v):
                        st = Steps(v, dve)
                        nv = nc.vector
                        tt = nv.tensor_tensor
                        for g in range(groups):
                            last = SC[1][:, :, C:C + 1].rearrange("p r j -> p (r j)")
                            st.do(nv.tensor_copy(LROW[:, 0, 0:64], last[:, 64 * g:64 * g + 64]))
                            if has_weights:
                                st.do(nv.tensor_copy(LROW[:, 0, 64:68], last[:, FE + 4 * g:FE + 4 * g + 4]))
                            if layer < 2:
                                m = MS[1][:, 4 * g:4 * g + 4, C:C + 1]
                                st.do(nv.tensor_copy(LROW[:, 1, 0:64].rearrange("p (h c) -> p h c", c=CH),
                                                     m.to_broadcast([P, 4, CH])))
                                st.do(nv.tensor_copy(LROW[:, 1, 64:68], m.rearrange("p h j -> p (h j)")))
                            else:
                                st.do(nv.memset(LROW[:, 1, :], 0.0))
                            st.do(nv.tensor_copy(LROW[:, 2, :], PASS[:, 0:1].to_broadcast([P, GR])))
                            st.wait()
                            nv.tensor_scalar(SM[:, 7, 0:1], PASS[:, 0:1], 1.0, None, ALU.mult).then_inc(c_rows, 1)
                            v.wait_ge(c_tp, g + 1)
                            st.then(nv.tensor_copy(CT[0:GR, :, :], CP[0:GR, 0:3 * P]
                                                   .rearrange("p (n q) -> p n q", n=3)))
                            st.then(nv.tensor_tensor_scan(CW[0:GR, 0, :], CT[0:GR, 2, :], CT[0:GR, 1, :], NEG,
                                                          ALU.add, ALU.max))
                            st.do(nv.memset(CW[0:GR, 1, 0:1], NEG))
                            st.do(tt(CW[0:GR, 1, 1:P], CW[0:GR, 0, 0:P - 1], CW[0:GR, 0, 1:P], ALU.subtract))
                            st.do(tt(CW[0:GR, 2, :], CT[0:GR, 1, :], CW[0:GR, 0, :], ALU.subtract))
                            st.wait()
                            tt(CW[0:GR, 1, :], CW[0:GR, 1, :], CT[0:GR, 2, :], ALU.add).then_inc(c_arg, 1)
                            v.wait_ge(c_exp, g + 1)
                            st.do(tt(CW[0:GR, 4, :], CT[0:GR, 0, :], CW[0:GR, 2, :], ALU.mult))
                            st.do(nv.memset(CS[0:GR, 0, 0:1], 0.0))
                            st.do(nv.memset(CS[0:GR, 1, 0:1], NEG))
                            st.do(nv.tensor_copy(CS[0:GR, 1, 1:1 + P], CW[0:GR, 0, :]))
                            st.wait()
                            nv.tensor_tensor_scan(CS[0:GR, 0, 1:1 + P], CW[0:GR, 1, :], CW[0:GR, 4, :], 0.0, ALU.mult,
                                                  ALU.add).then_inc(c_sum, 1)
                            v.wait_ge(c_back, 2 * g + 2)
                            st.do(nv.tensor_copy(CROW[:, 64 * g:64 * g + 64], CB[:, 0:64]))
                            if has_weights:
                                st.do(nv.tensor_copy(CROW[:, FE + 4 * g:FE + 4 * g + 4], CB[:, 64:68]))
                            st.wait()
                            nv.tensor_copy(CROW[:, R + 4 * g:R + 4 * g + 4], CB[:, P:P + 64:CH])\
                                .then_inc(c_row, 1)
                        v.wait_ge(rows_in, 16 * K)
                        v.wait_ge(carry_in, 16)
                        st.then(tt(MX[N, :, :], GN[N, :, R:WD], GC[N, :, R:WD], ALU.max))
                        st.then(tt(GN[N, :, R:WD], GN[N, :, R:WD], MX[N, :, :], ALU.subtract))
                        tt(GC[N, :, R:WD], GC[N, :, R:WD], MX[N, :, :], ALU.subtract).then_inc(merge_arg, 1)
                        v.wait_ge(merge_exp, 2)
                        for G in (GN, GC):
                            fac = G[N, :, R:WD]
                            st.do(tt(G[N, :, 0:FE].rearrange("p k (h c) -> p k h c", c=CH),
                                     G[N, :, 0:FE].rearrange("p k (h c) -> p k h c", c=CH),
                                     fac.unsqueeze(3).to_broadcast([NP, K, H, CH]), ALU.mult))
                            if has_weights:
                                st.do(tt(G[N, :, FE:R], G[N, :, FE:R], fac, ALU.mult))
                        st.wait()
                        st.then(tt(GN[N, :, 0:R], GN[N, :, 0:R], GC[N, :, 0:R], ALU.add))
                        st.then(tt(GN[N, :, 0:R], GN[N, :, 0:R],
                                   HAS[N, :].unsqueeze(2).to_broadcast([NP, K, R]), ALU.mult))
                        if has_weights:
                            st.then(nv.tensor_scalar(GN[N, :, FE:R], GN[N, :, FE:R], 1.0 if layer == 2 else 1e-16,
                                                     None, ALU.add))
                            st.then(nv.reciprocal(MX[N, :, :], GN[N, :, FE:R]))
                            agg = GN[N, :, 0:FE].rearrange("p k (h c) -> p k h c", c=CH)
                            st.then(tt(agg, agg, MX[N, :, :].unsqueeze(3).to_broadcast([NP, K, H, CH]), ALU.mult))
                        if project_agg:
                            nv.tensor_scalar(SM[N, 7, 0:1], PASS[N, 0:1], 1.0, None, ALU.mult)\
                                .then_inc(agg_ready, 1)
                            for u, (k0, m) in enumerate(units):
                                v.wait_ge(agg_mm, u + 1)
                                tt(Y[N, k0:k0 + m, :], PO[u % 2][N, 0:m * 64].rearrange("p (k n) -> p k n", k=m),
                                   KEEP[N, k0:k0 + m, :], ALU.add).then_inc(agg_add, 1)
                            v.wait_ge(agg_add, len(units))
                            if layer == 2:
                                st.then(tt(Y[N, :, :], Y[N, :, :], over_nodes(vec("bo")), ALU.add))
                        elif layer == 0:
                            st.then(tt(Y[N, :, :], GN[N, :, 0:64], over_nodes(vec("bias0")), ALU.add))
                        else:
                            st.then(tt(Y[N, :, :], GN[N, :, 0:64], over_nodes(vec("bias3")), ALU.add))
                            st.then(nv.scalar_tensor_tensor(out=Y[N, :, :], in0=Y[N, :, :], scalar=0.0,
                                                            in1=KEEP[N, :, :], op0=ALU.max, op1=ALU.add))

                        def layer_norm(x_ap, turn):
                            st.then(nv.tensor_reduce(SN[N, 0, :], x_ap, AX.X, ALU.add))
                            st.then(nv.tensor_scalar(SN[N, 1, :], SN[N, 0, :], 1.0 / 64, None, ALU.mult))
                            st.then(tt(SQ[N, :, :], x_ap, SN[N, 1, :].unsqueeze(2).to_broadcast([NP, K, 64]),
                                       ALU.subtract))
                            st.then(tt(GC[N, :, 0:64], SQ[N, :, :], SQ[N, :, :], ALU.mult))
                            st.then(nv.tensor_reduce(SN[N, 3, :], GC[N, :, 0:64], AX.X, ALU.add))
                            nv.tensor_scalar(SN[N, 2, :], SN[N, 3, :], 1.0 / 64, 1e-5, ALU.mult, ALU.add)\
                                .then_inc(ln_var, 1)
                            v.wait_ge(ln_sd, turn)
                            st.then(nv.reciprocal(SN[N, 4, :], SN[N, 2, :]))
                            return SN[N, 4, :].unsqueeze(2).to_broadcast([NP, K, 64])

                        if layer == 2:
                            rs = layer_norm(Y[N, :, :], 1)
                            st.then(tt(SQ[N, :, :], SQ[N, :, :], rs, ALU.mult))
                            st.then(tt(SQ[N, :, :], SQ[N, :, :], over_nodes(vec("gamma2")), ALU.mult))
                            st.then(tt(SQ[N, :, :], SQ[N, :, :], over_nodes(vec("beta2")), ALU.add))
                            st.then(tt(Y[N, :, :], Y[N, :, :], SQ[N, :, :], ALU.add))
                        else:
                            nv.tensor_reduce(SM[N, 0, :], Y[N, :, :].rearrange("p k f -> p f k"), AX.X, ALU.add)\
                                .then_inc(bn_part, 1)
                            v.wait_ge(bn_sum, 1)
                            st.then(nv.tensor_scalar(SM[:, 2, :], PB[:, 0:64], 1.0 / NODES, None, ALU.mult))
                            st.then(tt(Y[N, :, :], Y[N, :, :], over_nodes(SM[:, 2, :]), ALU.subtract))
                            st.then(tt(SQ[N, :, :], Y[N, :, :], Y[N, :, :], ALU.mult))
                            nv.tensor_reduce(SM[N, 1, :], SQ[N, :, :].rearrange("p k f -> p f k"), AX.X, ALU.add)\
                                .then_inc(bn_part, 1)
                            v.wait_ge(bn_sum, 2)
                            nv.tensor_scalar(SM[:, 3, :], PB[:, 64:128], 1.0 / NODES, 1e-5, ALU.mult, ALU.add)\
                                .then_inc(bn_var, 1)
                            v.wait_ge(bn_sd, 1)
                            st.then(nv.reciprocal(SM[:, 4, :], SM[:, 3, :]))
                            st.then(tt(SM[:, 5, :], SM[:, 4, :], vec(f"gamma{layer}"), ALU.mult))
                            st.then(tt(Y[N, :, :], Y[N, :, :], over_nodes(SM[:, 5, :]), ALU.mult))
                            st.then(tt(Y[N, :, :], Y[N, :, :], over_nodes(vec(f"beta{layer}")), ALU.add))
                        if layer == 0:
                            tt(Y[N, :, :], Y[N, :, :], X[N, :, :], ALU.add).then_inc(gelu_in, 1)
                            v.wait_ge(gelu_out, 1)
                        st.then(tt(Y[N, :, :], Y[N, :, :], X[N, :, :], ALU.add))
                        rs = layer_norm(Y[N, :, :], 2 if layer == 2 else 1)
                        tt(X[N, :, :], SQ[N, :, :], rs, ALU.mult).then_inc(done, 1)

        end_phase()
        project(wcol("W_l", "W_r"), 128, vec("b_l", 2), [(xl_tab, 0, 64), (xr_tab, 64, 64)], None, 64)
        blanks.close()
        end_phase()
        edges_0(src)
        end_phase()
        finish_layer(0)
        end_phase()
        project(wcol("Wq1", "W_self"), 192, vec("zero_q0", 3), [(q1_tab, 0, 128), (x1_tab, None, 64)], 128)
        end_phase()
        edges_1(src, dst_of_edges)
        end_phase()
        finish_layer(1)
        end_phase()
        project(wcol("Wk", "Wf"), 256, vec("bk", 4), [(kv_tab, 0, 128), (q2_tab, 128, 64)], 192,
                128)
        end_phase()
        edges_2(src)
        end_phase()
        finish_layer(2)
        end_phase()
        project_relations()
        end_phase()
        edges_3()
        end_phase()
        finish_layer(3)
        end_phase()


_VECS = ["L0_gnn_b_l", "L0_gnn_b_r", None, None, None, "L2_gnn_bk", "L2_gnn_bv", "L2_gnn_bq", "L2_gnn_bf",
         "L0_gnn_att", "L0_gnn_bias", "L0_gnn_gamma", "L0_gnn_beta", "L1_gnn_gamma", "L1_gnn_beta", "L2_gnn_bo",
         "L2_gnn_gamma", "L2_gnn_beta", "L3_gnn_bias", "L3_gnn_res_b", "L3_gnn_gamma", "L3_gnn_beta"]


def kernel(**inputs):
    import numpy as np
    import concourse.bacc as bacc
    from concourse.bass_utils import run_bass_kernel_spmd

    a = {k: np.asarray(v) for k, v in inputs.items()}
    f32 = np.float32

    def padded(v, rows):
        return np.concatenate([v, np.zeros((rows - v.shape[0],) + v.shape[1:], v.dtype)])

    dst = a["dst"].astype(np.int32)
    w64 = np.concatenate([a["L0_gnn_W_l"], a["L0_gnn_W_r"], a["L1_gnn_Wq"], a["L1_gnn_W_self"], a["L1_gnn_k_w1"],
                          a["L1_gnn_v_w1"], a["L2_gnn_Wk"], a["L2_gnn_Wv"], a["L2_gnn_Wq"], a["L2_gnn_Wf"],
                          a["L2_gnn_Wo"], a["L3_gnn_res_w"], a["L3_gnn_comp"]], axis=1)
    arrays = {
        "x": padded(a["x"], NPAD),
        "dst_shifted": np.concatenate([np.full(1, -1, np.int32), dst, np.full(EPAD - EDGES + J, NODES, np.int32)]),
        "src": padded(a["src"].astype(np.int32), EPAD).reshape(P, J),
        "ea16": padded(a["edge_attr_16"], EPAD),
        "ea64": padded(a["edge_attr_64"], EPAD),
        "ea9": padded(np.concatenate([a["edge_attr_9"], a["edge_attr_9"][:, SH - 1:]], axis=1), EPAD),
        "etype": padded(a["edge_type_64"].astype(np.int32), EPAD).reshape(P, J),
        "ew": padded(a["edge_weight1"], EPAD).reshape(P, J),
        "w64": w64,
        "we": a["L0_gnn_W_e"],
        "cfix": np.concatenate([a["L1_gnn_Cqk"].transpose(1, 0, 2), a["L1_gnn_Cv"].transpose(1, 0, 2)], axis=2)
                .reshape(SH * 64, 256),
        "w2": np.concatenate([a["L1_gnn_k_w2"], a["L1_gnn_v_w2"]], axis=1),
        "b1": np.concatenate([a["L1_gnn_k_b1"], a["L1_gnn_v_b1"]]).reshape(P, 1),
        "b2": np.concatenate([a["L1_gnn_k_b2"], a["L1_gnn_v_b2"]]).reshape(1, 256),
        "wout": a["L1_gnn_W_out"],
        "vecs": np.concatenate([np.zeros(64, f32) if n is None else a[n].reshape(64) for n in _VECS])
                .reshape(1, V_ALL),
        "basis": a["L3_gnn_basis"],
    }
    nc = bacc.Bacc("TRN2", target_bir_lowering=False, num_devices=1)
    args = {}
    for name in arrays:
        arrays[name] = np.ascontiguousarray(arrays[name])
        args[name] = nc.dram_tensor(name, arrays[name].shape, mybir.dt.from_np(arrays[name].dtype),
                                    kind="ExternalInput").ap()
    out = nc.dram_tensor("out", (NODES, D), F32, kind="ExternalOutput").ap()
    graph_kernel(nc, out=out, **args)
    r = run_bass_kernel_spmd(nc, [arrays], core_ids=[0])
    return r.results[0]["out"]
```
